# Optimizing a Trainium2 kernel written in Bass

```python
import numpy as np
import jax
import jax.numpy as jnp

def _softmax(x, axis=-1):
    return jax.nn.softmax(x, axis=axis)

def _gelu(x):
    return jax.nn.gelu(x, approximate=True)

def _silu(x):
    return jax.nn.silu(x)

def _sigmoid(x):
    return jax.nn.sigmoid(x)

def _layernorm(x, axis=-1, eps=1e-05):
    m = jnp.mean(x, axis=axis, keepdims=True)
    v = jnp.var(x, axis=axis, keepdims=True)
    return (x - m) / jnp.sqrt(v + eps)

def _scatter_add(tgt, idx, src, axis=0):
    return tgt.at[idx].add(src)

def _segment_sum(src, seg, n):
    return jax.ops.segment_sum(src, seg, n)
kernel_name = 'mk_xattn_ffn_d2_seqx_r4_8dee10'

def setup_inputs(seed: int=0):
    np.random.seed(seed)
    _w = jnp.asarray

    def _rec_inputs():
        import jax
        import jax.numpy as jnp
        _rk = jax.random.key(seed)
        x = 7.22e-05 + 1 * jax.random.normal(jax.random.fold_in(_rk, 1), (8, 512, 256), jnp.float32)
        _lenS = 512 - jax.random.randint(jax.random.fold_in(_rk, 7), (8,), 0, max(1, 512 // 4) + 1, jnp.int32)
        _lenS2 = 1024 - jax.random.randint(jax.random.fold_in(_rk, 8), (8,), 0, max(1, 1024 // 4) + 1, jnp.int32)
        _ctx_1024P = jax.random.normal(jax.random.fold_in(_rk, 11), (8, 16, 256), jnp.float32)
        _ctx_1024c = jax.random.dirichlet(jax.random.fold_in(_rk, 511), 0.3 * jnp.ones((16,), jnp.float32), (8, 1024))
        _ctx_1024t = jnp.einsum('bsk,bkd->bsd', _ctx_1024c, _ctx_1024P)
        _ctx_1024t = _ctx_1024t * jax.lax.rsqrt(jnp.mean(jnp.square(_ctx_1024t)) + 1e-12) * 0.953939
        ctx_1024 = 4.13588e-05 + 0.999923 * (_ctx_1024t + 0.3 * jax.random.normal(jax.random.fold_in(_rk, 611), (8, 1024, 256), jnp.float32))
        _validS = jnp.arange(512)[None, :] < _lenS[:, None]
        _validS2 = jnp.arange(1024)[None, :] < _lenS2[:, None]
        _causal = jnp.tril(jnp.ones((512, 512), dtype=bool))
        mask_SxS2_bk0 = jnp.logical_not(jnp.broadcast_to(_validS2[0:1, :], (512, 1024)))
        mask_Bx1x1xS2_ik0 = jnp.where(jnp.broadcast_to(_validS2[:, None, None, :], (8, 1, 1, 1024)), 0, 1).astype(jnp.int32)
        return (x, ctx_1024, mask_SxS2_bk0, mask_Bx1x1xS2_ik0)
    x, ctx_1024, mask_SxS2_bk0, mask_Bx1x1xS2_ik0 = _rec_inputs()

    def _L0_xattn_setup():
        import jax, jax.numpy as jnp
        import numpy as np
        B, T, D, H = (4, 512, 256, 16)
        DH = D // H
        key = jax.random.key(seed)
        ks = jax.random.split(key, 8)
        scale = 1.0 / np.sqrt(D)
        return {'q': jax.random.normal(ks[0], (B, T, D), dtype=jnp.float32), 'k': jax.random.normal(ks[1], (B, T, D), dtype=jnp.float32), 'v': jax.random.normal(ks[2], (B, T, D), dtype=jnp.float32), 'wq': jax.random.normal(ks[3], (D, D), dtype=jnp.float32) * scale, 'wk': jax.random.normal(ks[4], (D, D), dtype=jnp.float32) * scale, 'wv': jax.random.normal(ks[5], (D, D), dtype=jnp.float32) * scale, 'wo': jax.random.normal(ks[6], (D, D), dtype=jnp.float32) * scale, 'mask': jnp.tril(jnp.ones((T, T), dtype=bool))}
    _L0_xattn_all = _L0_xattn_setup()
    _L0_xattn_in = {k: v for k, v in _L0_xattn_all.items() if k in ('wq', 'wk', 'wv', 'wo')}
    del _L0_xattn_all

    def _L0_ffn_setup():
        import jax, jax.numpy as jnp
        import numpy as np
        EPS = 1e-09
        key = jax.random.key(seed)
        k1, k2, k3, k4 = jax.random.split(key, 4)
        B, T, H, D, E = (2, 512, 256, 256, 8)
        x = jax.random.normal(k1, (B, T, H), dtype=jnp.float32)
        gate_w = jax.random.normal(k2, (E, H), dtype=jnp.float32) * 0.02
        gate_up_proj = jax.random.normal(k3, (E, H, 2 * D), dtype=jnp.float32) * 0.02
        down_proj = jax.random.normal(k4, (E, D, H), dtype=jnp.float32) * 0.02
        return {'x': x, 'gate_w': gate_w, 'gate_up_proj': gate_up_proj, 'down_proj': down_proj}
    _L0_ffn_all = _L0_ffn_setup()
    _L0_ffn_in = {k: v for k, v in _L0_ffn_all.items() if k in ('gate_w', 'gate_up_proj', 'down_proj')}
    del _L0_ffn_all

    def _L1_xattn_setup():
        import jax, jax.numpy as jnp
        import numpy as np
        EMBED_DIM = 256
        NUM_HEADS = 16
        HEAD_DIM = EMBED_DIM // NUM_HEADS
        NEG = -1000000000.0

        def _split_heads(x):
            B, S, D = x.shape
            return x.reshape(B, S, NUM_HEADS, HEAD_DIM).transpose(0, 2, 1, 3)
        key = jax.random.key(seed)
        ks = jax.random.split(key, 13)
        B, S, D = (4, 512, EMBED_DIM)
        scale = 1.0 / np.sqrt(D)
        inp = {'query': jax.random.normal(ks[0], (B, S, D), jnp.float32), 'key': jax.random.normal(ks[1], (B, S, D), jnp.float32), 'value': jax.random.normal(ks[2], (B, S, D), jnp.float32), 'mask': jax.random.randint(ks[3], (B, 1, 1, S), 0, 2, jnp.int32), 'Wq': jax.random.normal(ks[4], (D, D), jnp.float32) * scale, 'bq': jnp.zeros((D,), jnp.float32), 'Wk': jax.random.normal(ks[5], (D, D), jnp.float32) * scale, 'bk': jnp.zeros((D,), jnp.float32), 'Wv': jax.random.normal(ks[6], (D, D), jnp.float32) * scale, 'bv': jnp.zeros((D,), jnp.float32), 'Wo': jax.random.normal(ks[7], (D, D), jnp.float32) * scale, 'bo': jnp.zeros((D,), jnp.float32)}
        return inp
    _L1_xattn_all = _L1_xattn_setup()
    _L1_xattn_in = {k: v for k, v in _L1_xattn_all.items() if k in ('Wq', 'bq', 'Wk', 'bk', 'Wv', 'bv', 'Wo', 'bo')}
    del _L1_xattn_all

    def _L1_ffn_setup():
        import jax, jax.numpy as jnp
        import numpy as np
        TOP_K = 8
        CAPACITY = 128

        def _silu(x):
            return x * jax.nn.sigmoid(x)
        key = jax.random.key(seed)
        ks = jax.random.split(key, 7)
        B, S, H, E, I, Is = (2, 256, 256, 64, 128, 512)
        s = 0.05
        return {'hidden_states': jax.random.normal(ks[0], (B, S, H), jnp.float32), 'gate_w': jax.random.normal(ks[1], (H, E), jnp.float32) * s, 'shared_gate_w': jax.random.normal(ks[2], (H, 1), jnp.float32) * s, 'shared_gate_up_w': jax.random.normal(ks[3], (H, 2 * Is), jnp.float32) * s, 'shared_down_w': jax.random.normal(ks[4], (Is, H), jnp.float32) * s, 'expert_gate_up_w': jax.random.normal(ks[5], (E, H, 2 * I), jnp.float32) * s, 'expert_down_w': jax.random.normal(ks[6], (E, I, H), jnp.float32) * s}
    _L1_ffn_all = _L1_ffn_setup()
    _L1_ffn_in = {k: v for k, v in _L1_ffn_all.items() if k in ('gate_w', 'shared_gate_w', 'shared_gate_up_w', 'shared_down_w', 'expert_gate_up_w', 'expert_down_w')}
    del _L1_ffn_all
    return {'x': x, 'ctx_1024': ctx_1024, 'mask_SxS2_bk0': mask_SxS2_bk0, 'mask_Bx1x1xS2_ik0': mask_Bx1x1xS2_ik0, 'L0_xattn_wq': _L0_xattn_in['wq'], 'L0_xattn_wk': _L0_xattn_in['wk'], 'L0_xattn_wv': _L0_xattn_in['wv'], 'L0_xattn_wo': _L0_xattn_in['wo'], 'L0_ffn_gate_w': _L0_ffn_in['gate_w'], 'L0_ffn_gate_up_proj': _L0_ffn_in['gate_up_proj'], 'L0_ffn_down_proj': _L0_ffn_in['down_proj'], 'L1_xattn_Wq': _L1_xattn_in['Wq'], 'L1_xattn_bq': _L1_xattn_in['bq'], 'L1_xattn_Wk': _L1_xattn_in['Wk'], 'L1_xattn_bk': _L1_xattn_in['bk'], 'L1_xattn_Wv': _L1_xattn_in['Wv'], 'L1_xattn_bv': _L1_xattn_in['bv'], 'L1_xattn_Wo': _L1_xattn_in['Wo'], 'L1_xattn_bo': _L1_xattn_in['bo'], 'L1_ffn_gate_w': _L1_ffn_in['gate_w'], 'L1_ffn_shared_gate_w': _L1_ffn_in['shared_gate_w'], 'L1_ffn_shared_gate_up_w': _L1_ffn_in['shared_gate_up_w'], 'L1_ffn_shared_down_w': _L1_ffn_in['shared_down_w'], 'L1_ffn_expert_gate_up_w': _L1_ffn_in['expert_gate_up_w'], 'L1_ffn_expert_down_w': _L1_ffn_in['expert_down_w']}

def reference(x, ctx_1024, mask_SxS2_bk0, mask_Bx1x1xS2_ik0, L0_xattn_wq, L0_xattn_wk, L0_xattn_wv, L0_xattn_wo, L0_ffn_gate_w, L0_ffn_gate_up_proj, L0_ffn_down_proj, L1_xattn_Wq, L1_xattn_bq, L1_xattn_Wk, L1_xattn_bk, L1_xattn_Wv, L1_xattn_bv, L1_xattn_Wo, L1_xattn_bo, L1_ffn_gate_w, L1_ffn_shared_gate_w, L1_ffn_shared_gate_up_w, L1_ffn_shared_down_w, L1_ffn_expert_gate_up_w, L1_ffn_expert_down_w):
    import jax
    import jax.numpy as jnp

    def _L0_xattn_ref(q, k, v, wq, wk, wv, wo, mask):
        import jax, jax.numpy as jnp
        import numpy as np
        B, T, D, H = (4, 512, 256, 16)
        DH = D // H
        Bq, Tq, C = q.shape
        Tk = k.shape[1]
        qh = (q @ wq.T).reshape(Bq, Tq, H, DH).transpose(0, 2, 1, 3)
        kh = (k @ wk.T).reshape(Bq, Tk, H, DH).transpose(0, 2, 1, 3)
        vh = (v @ wv.T).reshape(Bq, Tk, H, DH).transpose(0, 2, 1, 3)
        att = jnp.einsum('bhqd,bhkd->bhqk', qh, kh) / np.sqrt(DH)
        att = jnp.where(mask[None, None, :, :], att, -jnp.inf)
        att = jax.nn.softmax(att, axis=-1)
        out = jnp.einsum('bhqk,bhkd->bhqd', att, vh)
        out = out.transpose(0, 2, 1, 3).reshape(Bq, Tq, C)
        return out @ wo.T

    def _L0_ffn_ref(x, gate_w, gate_up_proj, down_proj):
        import jax, jax.numpy as jnp
        import numpy as np
        EPS = 1e-09
        B, T, H = x.shape
        E = gate_w.shape[0]
        top_k = 2
        hidden = x.reshape(-1, H)
        router_logits = hidden @ gate_w.T
        routing_weights = jax.nn.softmax(router_logits.astype(jnp.float32), axis=-1)
        topk_weights, topk_indices = jax.lax.top_k(routing_weights, top_k)
        topk_weights = topk_weights / (jnp.sum(topk_weights, axis=-1, keepdims=True) + EPS)
        N = hidden.shape[0]
        routed = jnp.zeros((N, E), dtype=router_logits.dtype)
        rows = jnp.arange(N)[:, None]
        routed = routed.at[rows, topk_indices].set(topk_weights.astype(router_logits.dtype))
        routed = routed / (jnp.sum(routed, axis=-1, keepdims=True) + EPS)
        routed = routed.astype(hidden.dtype)
        gate_up = jnp.einsum('th,ehq->teq', hidden, gate_up_proj)
        gate, up = jnp.split(gate_up, 2, axis=-1)
        expert_outputs = jnp.einsum('teq,eqh->teh', jax.nn.silu(gate) * up, down_proj)
        out = jnp.sum(expert_outputs * routed[:, :, None], axis=1)
        return out.reshape(B, T, H)

    def _L1_xattn_ref(query, key, value, mask, Wq, bq, Wk, bk, Wv, bv, Wo, bo):
        import jax, jax.numpy as jnp
        import numpy as np
        EMBED_DIM = 256
        NUM_HEADS = 16
        HEAD_DIM = EMBED_DIM // NUM_HEADS
        NEG = -1000000000.0

        def _split_heads(x):
            B, S, D = x.shape
            return x.reshape(B, S, NUM_HEADS, HEAD_DIM).transpose(0, 2, 1, 3)
        B, S, D = query.shape
        Q = _split_heads(query @ Wq + bq)
        K = _split_heads(key @ Wk + bk)
        V = _split_heads(value @ Wv + bv)
        scores = jnp.einsum('bhqd,bhkd->bhqk', Q, K) / jnp.sqrt(jnp.float32(HEAD_DIM))
        scores = jnp.where(mask == 0, jnp.float32(NEG), scores)
        attn = jax.nn.softmax(scores, axis=-1)
        out = jnp.einsum('bhqk,bhkd->bhqd', attn, V)
        out = out.transpose(0, 2, 1, 3).reshape(B, S, D)
        return out @ Wo + bo

    def _L1_ffn_ref(hidden_states, gate_w, shared_gate_w, shared_gate_up_w, shared_down_w, expert_gate_up_w, expert_down_w):
        import jax, jax.numpy as jnp
        import numpy as np
        TOP_K = 8
        CAPACITY = 128

        def _silu(x):
            return x * jax.nn.sigmoid(x)
        B, S, H = hidden_states.shape
        x = hidden_states.reshape(-1, H)
        T = x.shape[0]
        E = gate_w.shape[1]
        Is = shared_gate_up_w.shape[1] // 2
        I = expert_gate_up_w.shape[2] // 2
        gu = x @ shared_gate_up_w
        shared = _silu(gu[:, :Is]) * gu[:, Is:] @ shared_down_w
        shared = shared * jax.nn.sigmoid(x @ shared_gate_w)
        logits = x @ gate_w
        probs = jax.nn.softmax(logits.astype(jnp.float32), axis=-1)
        w, idx = jax.lax.top_k(probs, TOP_K)
        w = (w / jnp.sum(w, axis=-1, keepdims=True)).astype(x.dtype)
        e_flat = idx.reshape(-1)
        w_flat = w.reshape(-1)
        A = e_flat.shape[0]
        tok = jnp.arange(A) // TOP_K
        onehot = jax.nn.one_hot(e_flat, E, dtype=jnp.int32)
        pos = jnp.take_along_axis(jnp.cumsum(onehot, axis=0) - 1, e_flat[:, None], axis=1)[:, 0]
        slot = jnp.minimum(pos, CAPACITY)
        buf = jnp.zeros((E, CAPACITY + 1, H), x.dtype).at[e_flat, slot].set(x[tok])
        gu_e = jnp.einsum('ech,ehf->ecf', buf, expert_gate_up_w)
        act = _silu(gu_e[..., :I]) * gu_e[..., I:]
        out_e = jnp.einsum('eci,eih->ech', act, expert_down_w)
        y = out_e[e_flat, slot] * w_flat[:, None]
        y = jnp.where((pos < CAPACITY)[:, None], y, jnp.zeros_like(y))
        y = y.reshape(T, TOP_K, H).sum(axis=1)
        return (y + shared).reshape(B, S, H)
    x = x + _L0_xattn_ref(_layernorm(x, axis=-1), ctx_1024, ctx_1024, L0_xattn_wq, L0_xattn_wk, L0_xattn_wv, L0_xattn_wo, mask_SxS2_bk0)
    x = x + _L0_ffn_ref(_layernorm(x, axis=-1), L0_ffn_gate_w, L0_ffn_gate_up_proj, L0_ffn_down_proj)
    x = x + _L1_xattn_ref(_layernorm(x, axis=-1), ctx_1024, ctx_1024, mask_Bx1x1xS2_ik0, L1_xattn_Wq, L1_xattn_bq, L1_xattn_Wk, L1_xattn_bk, L1_xattn_Wv, L1_xattn_bv, L1_xattn_Wo, L1_xattn_bo)
    x = x + _L1_ffn_ref(_layernorm(x, axis=-1), L1_ffn_gate_w, L1_ffn_shared_gate_w, L1_ffn_shared_gate_up_w, L1_ffn_shared_down_w, L1_ffn_expert_gate_up_w, L1_ffn_expert_down_w)
    return x

_drawn_inputs = setup_inputs


def setup_inputs(seed=0):
    import zlib

    import numpy as np

    out = dict(_drawn_inputs(seed))
    spreads = {'L1_xattn_bq': (0.0, 0.364),
     'L1_xattn_bk': (0.0, 2.0),
     'L1_xattn_bv': (0.0, 0.1),
     'L1_xattn_bo': (0.0, 0.1)}
    factors = {'L0_ffn_gate_w': 6.136,
     'L0_ffn_gate_up_proj': 5.417,
     'L0_ffn_down_proj': 5.449,
     'L1_ffn_gate_w': 4.593,
     'L1_ffn_expert_gate_up_w': 4.403,
     'L1_ffn_expert_down_w': 4.391,
     'L1_ffn_shared_gate_w': 5.842}
    for name, (base, spread) in spreads.items():
        noise = np.random.default_rng([zlib.crc32(name.encode()), seed]).standard_normal(out[name].shape)
        drawn = base * np.exp(spread * noise) if base else spread * noise
        out[name] = jnp.asarray(drawn.astype(out[name].dtype))
    for name, factor in factors.items():
        out[name] = (out[name] * factor).astype(out[name].dtype)
    return out
```

```python
from contextlib import ExitStack

import concourse.bass as bass
from concourse import mybir

F32 = mybir.dt.float32
BF16 = mybir.dt.bfloat16
I32 = mybir.dt.int32
U32 = mybir.dt.uint32
U8 = mybir.dt.uint8
ALU = mybir.AluOpType
ACT = mybir.ActivationFunctionType
AX = mybir.AxisListType
ds = bass.ds

P = 128
PARTS = (0, 0, 1, 1, 0, 2), (0, 1, 0, 1, 2, 0)
ROW_NEG, ROW_MAX, ROW_END = 96, 99, 102
LOWEST = -3.0e38
MASKED = -1.0e30
LN_EPS, ROUTE_EPS = 1e-5, 1e-9
FAR = 1048576.0

C_ID, C_TRI, C_SEL, C_E1, C_I8, C_UP, C_DOWN, C_NEG, C_TOK, C_END = (
    0, 128, 256, 384, 448, 456, 460, 464, 467, 471)


class Steps:

    def __init__(self, engine, sem, base, stride):
        self.engine, self.sem, self.base, self.stride, self.n = engine, sem, base, stride, 0

    def step(self, instruction):
        instruction.then_inc(self.sem, 1)
        self.n += 1

    def settle(self, apart=None):
        self.engine.wait_ge(self.sem, self.base + self.n)
        if apart is not None:
            self.engine.sem_inc(apart, 1)

    def fill(self):
        assert 0 < self.n < self.stride
        self.settle()
        self.engine.sem_inc(self.sem, self.stride - self.n)


def build(nc, a, out):
    B, T, D = a["x"].shape
    S = a["ctxT"].shape[2]
    H = 16
    DH = D // H
    KD = D // P
    TT = T // P
    CH = 256
    NCH = S // CH
    KT = CH // P
    G = H // 4
    E0, E1 = 8, 64
    CAP = 128
    XW = D + E1
    NTOK = B * T
    SHK = 4
    PAIRS = 2 * E0 + SHK
    EU = 8
    N_WEIGHTS = 2 * (3 + 4) + 3 + 2
    K_DMAS = 6 + H

    with ExitStack() as ctx:
        def sb(name, shape, dt=F32):
            return ctx.enter_context(nc.sbuf_tensor(name, shape, dt))

        def ps(name, shape, dt=F32):
            return ctx.enter_context(nc.psum_tensor(name, shape, dt))

        def sems(text, suffix=""):
            return {n: ctx.enter_context(nc.semaphore(n + suffix)) for n in text.split()}

        q_scratch = nc.dram_tensor("q_scratch", (3, D, T), BF16).ap()
        k_scratch = nc.dram_tensor("k_scratch", (3, D, CH), BF16).ap()
        xw_table = nc.dram_tensor("xw_table", (NTOK + P, XW), F32).ap()
        slot_token = nc.dram_tensor("slot_token", (CAP * E1, 1), I32).ap()
        acc_table = nc.dram_tensor("acc_table", (NTOK + P, D), F32).ap()

        consts = sb("consts", [P, C_END])
        ident = consts[:, C_ID:C_ID + P]
        sel = consts[:, C_SEL:C_SEL + P]
        ident_b = sb("ident_b", [P, P], BF16)
        tri_b = sb("tri_b", [P, P], BF16)
        ones_b = sb("ones_b", [P, P], BF16)
        ones_f = sb("ones_f", [P, P])
        wq = [sb(f"wq{l}", [P, KD, D]) for l in range(2)]
        wk = [sb(f"wk{l}", [P, KD, D]) for l in range(2)]
        wv = [sb(f"wv{l}", [P, KD, D]) for l in range(2)]
        wo = [sb(f"wo{l}", [P, G, D]) for l in range(2)]
        bqk = sb("bqk", [P, 2, KD])
        bvo = sb("bvo", [1, 2, D])
        gate0 = sb("gate0", [P, KD, E0])
        gate1 = sb("gate1", [P, KD, E1 + 1])
        gu0 = sb("gu0", [P, E0, KD, 2 * D])
        down0 = sb("down0", [P, E0, KD, D])
        mask0 = sb("mask0", [P, S // P, T], BF16)
        nan_bias = sb("nan_bias", [P, TT])
        info = sb("info", [1, 2, 3, B], I32)

        x = sb("x_row", [P, TT, D])
        xw = sb("xw_row", [P, TT, XW])
        xnT = sb("xnT", [P, KD, T])
        q_stack = sb("q_stack", [P, H, T], BF16)
        k_stack = sb("k_stack", [P, H, S], BF16)
        v_all = sb("v_all", [P, S // P, D])
        v_now = sb("v_now", [P, KT, H, 32])
        ot = sb("ot", [P, G, T])
        work = sb("work", [P, 8192])
        stats = sb("stats", [P, TT, 6])
        mv = sb("mv", [P, TT, 2])
        var = sb("var", [P, TT])
        half = sb("half", [P, TT])
        rstd = sb("rstd", [P, TT])
        mx = sb("mx", [P, TT, H])
        mxu = sb("mxu", [P, TT, H])
        mres = sb("mres", [P, TT, H])
        msp = sb("msp", [P, TT, 3, H], BF16)
        mT = sb("mT", [3 * H, T], BF16)
        small = sb("small", [P, 16, TT])
        r8 = sb("r8", [P, 6, TT, 8])
        ix = sb("ix", [P, TT, 8], U32)
        r64 = sb("r64", [P, 5, TT, E1])
        chosen = sb("chosen", [P, TT, E1], BF16)
        carry = sb("carry", [P, E1])
        slots = sb("slots", [P, TT, 8], I32)
        tok_f = sb("tok_f", [P, TT])
        tok_i = sb("tok_i", [P, TT], I32)

        key_rows0 = sb("key_rows0", [P, CH], BF16)
        probs = work[:, :].rearrange("p (s k t) -> p s k t", s=8, k=KT)
        qf = work[:, 0:1024].rearrange("p (m t) -> p m t", m=KD)
        qr = work[:, 1024:2048].rearrange("p (m t) -> p m t", m=KD)
        qsp = work[:, 2048:3584].bitcast(BF16).rearrange("p (a m t) -> p a m t", a=3, m=KD)
        kf = work[:, 3584:4096].rearrange("p (m t) -> p m t", m=KD)
        kr = work[:, 4096:4608].rearrange("p (m t) -> p m t", m=KD)
        ksp = work[:, 4608:5376].bitcast(BF16).rearrange("p (a m t) -> p a m t", a=3, m=KD)
        ctxc = work[:, 5376:5888].rearrange("p (k t) -> p k t", k=KD)
        keym_i = work[:, 5888:6144].bitcast(I32)
        keym = work[:, 6144:6400]
        key_rows = [key_rows0[:, :], work[:, 6400:6528].bitcast(BF16)]
        otn = work[:, 0:2048].rearrange("p (g t) -> p g t", g=G)
        rcp = work[:, 2048:3072].rearrange("p (s t) -> p s t", s=2)
        act0 = work[:, 0:2048].rearrange("p (s k t) -> p s k t", s=2, k=KD)
        silu = work[:, 2048:3072].rearrange("p (s t) -> p s t", s=2)
        act1 = work[:, 3072:5120].rearrange("p (k t) -> p k t", k=SHK)
        mask01 = work[:, 2112:4160].bitcast(BF16).rearrange("p (c t) -> p c t", c=S // P)
        slots_init = work[:, 6528:6592].bitcast(I32)
        zeros = work[:, 6592:6592 + XW]
        xg = work[:, 0:EU * XW].rearrange("p (s n) -> p s n", s=EU)
        xgT = work[:, 2560:3072].rearrange("p (s k c) -> p s k c", s=2, k=KD)
        esilu = work[:, 3072:3328].rearrange("p (s c) -> p s c", s=2)
        eact = work[:, 3328:3584].rearrange("p (s c) -> p s c", s=2)
        eout = work[:, 3584:4096].rearrange("p (s n) -> p s n", s=2)
        ecol = work[:, 4096:4104]
        tok_of = work[:, 4160:4224].bitcast(I32)
        tok_now = work[:, 4224:4232].bitcast(I32)
        ew = gu0[:, :, :, :].rearrange("p e k f -> p e (k f)")
        ew_gu = [ew[:, j, 0:KD * 2 * P].rearrange("p (k f) -> p k f", k=KD) for j in range(EU)]
        ew_down = [ew[:, j, KD * 2 * P:KD * 2 * P + D] for j in range(EU)]
        sh_w = k_stack[:, :, :].rearrange("p h s -> p (h s)").bitcast(F32)
        gu_s = sh_w[:, 0:2048].rearrange("p (k f) -> p k f", k=KD)
        down_s = sh_w[:, 2048:3072].rearrange("p (k n) -> p k n", k=SHK)

        sc = ps("sc", [P, 2, 1024])
        yy = ps("yy", [P, 1024])
        mm = ps("mm", [P, 1024])
        sc_a = [sc[:, s, :].rearrange("p (t k) -> p t k", t=TT) for s in range(2)]
        sc_b = [sc[:, s, :].rearrange("p (k t) -> p k t", k=KT) for s in range(2)]
        y_rows = yy[:, :].rearrange("p (t n) -> p t n", t=TT)
        y_q = yy[:, :].rearrange("p (m t) -> p m t", m=KD)
        y_k = yy[:, 0:512].rearrange("p (m t) -> p m t", m=KD)
        y_v = yy[:, 512:1024].rearrange("p (k n) -> p k n", k=KT)
        m_xT = mm[:, :].rearrange("p (k t) -> p k t", k=KD)
        m_pv = [mm[:, 512 * s:512 * s + 512] for s in range(2)]
        m_mT = mm[0:3 * H, 0:T // 2].bitcast(BF16)
        m_l0 = mm[:, 0:TT * E0].rearrange("p (t e) -> p t e", t=TT)
        m_l1 = mm[:, 0:TT * (E1 + 1)].rearrange("p (t e) -> p t e", t=TT)
        m_cnt = mm[:, 512 + TT * E1:512 + (TT + 1) * E1]
        m_pos = mm[:, 512:512 + TT * E1].rearrange("p (t e) -> p t e", t=TT)
        m_cnt = mm[:, 512 + TT * E1:512 + (TT + 1) * E1]

        s = sems("""consts_in weights_in experts_in wo_zeroed tables_made half_made waits_passed consts_made masks_in active_made active_ps mask_made row_ps info_made
            table_filled x_loaded var_ready rstd_ready xn_ready xnT_ps xnT_ready
            router_ps router_sub router_exp pair_ready silu_ready act_ready y_ready y_added
            shared_in chosen_ready pos_ps slots_ready tok_scattered row_stored xw_stored
            dve_step prologue_step
            tokens_in ew_used tok_col xgT_ps xgT_kept egu_ps esilu_ready eact_ready
            ey_ps ecol_ready ey_ready ey_added copied""")
        xg_in = [ctx.enter_context(nc.semaphore(f"xg_in_{j}")) for j in range(EU)]
        ew_in = [ctx.enter_context(nc.semaphore(f"ew_in_{j}")) for j in range(EU)]
        at = [sems("""ctx_in kv_ps k_split k_spilled k_stacked v_kept kv_step q_ps q_split q_spilled
            q_stacked a_scores a_read a_step max_split mT_ps mT_kept max_rows v_placed b_scores
            exp_done pv_done ot_added den_ps otn_ready o_ps o_added""", f"_{l}") for l in range(2)]

        def units(engine, b, l):
            n = engine.value_load(info[0:1, l, 0, ds(b, 1)], min_val=1, max_val=NCH)
            first = engine.value_load(info[0:1, l, 1, ds(b, 1)], min_val=0, max_val=NCH - 1)
            before = engine.value_load(info[0:1, l, 2, ds(b, 1)], min_val=0, max_val=NCH * B)
            return n, first, before

        def wait_apart(engine, sem, value):
            engine.wait_ge(sem, value)
            engine.sem_inc(s["waits_passed"], 1)

        def chunk_of(engine, first, i):
            return nc.s_assert_within(engine.snap(first + i), 0, NCH - 1, skip_runtime_bounds_check_because="first + how many <= NCH")

        def unit_of(engine, before, i):
            return engine.snap(before + i)

        def steps_of(b, e):
            return b * EU + e + 1

        def experts_load(sp):
            sp.dma_start(tok_of, slot_token.rearrange("(p e) o -> p (e o)", p=P)).then_inc(s["tokens_in"], 16)
            with sp.Fori(0, E1 // EU) as r:
                for j in range(EU):
                    sp.wait_ge(s["ew_used"], steps_of(r, j))
                    sp.dma_start(ew_gu[j], a["egu"][ds(r * EU + j, 1), :, :].rearrange("e (k p) f -> p (e k) f", p=P)
                                 ).then_inc(ew_in[j], 16)
                    sp.dma_start(ew_down[j], a["edown"][ds(r * EU + j, 1), :, :].rearrange("e p n -> p (e n)")
                                 ).then_inc(ew_in[j], 16)
            sp.wait_ge(s["ey_added"], E1 * 16)
            sp.dma_start(out, acc_table[0:NTOK, :]).then_inc(s["copied"], 16)
            sp.wait_ge(s["copied"], 16)

        def experts_dma(pool):
            with pool.Fori(0, E1 // EU) as r:
                wait_apart(pool, s["tok_col"], r + 1)
                for j in range(EU):
                    pool.indirect_dma_start(
                        out=xg[:, j, :], out_offset=None, in_=xw_table,
                        in_offset=bass.IndirectOffsetOnAxis(ap=tok_now[:, j:j + 1].bitcast(U32), axis=0),
                        bounds_check=NTOK + P - 1, oob_is_err=True).then_inc(xg_in[j], 16)
                for j in range(EU):
                    wait_apart(pool, s["ey_ready"], steps_of(r, j))
                    if j:
                        wait_apart(pool, s["ey_added"], (r * EU + j) * 16)
                    pool.indirect_dma_start(
                        out=acc_table, in_=eout[:, j % 2, :], in_offset=None,
                        out_offset=bass.IndirectOffsetOnAxis(ap=tok_now[:, j:j + 1].bitcast(U32), axis=0),
                        bounds_check=NTOK + P - 1, oob_is_err=True,
                        compute_op=ALU.add).then_inc(s["ey_added"], 16)

        def experts_pe(pe):
            def columns(r, j):
                pe.wait_ge(xg_in[j], (r + 1) * 16)
                for k in range(KD):
                    last = pe.transpose(mm[:, 512 * (j % 2) + k * P:512 * (j % 2) + (k + 1) * P],
                                        xg[:, j, k * P:(k + 1) * P], ident)
                last.then_inc(s["xgT_ps"], 1)

            def gate_up(r, j):
                pe.wait_ge(s["xgT_kept"], steps_of(r, j))
                pe.wait_ge(ew_in[j], (r + 1) * 32)
                for half_ in range(2):
                    for k in range(KD):
                        last = pe.matmul(sc[:, j % 2, 512 * half_:512 * half_ + CAP],
                                         ew_gu[j][:, k, half_ * P:(half_ + 1) * P], xgT[:, j % 2, k, :],
                                         start=(k == 0), stop=(k == KD - 1))
                last.then_inc(s["egu_ps"], 1)

            def down_(r, j):
                pe.wait_ge(s["eact_ready"], steps_of(r, j))
                pe.matmul(yy[:, 512 * (j % 2):512 * (j % 2) + D], eact[:, j % 2, :], ew_down[j],
                          start=True, stop=True).then_inc(s["ey_ps"], 1)

            with pe.Fori(0, E1 // EU) as r:
                for q in range(EU + 2):
                    if q < EU:
                        columns(r, q)
                    if 1 <= q <= EU:
                        gate_up(r, q - 1)
                    if q >= 2:
                        down_(r, q - 2)

        def experts_act(act):
            with act.Fori(0, E1 // EU) as r:
                for q in range(EU + 1):
                    if q < EU:
                        act.wait_ge(s["xgT_ps"], steps_of(r, q))
                        act.activation(xgT[:, q % 2, :, :], mm[:, 512 * (q % 2):512 * (q % 2) + D].rearrange(
                            "p (k c) -> p k c", k=KD), ACT.Copy).then_inc(s["xgT_kept"], 1)
                    if q >= 1:
                        act.wait_ge(s["egu_ps"], steps_of(r, q - 1))
                        act.activation(esilu[:, (q - 1) % 2, :], sc[:, (q - 1) % 2, 0:CAP], ACT.Silu
                                       ).then_inc(s["esilu_ready"], 1)

        def experts_dve(dve):
            dve.wait_ge(s["tokens_in"], 16)
            with dve.Fori(0, E1 // EU) as r:
                dve.tensor_copy(tok_now, tok_of[:, ds(r * EU, EU)]).then_inc(s["tok_col"], 1)
                for q in range(EU + 1):
                    if q < EU:
                        dve.wait_ge(s["esilu_ready"], steps_of(r, q))
                        dve.tensor_tensor(eact[:, q % 2, :], sc[:, q % 2, 512:512 + CAP], esilu[:, q % 2, :],
                                          ALU.mult).then_inc(s["eact_ready"], 1)
                        dve.tensor_copy(ecol[:, q:q + 1], xg[:, q, ds(r * EU + (D + q), 1)]
                                        ).then_inc(s["ecol_ready"], 1)
                    if q >= 1:
                        j = q - 1
                        dve.wait_ge(s["ey_ps"], steps_of(r, j))
                        dve.wait_ge(s["ecol_ready"], steps_of(r, j))
                        if j >= 2:
                            dve.wait_ge(s["ey_added"], (r * EU + (j - 1)) * 16)
                        dve.tensor_scalar(eout[:, j % 2, :], yy[:, 512 * (j % 2):512 * (j % 2) + D],
                                          ecol[:, j:j + 1], None, ALU.mult).then_inc(s["ey_ready"], 1)
                dve.wait_ge(s["ey_added"], (r + 1) * EU * 16)
                dve.sem_inc(s["ew_used"], EU)

        block = ctx.enter_context(nc.Block())

        @block.sync
        def _(sp):
            def load(dst, src, sem=s["weights_in"]):
                sp.dma_start(dst, src).then_inc(sem, 16)

            load(consts[:, :], a["consts"], s["consts_in"])
            load(work[:, 0:1024].bitcast(U32).rearrange("p (c t) -> p c t", c=S // P),
                 a["mask0T"].rearrange("(c p) t -> p c t", p=P), s["masks_in"])
            load(work[0:B * NCH, 1024:1024 + CH].bitcast(I32), a["mask1"].rearrange("b (c k) -> (b c) k", k=CH), s["masks_in"])
            for l in range(2):
                load(wk[l][:, :, :], a["wk"][l].rearrange("(k p) n -> p k n", p=P))
                load(wv[l][:, :, :], a["wv"][l].rearrange("(k p) n -> p k n", p=P))
                load(wq[l][:, :, :], a["wq"][l].rearrange("(k p) n -> p k n", p=P))
                if l == 0:
                    load(bqk[:, :, :], a["bqk"])
                    load(bvo[:, 0, :], a["bv"].rearrange("(o n) -> o n", o=1))
                    load(bvo[:, 1, :], a["bo"].rearrange("(o n) -> o n", o=1))
                sp.wait_ge(s["wo_zeroed"], 2)
                for j in range(4):
                    load(wo[l][32 * j:32 * j + DH, :, :],
                         a["wo"][l].rearrange("(g j d) n -> j d g n", j=4, d=DH)[j])
            load(gate0[:, :, :], a["gate0"].rearrange("(k p) n -> p k n", p=P))
            load(gate1[:, :, :], a["gate1"].rearrange("(k p) n -> p k n", p=P))
            for e in range(E0):
                load(gu0[:, e, :, :], a["gu0"][e].rearrange("(k p) n -> p k n", p=P), s["experts_in"])
                load(down0[:, e, :, :], a["down0"][e].rearrange("(k p) n -> p k n", p=P), s["experts_in"])
            sp.wait_ge(s["tables_made"], 2)
            load(slot_token.rearrange("(p e) o -> p (e o)", p=P), slots_init, s["table_filled"])
            load(xw_table[NTOK:NTOK + P, :], zeros, s["table_filled"])
            load(acc_table[NTOK:NTOK + P, :], zeros[:, 0:D], s["table_filled"])
            sp.wait_ge(s["table_filled"], 48)
            sp.wait_ge(s["info_made"], 1)
            with sp.Fori(0, B) as b:
                sp.dma_start(x[:, :, :], a["x"][ds(b, 1), :, :].rearrange("b (t p) n -> p (b t) n", p=P)
                             ).then_inc(s["x_loaded"], 16)
                for l in range(2):
                    z = at[l]
                    n, first, before = units(sp, b, l)
                    if l:
                        wait_apart(sp, s["y_added"], b * (E0 + 1) + E0)
                    with sp.Fori(0, n) as i:
                        u = unit_of(sp, before, i)
                        key0 = chunk_of(sp, first, i) * CH
                        sp.dma_start(ctxc, a["ctxT"][ds(b, 1), :, ds(key0, CH)].rearrange(
                            "b (k p) t -> p (b k) t", p=P)).then_inc(z["ctx_in"], 16)
                        if l:
                            sp.dma_start(keym_i, a["mask1"][ds(b, 1), ds(key0, CH)].partition_broadcast(P)
                                         ).then_inc(z["ctx_in"], 16)
                        sp.wait_ge(z["k_split"], u + 1)
                        sp.dma_start(k_scratch.rearrange("a (m p) t -> p a m t", p=P), ksp
                                     ).then_inc(z["k_spilled"], 16)
                        for h in range(H):
                            sp.dma_start(k_stack[ROW_NEG:ROW_END, h, ds(i * CH, CH)],
                                         key_rows[l][ROW_NEG:ROW_END, :]).then_inc(z["k_stacked"], 16)
                        sp.wait_ge(z["k_spilled"], (u + 1) * 16)
                        for g, part in enumerate(PARTS[1]):
                            sp.dma_start(k_stack[DH * g:DH * (g + 1), :, ds(i * CH, CH)],
                                         k_scratch[part].rearrange("(h d) t -> d h t", d=DH)
                                         ).then_inc(z["k_stacked"], 16)
                        wait_apart(sp, z["k_stacked"], (u + 1) * 16 * K_DMAS)
                    sp.wait_ge(z["q_split"], b + 1)
                    sp.dma_start(q_scratch.rearrange("a (m p) t -> p a m t", p=P), qsp
                                 ).then_inc(z["q_spilled"], 16)
                    sp.wait_ge(z["q_spilled"], (b + 1) * 16)
                    for g, part in enumerate(PARTS[0]):
                        sp.dma_start(q_stack[DH * g:DH * (g + 1), :, :],
                                     q_scratch[part].rearrange("(h d) t -> d h t", d=DH)
                                     ).then_inc(z["q_stacked"], 16)
                    sp.wait_ge(z["q_stacked"], (b + 1) * 96)
                    sp.wait_ge(z["mT_kept"], b + 1)
                    for part in range(3):
                        sp.dma_start(q_stack[ROW_MAX + part:ROW_MAX + part + 1, :, :],
                                     mT[part * H:(part + 1) * H, :]).then_inc(z["max_rows"], 16)
                sp.wait_ge(at[1]["o_added"], b + 1)
                sp.dma_start(gu_s, a["gu_s"].rearrange("(k p) n -> p k n", p=P)).then_inc(s["shared_in"], 16)
                sp.dma_start(down_s, a["down_s"].rearrange("(k p) n -> p k n", p=P)).then_inc(s["shared_in"], 16)
                sp.wait_ge(s["slots_ready"], b + 1)
                sp.dma_start(xw_table[ds(b * T, T), :].rearrange("(t p) n -> p t n", p=P), xw[:, :, :]
                             ).then_inc(s["xw_stored"], 16)
                sp.wait_ge(s["y_added"], (b + 1) * (E0 + 1))
                sp.dma_start(acc_table[ds(b * T, T), :].rearrange("(t p) n -> p t n", p=P), x[:, :, :]
                             ).then_inc(s["row_stored"], 16)
                sp.wait_ge(s["xw_stored"], (b + 1) * 16)
                sp.wait_ge(s["row_stored"], (b + 1) * 16)
                wait_apart(sp, s["tok_scattered"], (b + 1) * 16 * 8 * TT)
            experts_load(sp)

        @block.gpsimd
        def _(pool):
            pool.memset(wo[0][:, :, :], 0.0).then_inc(s["wo_zeroed"], 1)
            pool.memset(wo[1][:, :, :], 0.0).then_inc(s["wo_zeroed"], 1)
            pool.iota(slots_init, pattern=[[0, E1]], base=NTOK, channel_multiplier=1).then_inc(s["tables_made"], 1)
            pool.memset(zeros, 0.0).then_inc(s["tables_made"], 1)
            pool.memset(half[:, :], -0.5).then_inc(s["half_made"], 1)
            pool.wait_ge(s["half_made"], 1)
            pool.wait_ge(s["table_filled"], 48)
            with pool.Fori(0, B) as b:
                for z in range(4):
                    pool.wait_ge(s["var_ready"], b * 4 + z + 1)
                    pool.tensor_tensor(rstd[:, :], var[:, :], half[:, :], ALU.pow).then_inc(s["rstd_ready"], 1)
                wait_apart(pool, s["slots_ready"], b + 1)
                for t in range(TT):
                    for k in range(8):
                        pool.indirect_dma_start(
                            out=slot_token, out_offset=bass.IndirectOffsetOnAxis(
                                ap=slots[:, t, k:k + 1].bitcast(U32), axis=0),
                            in_=tok_i[:, t:t + 1], in_offset=None,
                            bounds_check=CAP * E1 - 1, oob_is_err=False).then_inc(s["tok_scattered"], 16)
                wait_apart(pool, s["tok_scattered"], (b + 1) * 16 * 8 * TT)
            experts_dma(pool)

        @block.tensor
        def _(pe):
            pe.wait_ge(s["consts_made"], 1)
            pe.wait_ge(s["active_made"], 3)
            pe.matmul(mm[0:1, 0:S // P], ones_f[:, 0:1], work[:, 2048:2048 + S // P], start=True, stop=True)
            pe.matmul(mm[0:1, 16:16 + B * NCH], work[0:B * NCH, 2064:2065], ident[0:B * NCH, 0:B * NCH],
                      start=True, stop=True).then_inc(s["active_ps"], 1)
            pe.wait_ge(s["mask_made"], 1)
            for t in range(TT):
                for c in range(S // P):
                    last = pe.matmul(mm[:, 512 + t:513 + t], mask01[:, c, t * P:(t + 1) * P], ones_b[:, 0:1],
                                     start=(c == 0), stop=(c == S // P - 1))
            last.then_inc(s["row_ps"], 1)
            pe.wait_ge(s["weights_in"], N_WEIGHTS * 16)
            pe.wait_ge(s["info_made"], 1)

            def tokens_to_columns(b, z):
                pe.wait_ge(s["xn_ready"], b * 4 + z + 1)
                for k in range(KD):
                    for t in range(TT):
                        last = pe.transpose(m_xT[:, k, t * P:(t + 1) * P], xw[:, t, k * P:(k + 1) * P], ident)
                last.then_inc(s["xnT_ps"], 1)
                pe.wait_ge(s["xnT_ready"], b * 4 + z + 1)

            def attention(b, l):
                z = at[l]
                n, first, before = units(pe, b, l)
                with pe.Fori(0, n) as i:
                    u = unit_of(pe, before, i)
                    pe.wait_ge(z["ctx_in"], (u + 1) * (32 if l else 16))
                    for m in range(KD):
                        for k in range(KD):
                            last = pe.matmul(y_k[:, m, :], wk[l][:, k, m * P:(m + 1) * P], ctxc[:, k, :],
                                             start=(k == 0), stop=(k == KD - 1))
                    last.then_inc(z["kv_ps"], 1)
                    for t in range(KT):
                        if l:
                            pe.matmul(y_v[:, t, :], ones_f[0:1, :], bvo[:, 0, :], start=True, stop=False)
                        for k in range(KD):
                            last = pe.matmul(y_v[:, t, :], ctxc[:, k, t * P:(t + 1) * P], wv[l][:, k, :],
                                             start=(k == 0 and not l), stop=(k == KD - 1))
                    last.then_inc(z["kv_ps"], 1)
                    pe.wait_ge(z["v_kept"], u + 1)
                    pe.wait_ge(z["k_split"], u + 1)
                tokens_to_columns(b, 2 * l)
                for m in range(KD):
                    for k in range(KD):
                        last = pe.matmul(y_q[:, m, :], wq[l][:, k, m * P:(m + 1) * P], xnT[:, k, :],
                                         start=(k == 0), stop=(k == KD - 1))
                last.then_inc(z["q_ps"], 1)
                wait_apart(pe, z["q_stacked"], (b + 1) * 96)
                with pe.Fori(0, n) as i:
                    u = unit_of(pe, before, i)
                    chunk = chunk_of(pe, first, i)
                    rows = ROW_MAX if l else ROW_NEG
                    pe.wait_ge(z["k_stacked"], (u + 1) * 16 * K_DMAS)
                    for h in range(H):
                        pe.wait_ge(z["a_read"], u * H + (h + 1))
                        for t in range(TT):
                            last = pe.matmul(sc_a[h % 2][:, t, :], q_stack[0:rows, h, t * P:(t + 1) * P],
                                             k_stack[0:rows, h, ds(i * CH, CH)], start=True, stop=bool(l))
                            if not l:
                                for c in range(KT):
                                    last = pe.matmul(sc_a[h % 2][:, t, c * P:(c + 1) * P],
                                                     mask0[:, ds(chunk * KT + c, 1), t * P:(t + 1) * P
                                                           ].rearrange("p c t -> p (c t)"),
                                                     ident_b[:, :], start=False, stop=(c == KT - 1))
                        last.then_inc(z["a_scores"], 1)
                wait_apart(pe, z["max_split"], b + 1)
                for t in range(TT):
                    last = pe.transpose(m_mT[:, t * P:(t + 1) * P], msp[:, t, :, :].rearrange("p a h -> p (a h)"),
                                        ident_b[:, :])
                last.then_inc(z["mT_ps"], 1)
                wait_apart(pe, z["max_rows"], (b + 1) * 48)

                def values(u, g):
                    pe.wait_ge(z["exp_done"], u * H + 4 * (g + 1))
                    pe.wait_ge(z["ot_added"], u * G + (g + 1))
                    for k in range(KT):
                        for j in range(4):
                            last = pe.matmul(m_pv[g % 2][32 * j:32 * j + 32, :], v_now[:, k, 4 * g + j, :],
                                             probs[:, 4 * (g % 2) + j, k, :], start=(k == 0),
                                             stop=(k == KT - 1), tile_position=(0, 32 * j))
                    last.then_inc(z["pv_done"], 1)

                with pe.Fori(0, n) as i:
                    u = unit_of(pe, before, i)
                    chunk = chunk_of(pe, first, i)
                    pe.wait_ge(z["v_placed"], u + 1)
                    for h in range(H):
                        pe.wait_ge(z["exp_done"], u * H + (h + 1) - 2) if h >= 2 else None
                        for c in range(KT):
                            last = pe.matmul(sc_b[h % 2][:, c, :], k_stack[0:ROW_END, h, ds(i * CH + c * P, P)],
                                             q_stack[0:ROW_END, h, :], start=True, stop=bool(l))
                            if not l:
                                last = pe.matmul(sc_b[h % 2][:, c, :], ident_b[:, :],
                                                 mask0[:, ds(chunk * KT + c, 1), :
                                                       ].rearrange("p c t -> p (c t)"), start=False, stop=True)
                        last.then_inc(z["b_scores"], 1)
                        if h >= 5 and h % 4 == 1:
                            values(u, h // 4 - 1)
                    values(u, G - 1)
                pe.wait_ge(z["ot_added"], (before + n) * G + 2)
                for g in range(G):
                    pe.matmul(sc[:, g // 2, (g % 2) * 512:(g % 2) * 512 + 512], sel, ot[:, g, :],
                              start=True, stop=True).then_inc(z["den_ps"], 1)
                pe.wait_ge(z["otn_ready"], (b + 1) * G)
                for t in range(TT):
                    if l:
                        pe.matmul(y_rows[:, t, :], ones_f[0:1, :], bvo[:, 1, :], start=True, stop=False)
                    for g in range(G):
                        last = pe.matmul(y_rows[:, t, :], otn[:, g, t * P:(t + 1) * P], wo[l][:, g, :],
                                         start=(g == 0 and not l), stop=(g == G - 1))
                last.then_inc(z["o_ps"], 1)

            def pair(b, p, gate, up):
                if p >= 2:
                    pe.wait_ge(s["act_ready"], b * PAIRS + p - 1)
                for half_, w in enumerate((gate, up)):
                    for k in range(KD):
                        last = pe.matmul(sc[:, p % 2, half_ * 512:half_ * 512 + 512], w(k), xnT[:, k, :],
                                         start=(k == 0), stop=(k == KD - 1))
                last.then_inc(s["pair_ready"], 1)

            def down(b, e, act, w, nk, pairs):
                pe.wait_ge(s["act_ready"], b * PAIRS + pairs)
                if e:
                    pe.wait_ge(s["y_added"], b * (E0 + 1) + e)
                for t in range(TT):
                    for k in range(nk):
                        last = pe.matmul(y_rows[:, t, :], act[:, k, t * P:(t + 1) * P], w(k),
                                         start=(k == 0), stop=(k == nk - 1))
                last.then_inc(s["y_ready"], 1)

            with pe.Fori(0, B) as b:
                attention(b, 0)
                tokens_to_columns(b, 1)
                pe.wait_ge(s["experts_in"], 2 * E0 * 16)
                for t in range(TT):
                    for k in range(KD):
                        last = pe.matmul(m_l0[:, t, :], xnT[:, k, t * P:(t + 1) * P], gate0[:, k, :],
                                         start=(k == 0), stop=(k == KD - 1))
                last.then_inc(s["router_ps"], 1)
                for e in range(E0 + 1):
                    if e < E0:
                        for f in range(2):
                            pair(b, 2 * e + f, lambda k: gu0[:, e, k, f * P:(f + 1) * P],
                                 lambda k: gu0[:, e, k, D + f * P:D + (f + 1) * P])
                    if e:
                        down(b, e - 1, act0[:, (e - 1) % 2], lambda k: down0[:, e - 1, k, :], KD, 2 * e)
                attention(b, 1)
                tokens_to_columns(b, 3)
                for t in range(TT):
                    for k in range(KD):
                        last = pe.matmul(m_l1[:, t, :], xnT[:, k, t * P:(t + 1) * P], gate1[:, k, :],
                                         start=(k == 0), stop=(k == KD - 1))
                last.then_inc(s["router_ps"], 1)
                pe.wait_ge(s["shared_in"], (b + 1) * 32)
                for j in range(SHK):
                    pair(b, 2 * E0 + j, lambda k: gu_s[:, k, j * P:(j + 1) * P],
                         lambda k: gu_s[:, k, (SHK + j) * P:(SHK + j + 1) * P])
                pe.wait_ge(s["chosen_ready"], b + 1)
                for t in range(TT):
                    for c in range(t):
                        pe.matmul(m_pos[:, t, :], ones_b[:, :], chosen[:, c, :], start=(c == 0), stop=False)
                    pe.matmul(m_pos[:, t, :], tri_b[:, :], chosen[:, t, :], start=(t == 0), stop=True)
                for t in range(TT):
                    last = pe.matmul(m_cnt, ones_b[:, :], chosen[:, t, :], start=(t == 0), stop=(t == TT - 1))
                last.then_inc(s["pos_ps"], 1)
                down(b, E0, act1, lambda k: down_s[:, k, :], SHK, PAIRS)
            experts_pe(pe)

        @block.scalar
        def _(act):
            act.wait_ge(s["info_made"], 1)

            def columns_kept(b, z):
                act.wait_ge(s["xnT_ps"], b * 4 + z + 1)
                act.activation(xnT[:, :, :], m_xT, ACT.Copy).then_inc(s["xnT_ready"], 1)

            def attention(b, l):
                z = at[l]
                n, first, before = units(act, b, l)
                with act.Fori(0, n) as i:
                    u = unit_of(act, before, i)
                    act.wait_ge(z["kv_ps"], 2 * u + 2)
                    act.activation(v_all[:, ds(i * KT, KT), :], y_v, ACT.Copy).then_inc(z["v_kept"], 1)
                columns_kept(b, 2 * l)
                act.wait_ge(z["mT_ps"], b + 1)
                act.activation(mT[:, :], m_mT, ACT.Copy).then_inc(z["mT_kept"], 1)
                act.wait_ge(z["v_kept"], before + n)
                with act.Fori(0, n) as i:
                    u = unit_of(act, before, i)
                    act.wait_ge(z["pv_done"], u * G + 1)
                    act.activation(v_now[:, :, :, 0:DH], v_all[:, ds(i * KT, KT), :].rearrange(
                        "p k (h d) -> p k h d", d=DH), ACT.Copy).then_inc(z["v_placed"], 1)
                    for h in range(H):
                        act.wait_ge(z["b_scores"], u * H + h + 1)
                        if h % 4 == 0 and h >= 8:
                            act.wait_ge(z["pv_done"], u * G + h // 4)
                        act.activation(probs[:, 4 * (h // 4 % 2) + h % 4, :, :], sc_b[h % 2], ACT.Exp
                                       ).then_inc(z["exp_done"], 1)

            def gated(b, p):
                act.wait_ge(s["pair_ready"], b * PAIRS + p + 1)
                act.activation(silu[:, p % 2, :], sc[:, p % 2, 0:512], ACT.Silu).then_inc(s["silu_ready"], 1)

            with act.Fori(0, B) as b:
                attention(b, 0)
                columns_kept(b, 1)
                act.wait_ge(s["router_sub"], b * 2 + 1)
                act.activation(r8[:, 1], r8[:, 0], ACT.Exp).then_inc(s["router_exp"], 1)
                for p in range(2 * E0):
                    gated(b, p)
                attention(b, 1)
                columns_kept(b, 3)
                act.wait_ge(s["router_sub"], b * 2 + 2)
                act.activation(small[:, 8], small[:, 7], ACT.Exp, scale=-1.0)
                act.activation(r64[:, 2], r64[:, 1], ACT.Exp).then_inc(s["router_exp"], 1)
                for p in range(2 * E0, PAIRS):
                    gated(b, p)
            experts_act(act)

        @block.vector
        def _(dve):
            pro = Steps(dve, s["prologue_step"], 0, 64)
            dve.memset(ones_b[:, :], 1.0)
            dve.memset(ones_f[:, :], 1.0)
            dve.memset(carry[:, :], 0.0)
            dve.memset(v_now[:, :, :, DH:DH + 1], 1.0)
            dve.memset(v_now[:, :, :, DH + 1:32], 0.0)
            dve.memset(work[:, 6144:6400], 1.0)
            dve.memset(q_stack[ROW_NEG:P, :, :], 1.0)
            dve.wait_ge(s["consts_in"], 16)
            dve.tensor_copy(tok_f[:, :], consts[:, C_TOK:C_TOK + TT])
            dve.tensor_copy(ident_b[:, :], ident)
            pro.step(dve.memset(small[:, 0], 0.0))
            pro.settle()
            dve.tensor_scalar(key_rows0[ROW_NEG:P, :], work[ROW_NEG:P, 6144:6400], 0.0,
                              consts[ROW_NEG:P, C_NEG + 2:C_NEG + 3], ALU.mult, ALU.add)
            dve.tensor_copy(tri_b[:, :], consts[:, C_TRI:C_TRI + P]).then_inc(s["consts_made"], 1)
            dve.wait_ge(s["masks_in"], 32)
            m_u8 = work[:, 0:1024].bitcast(U8).rearrange("p (c t) -> p c t", c=S // P)
            key_any = work[:, 2048:2048 + S // P]
            dve.tensor_reduce(key_any, m_u8, AX.X, ALU.max).then_inc(s["active_made"], 1)
            pro.step(dve.tensor_scalar(work[0:B * NCH, 1536:1536 + CH],
                                       work[0:B * NCH, 1024:1024 + CH].bitcast(I32), 0.0, None, ALU.not_equal))
            pro.settle()
            dve.tensor_reduce(work[0:B * NCH, 2064:2065], work[0:B * NCH, 1536:1536 + CH], AX.X, ALU.max
                              ).then_inc(s["active_made"], 1)
            dve.tensor_copy(mask01, m_u8).then_inc(s["mask_made"], 1)
            dve.tensor_scalar(mask0[:, :, :], m_u8, -1.0, -MASKED, ALU.add, ALU.mult).then_inc(s["active_made"], 1)
            dve.wait_ge(s["row_ps"], 1)
            dve.wait_ge(s["active_ps"], 1)
            pro.step(dve.tensor_scalar(small[:, 0], mm[:, 512:512 + TT], 1.0, None, ALU.min))
            pro.settle()
            pro.step(dve.reciprocal(small[:, 1], small[:, 0]))
            pro.settle()
            dve.tensor_scalar(nan_bias[:, :], small[:, 1], 0.0, None, ALU.mult)
            seen = work[0:1, 4224:4224 + 2 * B * NCH].rearrange("o (l b c) -> o l b c", l=2, b=B)
            for b in range(B):
                dve.tensor_reduce(seen[:, 0, b, :], mm[0:1, 0:S // P].rearrange("o (c k) -> o c k", k=KT),
                                  AX.X, ALU.max)
            pro.step(dve.tensor_copy(seen[:, 1], mm[0:1, 16:16 + B * NCH].rearrange("o (b c) -> o b c", b=B)))
            pro.settle()
            flat = work[0:1, 4224:4224 + 2 * B * NCH].rearrange("o (n c) -> o n c", c=NCH)
            up = work[0:1, 4352:4352 + 2 * B * NCH].rearrange("o (n c) -> o n c", c=NCH)
            down_ = work[0:1, 4608:4608 + 2 * B * NCH].rearrange("o (n c) -> o n c", c=NCH)
            pro.step(dve.tensor_scalar(flat, flat, 1.0, None, ALU.min))
            pro.settle()
            for c in range(NCH):
                dve.tensor_scalar(up[:, :, c], flat[:, :, c], float(c + 1), None, ALU.mult)
                pro.step(dve.tensor_scalar(down_[:, :, c], flat[:, :, c], float(NCH - c), None, ALU.mult))
            pro.settle()
            NB = 2 * B
            row = lambda k: work[0:1, 5120 + 64 * k:5120 + 64 * k + NB]
            dve.tensor_reduce(row(0), up, AX.X, ALU.max)
            pro.step(dve.tensor_reduce(row(1), down_, AX.X, ALU.max))
            pro.settle()
            pro.step(dve.tensor_scalar(row(2), row(0), 0.0, float(NCH), ALU.is_equal, ALU.mult))
            pro.settle()
            dve.tensor_tensor(row(3), row(0), row(2), ALU.add)
            pro.step(dve.tensor_tensor(row(4), row(1), row(2), ALU.add))
            pro.settle()
            pro.step(dve.tensor_scalar(row(5), row(4), -1.0, float(NCH), ALU.mult, ALU.add))
            pro.settle()
            dve.memset(work[0:1, 6144:6144 + B], 1.0)
            pro.step(dve.tensor_tensor(row(6), row(3), row(5), ALU.subtract))
            pro.settle()
            for l in range(2):
                pro.step(dve.tensor_tensor_scan(row(7)[:, l * B:(l + 1) * B], work[0:1, 6144:6144 + B],
                                                row(6)[:, l * B:(l + 1) * B], 0.0, ALU.mult, ALU.add))
            pro.settle()
            pro.step(dve.tensor_tensor(row(8), row(7), row(6), ALU.subtract))
            pro.settle()
            for k, r in enumerate((6, 5, 8)):
                last = dve.tensor_copy(info[:, :, k, :], row(r).rearrange("o (l b) -> o l b", l=2))
            last.then_inc(s["info_made"], 1)
            for z in at:
                dve.sem_inc(z["a_read"], 2)
                dve.sem_inc(z["ot_added"], 2)
                dve.sem_inc(z["pv_done"], 1)
            dve.sem_inc(s["ew_used"], EU)
            dve.wait_ge(s["info_made"], 1)
            dve.wait_ge(s["weights_in"], N_WEIGHTS * 16)

            def layer_norm(b, z, st):
                if z == 0:
                    dve.wait_ge(s["x_loaded"], (b + 1) * 16)
                for t in range(TT):
                    st.step(dve.bn_stats(stats[:, t, :], x[:, t, :]))
                st.settle(s["waits_passed"])
                for t in range(TT):
                    st.step(dve.bn_aggr(mv[:, t, :], stats[:, t, :]))
                st.settle()
                dve.tensor_scalar(var[:, :], mv[:, :, 1], LN_EPS, None, ALU.add).then_inc(s["var_ready"], 1)
                dve.wait_ge(s["rstd_ready"], b * 4 + z + 1)
                for t in range(TT):
                    last = dve.tensor_scalar(xw[:, t, 0:D], x[:, t, :], mv[:, t, 0:1], rstd[:, t:t + 1],
                                             ALU.subtract, ALU.mult)
                last.then_inc(s["xn_ready"], 1)

            def split(st, f, r, parts, done):
                st.settle()
                st.step(dve.tensor_copy(parts[:, 0], f))
                st.settle()
                st.step(dve.tensor_tensor(r, f, parts[:, 0], ALU.subtract))
                st.settle()
                st.step(dve.tensor_copy(parts[:, 1], r))
                st.settle()
                dve.tensor_tensor(parts[:, 2], r, parts[:, 1], ALU.subtract).then_inc(done, 1)

            def attention(b, l, st):
                z = at[l]
                n, first, before = units(dve, b, l)
                with dve.Fori(0, n) as i:
                    u = unit_of(dve, before, i)
                    kv = Steps(dve, z["kv_step"], u * 16, 16)
                    if l:
                        dve.wait_ge(z["ctx_in"], (u + 1) * 32)
                        kv.step(dve.tensor_scalar(keym, keym_i, 0.0, None, ALU.not_equal))
                        kv.settle()
                        kv.step(dve.tensor_scalar(key_rows[1][ROW_NEG:P, :], keym[ROW_NEG:P, :],
                                                  consts[ROW_NEG:P, C_NEG:C_NEG + 1],
                                                  consts[ROW_NEG:P, C_NEG + 1:C_NEG + 2], ALU.mult, ALU.add))
                    dve.wait_ge(z["kv_ps"], 2 * u + 2)
                    if l:
                        for m in range(KD):
                            kv.step(dve.scalar_tensor_tensor(
                                out=kf[:, m, :], in0=y_k[:, m, :], scalar=bqk[:, 1, m:m + 1], in1=keym,
                                op0=ALU.add, op1=ALU.mult))
                    else:
                        kv.step(dve.tensor_copy(kf, y_k))
                    split(kv, kf, kr, ksp, z["k_split"])
                    kv.fill()
                layer_norm(b, 2 * l, st)
                dve.wait_ge(z["q_ps"], b + 1)
                for m in range(KD):
                    if l:
                        st.step(dve.tensor_scalar(qf[:, m, :], y_q[:, m, :], bqk[:, 0, m:m + 1], DH ** -0.5,
                                                  ALU.add, ALU.mult))
                    else:
                        st.step(dve.tensor_scalar(qf[:, m, :], y_q[:, m, :], DH ** -0.5, None, ALU.mult))
                split(st, qf, qr, qsp, z["q_split"])
                st.step(dve.memset(mx[:, :, :], LOWEST))
                st.settle(s["waits_passed"])
                with dve.Fori(0, n) as i:
                    u = unit_of(dve, before, i)
                    for h in range(H):
                        dve.wait_ge(z["a_scores"], u * H + h + 1)
                        dve.tensor_reduce(mxu[:, :, h], sc_a[h % 2], AX.X, ALU.max).then_inc(z["a_read"], 1)
                    dve.wait_ge(z["a_read"], u * H + H + 2)
                    dve.tensor_tensor(mx[:, :, :], mx[:, :, :], mxu[:, :, :], ALU.max).then_inc(z["a_step"], 1)
                    dve.wait_ge(z["a_step"], u + 1)
                mx2, mr2 = mx[:, :, :], mres[:, :, :]
                st.step(dve.tensor_scalar(mx2, mx2, -1.0, None, ALU.mult))
                st.settle()
                st.step(dve.tensor_copy(msp[:, :, 0, :], mx2))
                st.settle()
                st.step(dve.tensor_tensor(mr2, mx2, msp[:, :, 0, :], ALU.subtract))
                st.settle()
                st.step(dve.tensor_copy(msp[:, :, 1, :], mr2))
                st.settle()
                dve.tensor_tensor(msp[:, :, 2, :], mr2, msp[:, :, 1, :], ALU.subtract).then_inc(z["max_split"], 1)
                st.step(dve.memset(ot[:, :, :], 0.0))
                st.settle(s["waits_passed"])
                with dve.Fori(0, n) as i:
                    u = unit_of(dve, before, i)
                    for g in range(G):
                        dve.wait_ge(z["pv_done"], u * G + g + 2)
                        dve.tensor_tensor(ot[:, g, :], m_pv[g % 2], ot[:, g, :], ALU.add).then_inc(z["ot_added"], 1)
                    dve.wait_ge(z["ot_added"], u * G + G + 2)
                for g in range(G):
                    dve.wait_ge(z["den_ps"], b * G + g + 1)
                    st.step(dve.reciprocal(rcp[:, g % 2, :], sc[:, g // 2, (g % 2) * 512:(g % 2) * 512 + 512]))
                    st.settle()
                    dve.tensor_tensor(otn[:, g, :], ot[:, g, :], rcp[:, g % 2, :], ALU.mult
                                      ).then_inc(z["otn_ready"], 1)
                dve.wait_ge(z["o_ps"], b + 1)
                for t in range(TT):
                    if l == 0:
                        last = dve.scalar_tensor_tensor(out=x[:, t, :], in0=y_rows[:, t, :],
                                                        scalar=nan_bias[:, t:t + 1], in1=x[:, t, :],
                                                        op0=ALU.add, op1=ALU.add)
                    else:
                        last = dve.tensor_tensor(x[:, t, :], y_rows[:, t, :], x[:, t, :], ALU.add)
                last.then_inc(z["o_added"], 1)
                dve.wait_ge(z["o_added"], b + 1)

            def gated(b, p, dst):
                dve.wait_ge(s["silu_ready"], b * PAIRS + p + 1)
                dve.tensor_tensor(dst, sc[:, p % 2, 512:1024], silu[:, p % 2, :], ALU.mult
                                  ).then_inc(s["act_ready"], 1)

            def weigh(b, e, w):
                dve.wait_ge(s["y_ready"], b * (E0 + 1) + e + 1)
                for t in range(TT):
                    last = dve.scalar_tensor_tensor(out=x[:, t, :], in0=y_rows[:, t, :], scalar=w(t),
                                                    in1=x[:, t, :], op0=ALU.mult, op1=ALU.add)
                last.then_inc(s["y_added"], 1)
                dve.wait_ge(s["y_added"], b * (E0 + 1) + e + 1)

            def softmax_terms(st, b, which, logits, sub, n):
                dve.wait_ge(s["router_ps"], b * 2 + which + 1)
                st.step(dve.tensor_reduce(small[:, 0], logits, AX.X, ALU.max))
                st.settle()
                for t in range(TT):
                    last = dve.tensor_scalar(sub[:, t, :], logits[:, t, :], small[:, 0, t:t + 1], None,
                                             ALU.subtract)
                return last

            def router0(b, st):
                p_, oh, oh2, m8 = r8[:, 2], r8[:, 3], r8[:, 4], r8[:, 5]
                softmax_terms(st, b, 0, m_l0, r8[:, 0], E0).then_inc(s["router_sub"], 1)
                dve.wait_ge(s["router_exp"], b * 2 + 1)
                st.step(dve.tensor_reduce(small[:, 1], r8[:, 1], AX.X, ALU.add))
                st.settle()
                st.step(dve.reciprocal(small[:, 2], small[:, 1]))
                st.settle()
                for t in range(TT):
                    st.step(dve.tensor_scalar(p_[:, t, :], r8[:, 1, t, :], small[:, 2, t:t + 1], None, ALU.mult))
                st.settle(s["waits_passed"])
                for t in range(TT):
                    st.step(dve.max(m8[:, t, :], p_[:, t, :]))
                st.settle(s["waits_passed"])
                for t in range(TT):
                    st.step(dve.max_index(ix[:, t, :], m8[:, t, :], p_[:, t, :]))
                st.step(dve.tensor_tensor(small[:, 3], m8[:, :, 0], m8[:, :, 1], ALU.add))
                st.settle()
                st.step(dve.tensor_copy(r8[:, 0], ix[:, :, :]))
                st.step(dve.tensor_scalar(small[:, 4], small[:, 3], ROUTE_EPS, None, ALU.add))
                st.settle()
                st.step(dve.reciprocal(small[:, 5], small[:, 4]))
                for t in range(TT):
                    for k, o in enumerate((oh, oh2)):
                        st.step(dve.scalar_tensor_tensor(
                            out=o[:, t, :], in0=consts[:, C_I8:C_I8 + 8], scalar=r8[:, 0, t, k:k + 1],
                            in1=p_[:, t, :], op0=ALU.is_equal, op1=ALU.mult))
                st.settle()
                st.step(dve.tensor_tensor(oh, oh, oh2, ALU.add))
                st.settle()
                for t in range(TT):
                    st.step(dve.tensor_scalar(oh2[:, t, :], oh[:, t, :], small[:, 5, t:t + 1], None, ALU.mult))
                st.settle()
                st.step(dve.tensor_reduce(small[:, 1], oh2, AX.X, ALU.add))
                st.settle()
                st.step(dve.tensor_scalar(small[:, 2], small[:, 1], ROUTE_EPS, None, ALU.add))
                st.settle()
                st.step(dve.reciprocal(small[:, 3], small[:, 2]))
                st.settle()
                for t in range(TT):
                    st.step(dve.tensor_scalar(oh[:, t, :], oh2[:, t, :], small[:, 3, t:t + 1], None, ALU.mult))
                st.settle()
                return oh

            def router1(b, st):
                lg, sub, ex, mk = r64[:, 0], r64[:, 1], r64[:, 2], r64[:, 3]
                m8 = r8[:, 5]
                dve.wait_ge(s["router_ps"], b * 2 + 2)
                st.step(dve.tensor_copy(lg, m_l1[:, :, 0:E1]))
                st.step(dve.tensor_copy(small[:, 7], m_l1[:, :, E1]))
                st.settle(s["waits_passed"])
                for t in range(TT):
                    st.step(dve.max(m8[:, t, :], lg[:, t, :]))
                st.settle()
                for t in range(TT):
                    last = dve.tensor_scalar(sub[:, t, :], lg[:, t, :], m8[:, t, 0:1], None, ALU.subtract)
                last.then_inc(s["router_sub"], 1)
                for t in range(TT):
                    st.step(dve.match_replace(mk[:, t, :], m8[:, t, :], lg[:, t, :], LOWEST))
                st.settle()
                st.step(dve.tensor_tensor(r64[:, 4], mk, lg, ALU.not_equal))
                st.settle()
                dve.tensor_copy(chosen[:, :, :], r64[:, 4]).then_inc(s["chosen_ready"], 1)
                dve.wait_ge(s["router_exp"], b * 2 + 2)
                st.step(dve.tensor_tensor(sub, ex, r64[:, 4], ALU.mult))
                st.step(dve.tensor_scalar(small[:, 9], small[:, 8], 1.0, None, ALU.add))
                st.settle()
                st.step(dve.tensor_reduce(small[:, 1], sub, AX.X, ALU.add))
                st.step(dve.reciprocal(small[:, 10], small[:, 9]))
                st.settle()
                st.step(dve.reciprocal(small[:, 2], small[:, 1]))
                st.settle()
                for t in range(TT):
                    st.step(dve.tensor_scalar(xw[:, t, D:XW], sub[:, t, :], small[:, 2, t:t + 1], None, ALU.mult))
                st.settle()

            def dispatch(b, st):
                pos, ok, val = r64[:, 0], r64[:, 1], r64[:, 3]
                d8, far = r8[:, 0], r8[:, 1]
                dve.wait_ge(s["pos_ps"], b + 1)
                for t in range(TT):
                    st.step(dve.tensor_tensor(pos[:, t, :], m_pos[:, t, :], carry[:, :], ALU.add))
                st.settle()
                st.step(dve.tensor_tensor(carry[:, :], m_cnt, carry[:, :], ALU.add))
                st.step(dve.scalar_tensor_tensor(out=ok, in0=pos, scalar=float(CAP), in1=r64[:, 4],
                                                 op0=ALU.is_lt, op1=ALU.mult))
                for t in range(TT):
                    st.step(dve.scalar_tensor_tensor(out=val[:, t, :], in0=pos[:, t, :], scalar=float(E1),
                                                     in1=consts[:, C_E1:C_E1 + E1], op0=ALU.mult, op1=ALU.add))
                st.settle()
                st.step(dve.tensor_tensor(sub_ := r64[:, 2], val, ok, ALU.mult))
                st.settle(s["waits_passed"])
                for t in range(TT):
                    st.step(dve.max(d8[:, t, :], sub_[:, t, :]))
                st.settle()
                st.step(dve.tensor_scalar(far, d8, 0.0, FAR, ALU.is_equal, ALU.mult))
                st.settle()
                st.step(dve.scalar_tensor_tensor(out=slots[:, :, :], in0=d8, scalar=-1.0, in1=far,
                                                 op0=ALU.add, op1=ALU.add))
                st.step(dve.tensor_copy(tok_i[:, :], tok_f[:, :]))
                st.settle()
                dve.tensor_scalar(tok_f[:, :], tok_f[:, :], float(T), None, ALU.add).then_inc(s["slots_ready"], 1)

            with dve.Fori(0, B) as b:
                st = Steps(dve, s["dve_step"], b * 512, 512)
                attention(b, 0, st)
                layer_norm(b, 1, st)
                w = router0(b, st)
                for e in range(E0 + 1):
                    if e < E0:
                        for f in range(2):
                            gated(b, 2 * e + f, act0[:, e % 2, f, :])
                    if e:
                        weigh(b, e - 1, lambda t: w[:, t, e - 1:e])
                attention(b, 1, st)
                layer_norm(b, 3, st)
                router1(b, st)
                for j in range(SHK):
                    gated(b, 2 * E0 + j, act1[:, j, :])
                dispatch(b, st)
                weigh(b, E0, lambda t: small[:, 10, t:t + 1])
                st.fill()
            experts_dve(dve)


def constants():
    import numpy as np
    c = np.zeros((P, C_END), np.float32)
    i = np.arange(P)
    c[:, C_ID:C_ID + P] = i[:, None] == i[None, :]
    c[:, C_TRI:C_TRI + P] = i[:, None] < i[None, :]
    c[:, C_SEL:C_SEL + P] = i[:, None] == i[None, :] // 32 * 32 + 16
    c[:, C_E1:C_E1 + 64] = np.arange(1, 65)
    c[:, C_I8:C_I8 + 8] = np.arange(8)
    rest = -1e9
    for part in range(3):
        v = float((np.float32(rest).view(np.uint32) & np.uint32(0xffff0000)).view(np.float32))
        rest -= v
        c[ROW_NEG + part, C_NEG], c[ROW_NEG + part, C_NEG + 1] = -v, v
        c[ROW_MAX + part, C_NEG + 1] = 1.0
        c[ROW_MAX + part, C_NEG + 2] = 1.0
    c[:, C_TOK:C_TOK + 4] = i[:, None] + P * np.arange(4)[None, :]
    return c


def kernel(**inputs):
    import concourse.bacc as bacc
    import numpy as np
    from concourse.bass_utils import run_bass_kernel_spmd

    g = {k: np.asarray(v) for k, v in inputs.items()}
    B, T, D = g["x"].shape
    arrays = {
        "consts": constants(),
        "x": g["x"],
        "ctxT": g["ctx_1024"].transpose(0, 2, 1),
        "mask0T": np.ascontiguousarray(g["mask_SxS2_bk0"].T).view(np.uint32),
        "mask1": g["mask_Bx1x1xS2_ik0"].reshape(B, -1),
        "wq0": g["L0_xattn_wq"].T, "wk0": g["L0_xattn_wk"].T,
        "wv0": g["L0_xattn_wv"].T, "wo0": g["L0_xattn_wo"].T,
        "wq1": g["L1_xattn_Wq"], "wk1": g["L1_xattn_Wk"], "wv1": g["L1_xattn_Wv"], "wo1": g["L1_xattn_Wo"],
        "bqk": np.stack([g["L1_xattn_bq"], g["L1_xattn_bk"]]).reshape(2, D // P, P).transpose(2, 0, 1), "bv": g["L1_xattn_bv"], "bo": g["L1_xattn_bo"],
        "gate0": g["L0_ffn_gate_w"].T, "gu0": g["L0_ffn_gate_up_proj"], "down0": g["L0_ffn_down_proj"],
        "gate1": np.concatenate([g["L1_ffn_gate_w"], g["L1_ffn_shared_gate_w"]], axis=1),
        "gu_s": g["L1_ffn_shared_gate_up_w"], "down_s": g["L1_ffn_shared_down_w"],
        "egu": g["L1_ffn_expert_gate_up_w"], "edown": g["L1_ffn_expert_down_w"],
    }
    arrays = {k: np.ascontiguousarray(v) for k, v in arrays.items()}
    nc = bacc.Bacc("TRN2", target_bir_lowering=False, num_devices=1)
    ap = {k: nc.dram_tensor("in_" + k, v.shape, mybir.dt.from_np(v.dtype), kind="ExternalInput").ap()
          for k, v in arrays.items()}
    for w in ("wq", "wk", "wv", "wo"):
        ap[w] = [ap[w + "0"], ap[w + "1"]]
    out = nc.dram_tensor("out", (B * T, D), F32, kind="ExternalOutput").ap()
    build(nc, ap, out)
    r = run_bass_kernel_spmd(nc, [{"in_" + k: v for k, v in arrays.items()}], core_ids=[0])
    return r.results[0]["out"].reshape(B, T, D)
```

```python
from contextlib import ExitStack

import concourse.bass as bass
from concourse import mybir

F32 = mybir.dt.float32
BF16 = mybir.dt.bfloat16
I32 = mybir.dt.int32
U32 = mybir.dt.uint32
U8 = mybir.dt.uint8
ALU = mybir.AluOpType
ACT = mybir.ActivationFunctionType
AX = mybir.AxisListType
ds = bass.ds

P = 128
PARTS = (0, 0, 1, 1, 0, 2), (0, 1, 0, 1, 2, 0)
ROW_NEG, ROW_MAX, ROW_END = 96, 99, 102
LOWEST = -3.0e38
MASKED = -1.0e30
LN_EPS, ROUTE_EPS = 1e-5, 1e-9
FAR = 1048576.0

C_ID, C_TRI, C_E1, C_I8, C_UP, C_DOWN, C_NEG, C_TOK, C_END = (
    0, 128, 256, 320, 328, 332, 336, 339, 343)


class Steps:

    def __init__(self, engine, sem, base, stride):
        self.engine, self.sem, self.base, self.stride, self.n = engine, sem, base, stride, 0

    def step(self, instruction):
        instruction.then_inc(self.sem, 1)
        self.n += 1

    def settle(self, apart=None):
        self.engine.wait_ge(self.sem, self.base + self.n)
        if apart is not None:
            self.engine.sem_inc(apart, 1)

    def fill(self):
        assert 0 < self.n < self.stride
        self.settle()
        self.engine.sem_inc(self.sem, self.stride - self.n)


def build(nc, a, out):
    B, T, D = a["x"].shape
    S = a["ctxT"].shape[2]
    H = 16
    DH = D // H
    KD = D // P
    TT = T // P
    CH = 256
    NCH = S // CH
    KT = CH // P
    G = H // 4
    E0, E1 = 8, 64
    CAP = 128
    E = (E0, E1)
    TOP = (2, 8)
    WIDTH = (D + E0, D + E1)
    XW = D + E1
    DUMMIES = 2 * P
    NTOK = B * T
    SHK = 4
    EU = 8
    N_WEIGHTS = 2 * 4 + 3 + 2
    K_DMAS = 6 + 1

    with ExitStack() as ctx:
        def sb(name, shape, dt=F32):
            return ctx.enter_context(nc.sbuf_tensor(name, shape, dt))

        def ps(name, shape, dt=F32):
            return ctx.enter_context(nc.psum_tensor(name, shape, dt))

        def sems(text, suffix=""):
            return {n: ctx.enter_context(nc.semaphore(n + suffix)) for n in text.split()}

        q_scratch = nc.dram_tensor("q_scratch", (3, D, T), BF16).ap()
        k_scratch = nc.dram_tensor("k_scratch", (3, D, CH), BF16).ap()
        xw_table = [nc.dram_tensor(f"xw_table_{l}", (NTOK + DUMMIES, WIDTH[l]), F32).ap() for l in range(2)]
        slot_token = [nc.dram_tensor(f"slot_token_{l}", (n, 1), I32).ap() for l, n in enumerate((NTOK * E0, CAP * E1))]
        row_table = [nc.dram_tensor(f"row_table_{l}", (NTOK + DUMMIES, D), F32).ap() for l in range(2)]
        spare = nc.dram_tensor("spare", (1, 1), F32).ap()

        consts = sb("consts", [P, C_END])
        ident = consts[:, C_ID:C_ID + P]
        ident_b = sb("ident_b", [P, P], BF16)
        tri_b = sb("tri_b", [P, P], BF16)
        ones_b = sb("ones_b", [P, P], BF16)
        ones_f = sb("ones_f", [P, P])
        wq = [sb(f"wq{l}", [P, KD, D]) for l in range(2)]
        wk = [sb(f"wk{l}", [P, KD, D]) for l in range(2)]
        wv = [sb(f"wv{l}", [P, KD, D]) for l in range(2)]
        wo = [sb(f"wo{l}", [P, KD, D]) for l in range(2)]
        bqk = sb("bqk", [P, 2, KD])
        bvo = sb("bvo", [1, 2, D])
        gate0 = sb("gate0", [P, KD, E0])
        gate1 = sb("gate1", [P, KD, E1 + 1])
        gu0 = sb("gu0", [P, E0, KD, 2 * D])
        down0 = sb("down0", [P, E0, KD, D])
        mask0 = sb("mask0", [P, S // P, T], BF16)
        nan_bias = sb("nan_bias", [P, TT])
        steps0 = sb("steps0", [1, 2, E0], I32)
        counted = sb("counted", [1, 4, E0])
        idx_all = sb("idx_all", [P, NTOK // P, E0], I32)
        idx_of = sb("idx_of", [P, 3, 2], I32)
        wcol0 = sb("wcol0", [P, 2, E0])
        info = sb("info", [1, 2, 3, B], I32)

        x = sb("x_row", [P, TT, D])
        xw = sb("xw_row", [P, TT, XW])
        xnT = sb("xnT", [P, KD, T])
        q_stack = sb("q_stack", [P, H, T], BF16)
        k_stack = sb("k_stack", [P, H, S], BF16)
        v_all = sb("v_all", [P, S // P, D])
        v_now = sb("v_now", [P, KT, H, 32])
        ot = sb("ot", [P, G, T])
        work = sb("work", [P, 8192])
        stats = sb("stats", [P, TT, 6])
        mv = sb("mv", [P, TT, 2])
        var = sb("var", [P, TT])
        half = sb("half", [P, TT])
        rstd = sb("rstd", [P, TT])
        mx = sb("mx", [P, TT, H])
        mxu = sb("mxu", [P, TT, H])
        mres = sb("mres", [P, TT, H])
        msp = sb("msp", [P, TT, 3, H], BF16)
        rden = sb("rden", [P, TT * H])
        mT = sb("mT", [3 * H, T], BF16)
        small = sb("small", [P, 16, TT])
        r8 = sb("r8", [P, 6, TT, 8])
        ix = sb("ix", [P, TT, 8], U32)
        r64 = sb("r64", [P, 5, TT, E1])
        chosen = sb("chosen", [P, TT, E1], BF16)
        carry = sb("carry", [P, 2, E1])
        slots = sb("slots", [P, TT, 8], I32)
        tok_f = sb("tok_f", [P, TT])
        tok_i = sb("tok_i", [P, TT], I32)

        key_rows0 = sb("key_rows0", [P, CH], BF16)
        probs = work[:, :].rearrange("p (s k t) -> p s k t", s=8, k=KT)
        qf = work[:, 0:1024].rearrange("p (m t) -> p m t", m=KD)
        qr = work[:, 1024:2048].rearrange("p (m t) -> p m t", m=KD)
        qsp = work[:, 2048:3584].bitcast(BF16).rearrange("p (a m t) -> p a m t", a=3, m=KD)
        kf = work[:, 3584:4096].rearrange("p (m t) -> p m t", m=KD)
        kr = work[:, 4096:4608].rearrange("p (m t) -> p m t", m=KD)
        ksp = work[:, 4608:5376].bitcast(BF16).rearrange("p (a m t) -> p a m t", a=3, m=KD)
        ctxc = work[:, 5376:5888].rearrange("p (k t) -> p k t", k=KD)
        keym_i = work[:, 5888:6144].bitcast(I32)
        keym = work[:, 6144:6400]
        key_rows = [key_rows0[:, :], work[:, 6400:6528].bitcast(BF16)]
        on = work[:, 0:1024]
        onT = work[:, 1024:2048].rearrange("p (t k c) -> p t k c", t=TT, k=KD)
        silu = work[:, 2048:3072].rearrange("p (s t) -> p s t", s=2)
        act1 = work[:, 3072:5120].rearrange("p (k t) -> p k t", k=SHK)
        xg0 = work[:, 0:2 * (D + E0)].rearrange("p (s n) -> p s n", s=2)
        xgT0 = work[:, 1024:1536].rearrange("p (s k c) -> p s k c", s=2, k=KD)
        silu0 = work[:, 1536:2048].rearrange("p (s n) -> p s n", s=2)
        act0 = work[:, 2048:2560].rearrange("p (s k c) -> p s k c", s=2, k=KD)
        out0 = work[:, 2560:3072].rearrange("p (s n) -> p s n", s=2)
        mask01 = work[:, 2112:4160].bitcast(BF16).rearrange("p (c t) -> p c t", c=S // P)
        slots_init = [work[:, 6912:7168].bitcast(I32), work[:, 6528:6592].bitcast(I32)]
        zeros = work[:, 6592:6592 + XW]
        xg = work[:, 0:EU * XW].rearrange("p (s n) -> p s n", s=EU)
        xgT = work[:, 2560:3072].rearrange("p (s k c) -> p s k c", s=2, k=KD)
        esilu = work[:, 3072:3328].rearrange("p (s c) -> p s c", s=2)
        eact = work[:, 3328:3584].rearrange("p (s c) -> p s c", s=2)
        eout = work[:, 3584:4096].rearrange("p (s n) -> p s n", s=2)
        ecol = work[:, 4096:4104]
        tok_of = work[:, 4160:4224].bitcast(I32)
        tok_now = work[:, 4224:4232].bitcast(I32)
        ew = gu0[:, :, :, :].rearrange("p e k f -> p e (k f)")
        ew_gu = [ew[:, j, 0:KD * 2 * P].rearrange("p (k f) -> p k f", k=KD) for j in range(EU)]
        ew_down = [ew[:, j, KD * 2 * P:KD * 2 * P + D] for j in range(EU)]
        sh_w = down0[:, :, :, :].rearrange("p e k n -> p (e k n)")
        gu_s = sh_w[:, 0:2048].rearrange("p (k f) -> p k f", k=KD)
        down_s = sh_w[:, 2048:3072].rearrange("p (k n) -> p k n", k=SHK)

        sc = ps("sc", [P, 2, 1024])
        yy = ps("yy", [P, 1024])
        mm = ps("mm", [P, 1024])
        sc_a = [sc[:, s, :].rearrange("p (t k) -> p t k", t=TT) for s in range(2)]
        sc_b = [sc[:, s, :].rearrange("p (k t) -> p k t", k=KT) for s in range(2)]
        y_rows = yy[:, :].rearrange("p (t n) -> p t n", t=TT)
        y_q = yy[:, :].rearrange("p (m t) -> p m t", m=KD)
        y_k = yy[:, 0:512].rearrange("p (m t) -> p m t", m=KD)
        y_v = yy[:, 512:1024].rearrange("p (k n) -> p k n", k=KT)
        m_xT = mm[:, :].rearrange("p (k t) -> p k t", k=KD)
        m_onT = mm[:, :].rearrange("p (t k c) -> p t k c", t=TT, k=KD)
        sc_oT = sc[:, :, :].rearrange("p s n -> p (s n)").rearrange("p (m c) -> p m c", c=32)
        m_pv = [mm[:, 512 * s:512 * s + 512] for s in range(2)]
        m_mT = mm[0:3 * H, 0:T // 2].bitcast(BF16)
        m_logits = [mm[:, 0:TT * n].rearrange("p (t e) -> p t e", t=TT) for n in (E0, E1 + 1)]
        m_cnt = [mm[:, 512 + TT * n:512 + (TT + 1) * n] for n in E]
        m_pos = [mm[:, 512:512 + TT * n].rearrange("p (t e) -> p t e", t=TT) for n in E]

        s = sems("""consts_in weights_in experts_in tables_made half_made waits_passed consts_made
            masks_in active_made active_ps mask_made row_ps info_made table_filled prologue_step
            pair_ready silu_ready act_ready y_ready y_added shared_in
            steps0_ready idx0_in idx0_step xgT0_ps xgT0_kept gu0_ps silu0_ready act0_ready y0_ps
            wcol0_ready out0_ready experts0_added
            tokens_in ew_used tok_col xgT_ps xgT_kept egu_ps esilu_ready eact_ready
            ey_ps ecol_ready ey_ready ey_added copied""")
        xg0_in = [ctx.enter_context(nc.semaphore(f"xg0_in_{j}")) for j in range(2)]
        added0 = [ctx.enter_context(nc.semaphore(f"added0_{j}")) for j in range(2)]
        xg_in = [ctx.enter_context(nc.semaphore(f"xg_in_{j}")) for j in range(EU)]
        ew_in = [ctx.enter_context(nc.semaphore(f"ew_in_{j}")) for j in range(EU)]
        at = [sems("""x_loaded var_ready rstd_ready xn_ready xnT_ps xnT_ready
            router_ps router_sub router_exp chosen_ready pos_ps slots_ready tok_scattered row_stored
            dve_step ctx_in kv_ps k_split k_spilled k_stacked v_kept kv_step q_ps q_split q_spilled
            q_stacked a_scores a_read a_step max_split mT_ps mT_kept max_rows v_placed b_scores
            exp_done pv_done ot_added oT_ps on_ready onT_ps onT_kept o_ps o_added""", f"_{l}") for l in range(2)]

        def units(engine, b, l):
            n = engine.value_load(info[0:1, l, 0, ds(b, 1)], min_val=1, max_val=NCH)
            first = engine.value_load(info[0:1, l, 1, ds(b, 1)], min_val=0, max_val=NCH - 1)
            before = engine.value_load(info[0:1, l, 2, ds(b, 1)], min_val=0, max_val=NCH * B)
            return n, first, before

        def wait_apart(engine, sem, value):
            engine.wait_ge(sem, value)
            engine.sem_inc(s["waits_passed"], 1)

        def chunk_of(engine, first, i):
            return nc.s_assert_within(engine.snap(first + i), 0, NCH - 1, skip_runtime_bounds_check_because="first + how many <= NCH")

        def unit_of(engine, before, i):
            return engine.snap(before + i)

        def steps_of_expert(engine, e):
            n = engine.value_load(steps0[0:1, 0, e:e + 1], min_val=1, max_val=NTOK // P // 2)
            before = engine.value_load(steps0[0:1, 1, e:e + 1], min_val=0, max_val=E0 * NTOK // P // 2)
            return n, before

        def steps_of(b, e):
            return b * EU + e + 1

        def experts_load(sp):
            sp.dma_start(tok_of, slot_token[1].rearrange("(p e) o -> p (e o)", p=P)).then_inc(s["tokens_in"], 16)
            with sp.Fori(0, E1 // EU) as r:
                for j in range(EU):
                    sp.wait_ge(s["ew_used"], steps_of(r, j))
                    sp.dma_start(ew_gu[j], a["egu"][ds(r * EU + j, 1), :, :].rearrange("e (k p) f -> p (e k) f", p=P)
                                 ).then_inc(ew_in[j], 16)
                    sp.dma_start(ew_down[j], a["edown"][ds(r * EU + j, 1), :, :].rearrange("e p n -> p (e n)")
                                 ).then_inc(ew_in[j], 16)
            sp.wait_ge(s["ey_added"], E1 * 16)
            sp.dma_start(out, row_table[1][0:NTOK, :]).then_inc(s["copied"], 16)
            sp.wait_ge(s["copied"], 16)

        def experts_dma(pool):
            with pool.Fori(0, E1 // EU) as r:
                wait_apart(pool, s["tok_col"], r + 1)
                for j in range(EU):
                    pool.indirect_dma_start(
                        out=xg[:, j, :], out_offset=None, in_=xw_table[1],
                        in_offset=bass.IndirectOffsetOnAxis(ap=tok_now[:, j:j + 1].bitcast(U32), axis=0),
                        bounds_check=NTOK + DUMMIES - 1, oob_is_err=True).then_inc(xg_in[j], 16)
                for j in range(EU):
                    wait_apart(pool, s["ey_ready"], steps_of(r, j))
                    if j:
                        wait_apart(pool, s["ey_added"], (r * EU + j) * 16)
                    pool.indirect_dma_start(
                        out=row_table[1], in_=eout[:, j % 2, :], in_offset=None,
                        out_offset=bass.IndirectOffsetOnAxis(ap=tok_now[:, j:j + 1].bitcast(U32), axis=0),
                        bounds_check=NTOK + DUMMIES - 1, oob_is_err=True,
                        compute_op=ALU.add).then_inc(s["ey_added"], 16)

        def experts_pe(pe):
            def columns(r, j):
                pe.wait_ge(xg_in[j], (r + 1) * 16)
                for k in range(KD):
                    last = pe.transpose(mm[:, 512 * (j % 2) + k * P:512 * (j % 2) + (k + 1) * P],
                                        xg[:, j, k * P:(k + 1) * P], ident)
                last.then_inc(s["xgT_ps"], 1)

            def gate_up(r, j):
                pe.wait_ge(s["xgT_kept"], steps_of(r, j))
                pe.wait_ge(ew_in[j], (r + 1) * 32)
                for half_ in range(2):
                    for k in range(KD):
                        last = pe.matmul(sc[:, j % 2, 512 * half_:512 * half_ + CAP],
                                         ew_gu[j][:, k, half_ * P:(half_ + 1) * P], xgT[:, j % 2, k, :],
                                         start=(k == 0), stop=(k == KD - 1))
                last.then_inc(s["egu_ps"], 1)

            def down_(r, j):
                pe.wait_ge(s["eact_ready"], steps_of(r, j))
                pe.matmul(yy[:, 512 * (j % 2):512 * (j % 2) + D], eact[:, j % 2, :], ew_down[j],
                          start=True, stop=True).then_inc(s["ey_ps"], 1)

            with pe.Fori(0, E1 // EU) as r:
                for q in range(EU + 2):
                    if q < EU:
                        columns(r, q)
                    if 1 <= q <= EU:
                        gate_up(r, q - 1)
                    if q >= 2:
                        down_(r, q - 2)

        def experts_act(act):
            with act.Fori(0, E1 // EU) as r:
                for q in range(EU + 1):
                    if q < EU:
                        act.wait_ge(s["xgT_ps"], steps_of(r, q))
                        act.activation(xgT[:, q % 2, :, :], mm[:, 512 * (q % 2):512 * (q % 2) + D].rearrange(
                            "p (k c) -> p k c", k=KD), ACT.Copy).then_inc(s["xgT_kept"], 1)
                    if q >= 1:
                        act.wait_ge(s["egu_ps"], steps_of(r, q - 1))
                        act.activation(esilu[:, (q - 1) % 2, :], sc[:, (q - 1) % 2, 0:CAP], ACT.Silu
                                       ).then_inc(s["esilu_ready"], 1)

        def experts_dve(dve):
            dve.wait_ge(s["tokens_in"], 16)
            with dve.Fori(0, E1 // EU) as r:
                dve.tensor_copy(tok_now, tok_of[:, ds(r * EU, EU)]).then_inc(s["tok_col"], 1)
                for q in range(EU + 1):
                    if q < EU:
                        dve.wait_ge(s["esilu_ready"], steps_of(r, q))
                        dve.tensor_tensor(eact[:, q % 2, :], sc[:, q % 2, 512:512 + CAP], esilu[:, q % 2, :],
                                          ALU.mult).then_inc(s["eact_ready"], 1)
                        dve.tensor_copy(ecol[:, q:q + 1], xg[:, q, ds(r * EU + (D + q), 1)]
                                        ).then_inc(s["ecol_ready"], 1)
                    if q >= 1:
                        j = q - 1
                        dve.wait_ge(s["ey_ps"], steps_of(r, j))
                        dve.wait_ge(s["ecol_ready"], steps_of(r, j))
                        if j >= 2:
                            dve.wait_ge(s["ey_added"], (r * EU + (j - 1)) * 16)
                        dve.tensor_scalar(eout[:, j % 2, :], yy[:, 512 * (j % 2):512 * (j % 2) + D],
                                          ecol[:, j:j + 1], None, ALU.mult).then_inc(s["ey_ready"], 1)
                dve.wait_ge(s["ey_added"], (r + 1) * EU * 16)
                dve.sem_inc(s["ew_used"], EU)

        block = ctx.enter_context(nc.Block())

        @block.sync
        def _(sp):
            def load(dst, src, sem=s["weights_in"]):
                sp.dma_start(dst, src).then_inc(sem, 16)

            load(consts[:, :], a["consts"], s["consts_in"])
            load(work[:, 0:1024].bitcast(U32).rearrange("p (c t) -> p c t", c=S // P),
                 a["mask0T"].rearrange("(c p) t -> p c t", p=P), s["masks_in"])
            load(work[0:B * NCH, 1024:1024 + CH].bitcast(I32), a["mask1"].rearrange("b (c k) -> (b c) k", k=CH), s["masks_in"])
            for l in range(2):
                load(wk[l][:, :, :], a["wk"][l].rearrange("(k p) n -> p k n", p=P))
                load(wv[l][:, :, :], a["wv"][l].rearrange("(k p) n -> p k n", p=P))
                load(wq[l][:, :, :], a["wq"][l].rearrange("(k p) n -> p k n", p=P))
                if l == 0:
                    load(bqk[:, :, :], a["bqk"])
                    load(bvo[:, 0, :], a["bv"].rearrange("(o n) -> o n", o=1))
                    load(bvo[:, 1, :], a["bo"].rearrange("(o n) -> o n", o=1))
                load(wo[l][:, :, :], a["wo"][l].rearrange("(k p) n -> p k n", p=P))
            load(gate0[:, :, :], a["gate0"].rearrange("(k p) n -> p k n", p=P))
            load(gate1[:, :, :], a["gate1"].rearrange("(k p) n -> p k n", p=P))
            for e in range(E0):
                load(gu0[:, e, :, :], a["gu0"][e].rearrange("(k p) n -> p k n", p=P), s["experts_in"])
                load(down0[:, e, :, :], a["down0"][e].rearrange("(k p) n -> p k n", p=P), s["experts_in"])
            sp.wait_ge(s["tables_made"], 3)
            load(slot_token[0].rearrange("(j p e) o -> p j (e o)", p=P, e=E0),
                 slots_init[0].rearrange("p (j e) -> p j e", e=E0), s["table_filled"])
            load(slot_token[1].rearrange("(p e) o -> p (e o)", p=P), slots_init[1], s["table_filled"])
            for l in range(2):
                for d in range(DUMMIES // P):
                    load(xw_table[l][NTOK + d * P:NTOK + (d + 1) * P, :], zeros[:, 0:WIDTH[l]], s["table_filled"])
                    load(row_table[l][NTOK + d * P:NTOK + (d + 1) * P, :], zeros[:, 0:D], s["table_filled"])
            sp.wait_ge(s["table_filled"], 160)
            sp.wait_ge(s["info_made"], 1)

            def rows(l):
                z = at[l]
                source = (a["x"].rearrange("b t n -> (b t) n"), row_table[0])[l]
                with sp.Fori(0, B) as b:
                    sp.dma_start(x[:, :, :], source[ds(b * T, T), :].rearrange("(t p) n -> p t n", p=P)
                                 ).then_inc(z["x_loaded"], 16)
                    n, first, before = units(sp, b, l)
                    with sp.Fori(0, n) as i:
                        u = unit_of(sp, before, i)
                        key0 = chunk_of(sp, first, i) * CH
                        sp.dma_start(ctxc, a["ctxT"][ds(b, 1), :, ds(key0, CH)].rearrange(
                            "b (k p) t -> p (b k) t", p=P)).then_inc(z["ctx_in"], 16)
                        if l:
                            sp.dma_start(keym_i, a["mask1"][ds(b, 1), ds(key0, CH)].partition_broadcast(P)
                                         ).then_inc(z["ctx_in"], 16)
                        sp.wait_ge(z["k_split"], u + 1)
                        sp.dma_start(k_scratch.rearrange("a (m p) t -> p a m t", p=P), ksp
                                     ).then_inc(z["k_spilled"], 16)
                        sp.dma_start(k_stack[ROW_NEG:ROW_END, :, ds(i * CH, CH)],
                                     key_rows[l][ROW_NEG:ROW_END, :].unsqueeze(1).to_broadcast(
                                         (ROW_END - ROW_NEG, H, CH))).then_inc(z["k_stacked"], 16)
                        sp.wait_ge(z["k_spilled"], (u + 1) * 16)
                        for g, part in enumerate(PARTS[1]):
                            sp.dma_start(k_stack[DH * g:DH * (g + 1), :, ds(i * CH, CH)],
                                         k_scratch[part].rearrange("(h d) t -> d h t", d=DH)
                                         ).then_inc(z["k_stacked"], 16)
                        wait_apart(sp, z["k_stacked"], (u + 1) * 16 * K_DMAS)
                    sp.wait_ge(z["q_split"], b + 1)
                    sp.dma_start(q_scratch.rearrange("a (m p) t -> p a m t", p=P), qsp
                                 ).then_inc(z["q_spilled"], 16)
                    sp.wait_ge(z["q_spilled"], (b + 1) * 16)
                    for g, part in enumerate(PARTS[0]):
                        sp.dma_start(q_stack[DH * g:DH * (g + 1), :, :],
                                     q_scratch[part].rearrange("(h d) t -> d h t", d=DH)
                                     ).then_inc(z["q_stacked"], 16)
                    sp.wait_ge(z["q_stacked"], (b + 1) * 96)
                    sp.wait_ge(z["mT_kept"], b + 1)
                    for part in range(3):
                        sp.dma_start(q_stack[ROW_MAX + part:ROW_MAX + part + 1, :, :],
                                     mT[part * H:(part + 1) * H, :]).then_inc(z["max_rows"], 16)
                    sp.wait_ge(z["slots_ready"], b + 1)
                    sp.dma_start(xw_table[l][ds(b * T, T), :].rearrange("(t p) n -> p t n", p=P),
                                 xw[:, :, 0:WIDTH[l]]).then_inc(z["row_stored"], 16)
                    if l:
                        sp.wait_ge(s["y_added"], b + 1)
                    sp.dma_start(row_table[l][ds(b * T, T), :].rearrange("(t p) n -> p t n", p=P), x[:, :, :]
                                 ).then_inc(z["row_stored"], 16)
                    wait_apart(sp, z["row_stored"], (b + 1) * 32)

            rows(0)
            sp.wait_ge(at[0]["tok_scattered"], (B * TOP[0] * TT + 1) * 16)
            sp.dma_start(idx_all[:, :, :], slot_token[0].rearrange("(j p e) o -> p j (e o)", p=P, e=E0)
                         ).then_inc(s["idx0_in"], 16)
            sp.wait_ge(s["experts0_added"], 1)
            sp.dma_start(gu_s, a["gu_s"].rearrange("(k p) n -> p k n", p=P)).then_inc(s["shared_in"], 16)
            sp.dma_start(down_s, a["down_s"].rearrange("(k p) n -> p k n", p=P)).then_inc(s["shared_in"], 16)
            rows(1)
            sp.wait_ge(at[1]["tok_scattered"], (B * TOP[1] * TT + 1) * 16)
            experts_load(sp)

        @block.gpsimd
        def _(pool):
            pool.iota(slots_init[0], pattern=[[0, NTOK // P // 2], [P, 2], [0, E0]], base=NTOK,
                      channel_multiplier=1).then_inc(s["tables_made"], 1)
            pool.iota(slots_init[1], pattern=[[0, E1]], base=NTOK, channel_multiplier=1
                      ).then_inc(s["tables_made"], 1)
            pool.iota(idx_of[:, 0, :], pattern=[[P, 2]], base=NTOK, channel_multiplier=1)
            pool.memset(zeros, 0.0).then_inc(s["tables_made"], 1)
            pool.memset(half[:, :], -0.5).then_inc(s["half_made"], 1)
            pool.wait_ge(s["half_made"], 1)
            for sem in (at[0]["tok_scattered"], at[1]["tok_scattered"], *added0):
                pool.dma_start(spare, half[0:1, 0:1]).then_inc(sem, 16)
                pool.wait_ge(sem, 16)
            pool.wait_ge(s["table_filled"], 160)

            def rows(l):
                z = at[l]
                with pool.Fori(0, B) as b:
                    for norm in range(2):
                        if norm:
                            wait_apart(pool, z["tok_scattered"], b * (16 * TOP[l] * TT) + 16)
                        pool.wait_ge(z["var_ready"], b * 2 + norm + 1)
                        pool.tensor_tensor(rstd[:, :], var[:, :], half[:, :], ALU.pow).then_inc(z["rstd_ready"], 1)
                    wait_apart(pool, z["slots_ready"], b + 1)
                    for t in range(TT):
                        for k in range(TOP[l]):
                            pool.indirect_dma_start(
                                out=slot_token[l], out_offset=bass.IndirectOffsetOnAxis(
                                    ap=slots[:, t, k:k + 1].bitcast(U32), axis=0),
                                in_=tok_i[:, t:t + 1], in_offset=None,
                                bounds_check=CAP * E1 - 1 if l else NTOK * E0 - 1,
                                oob_is_err=False).then_inc(z["tok_scattered"], 16)
                pool.wait_ge(z["tok_scattered"], (B * TOP[l] * TT + 1) * 16)

            def copied(u, k, dst, src):
                pool.tensor_copy(dst, src).then_inc(s["idx0_step"], 1)
                wait_apart(pool, s["idx0_step"], u * 6 + k + 1)

            def gather0(u, j, column):
                wait_apart(pool, s["xgT0_ps"], u * 2 + j + 1)
                wait_apart(pool, s["wcol0_ready"], u * 2 + j + 1)
                copied(u, 2 * j, idx_of[:, 1, j:j + 1], idx_of[:, 0, j:j + 1])
                copied(u, 2 * j + 1, idx_of[:, 0, j:j + 1], column)
                pool.indirect_dma_start(
                    out=xg0[:, j, :], out_offset=None, in_=xw_table[0],
                    in_offset=bass.IndirectOffsetOnAxis(ap=idx_of[:, 0, j:j + 1].bitcast(U32), axis=0),
                    bounds_check=NTOK + DUMMIES - 1, oob_is_err=True).then_inc(xg0_in[j], 16)

            def add0(u):
                for j in range(2):
                    wait_apart(pool, added0[j], u * 16 + 16)
                for j in range(2):
                    copied(u, 4 + j, idx_of[:, 2, j:j + 1], idx_of[:, 1, j:j + 1])
                    wait_apart(pool, s["out0_ready"], u * 2 + j + 1)
                    pool.indirect_dma_start(
                        out=row_table[0], in_=out0[:, j, :], in_offset=None,
                        out_offset=bass.IndirectOffsetOnAxis(ap=idx_of[:, 2, j:j + 1].bitcast(U32), axis=0),
                        bounds_check=NTOK + DUMMIES - 1, oob_is_err=True,
                        compute_op=ALU.add).then_inc(added0[j], 16)

            rows(0)
            pool.wait_ge(at[0]["row_stored"], B * 32)
            pool.wait_ge(s["idx0_in"], 16)
            wait_apart(pool, s["steps0_ready"], 1)
            for e in range(E0):
                n, before = steps_of_expert(pool, e)
                with pool.Fori(0, n) as i:
                    u = unit_of(pool, before, i)
                    for j in range(2):
                        gather0(u, j, idx_all[:, ds(i * 2 + j, 1), e])
                    add0(u)
            u = pool.snap(n + before)
            gather0(u, 0, idx_all[:, 0:1, 0])
            copied(u, 2, idx_of[:, 1, 1:2], idx_of[:, 0, 1:2])
            pool.sem_inc(s["idx0_step"], 1)
            add0(u)
            for j in range(2):
                wait_apart(pool, added0[j], u * 16 + 32)
            pool.sem_inc(s["experts0_added"], 1)
            rows(1)
            pool.wait_ge(at[1]["row_stored"], B * 32)
            experts_dma(pool)

        @block.tensor
        def _(pe):
            pe.wait_ge(s["consts_made"], 1)
            pe.wait_ge(s["active_made"], 3)
            pe.matmul(mm[0:1, 0:S // P], ones_f[:, 0:1], work[:, 2048:2048 + S // P], start=True, stop=True)
            pe.matmul(mm[0:1, 16:16 + B * NCH], work[0:B * NCH, 2064:2065], ident[0:B * NCH, 0:B * NCH],
                      start=True, stop=True).then_inc(s["active_ps"], 1)
            pe.wait_ge(s["mask_made"], 1)
            for t in range(TT):
                for c in range(S // P):
                    last = pe.matmul(mm[:, 512 + t:513 + t], mask01[:, c, t * P:(t + 1) * P], ones_b[:, 0:1],
                                     start=(c == 0), stop=(c == S // P - 1))
            last.then_inc(s["row_ps"], 1)
            pe.wait_ge(s["weights_in"], N_WEIGHTS * 16)
            pe.wait_ge(s["info_made"], 1)

            def tokens_to_columns(b, l, norm):
                pe.wait_ge(at[l]["xn_ready"], b * 2 + norm + 1)
                for k in range(KD):
                    for t in range(TT):
                        last = pe.transpose(m_xT[:, k, t * P:(t + 1) * P], xw[:, t, k * P:(k + 1) * P], ident)
                last.then_inc(at[l]["xnT_ps"], 1)
                pe.wait_ge(at[l]["xnT_ready"], b * 2 + norm + 1)

            def attention(b, l):
                z = at[l]
                n, first, before = units(pe, b, l)
                with pe.Fori(0, n) as i:
                    u = unit_of(pe, before, i)
                    pe.wait_ge(z["ctx_in"], (u + 1) * (32 if l else 16))
                    for m in range(KD):
                        for k in range(KD):
                            last = pe.matmul(y_k[:, m, :], wk[l][:, k, m * P:(m + 1) * P], ctxc[:, k, :],
                                             start=(k == 0), stop=(k == KD - 1))
                    last.then_inc(z["kv_ps"], 1)
                    for t in range(KT):
                        if l:
                            pe.matmul(y_v[:, t, :], ones_f[0:1, :], bvo[:, 0, :], start=True, stop=False)
                        for k in range(KD):
                            last = pe.matmul(y_v[:, t, :], ctxc[:, k, t * P:(t + 1) * P], wv[l][:, k, :],
                                             start=(k == 0 and not l), stop=(k == KD - 1))
                    last.then_inc(z["kv_ps"], 1)
                    pe.wait_ge(z["v_kept"], u + 1)
                    pe.wait_ge(z["k_split"], u + 1)
                tokens_to_columns(b, l, 0)
                for m in range(KD):
                    for k in range(KD):
                        last = pe.matmul(y_q[:, m, :], wq[l][:, k, m * P:(m + 1) * P], xnT[:, k, :],
                                         start=(k == 0), stop=(k == KD - 1))
                last.then_inc(z["q_ps"], 1)
                wait_apart(pe, z["q_stacked"], (b + 1) * 96)
                with pe.Fori(0, n) as i:
                    u = unit_of(pe, before, i)
                    chunk = chunk_of(pe, first, i)
                    rows = ROW_MAX if l else ROW_NEG
                    pe.wait_ge(z["k_stacked"], (u + 1) * 16 * K_DMAS)
                    for h in range(H):
                        pe.wait_ge(z["a_read"], u * H + (h + 1))
                        for t in range(TT):
                            last = pe.matmul(sc_a[h % 2][:, t, :], q_stack[0:rows, h, t * P:(t + 1) * P],
                                             k_stack[0:rows, h, ds(i * CH, CH)], start=True, stop=bool(l))
                            if not l:
                                for c in range(KT):
                                    last = pe.matmul(sc_a[h % 2][:, t, c * P:(c + 1) * P],
                                                     mask0[:, ds(chunk * KT + c, 1), t * P:(t + 1) * P
                                                           ].rearrange("p c t -> p (c t)"),
                                                     ident_b[:, :], start=False, stop=(c == KT - 1))
                        last.then_inc(z["a_scores"], 1)
                wait_apart(pe, z["max_split"], b + 1)
                for t in range(TT):
                    last = pe.transpose(m_mT[:, t * P:(t + 1) * P], msp[:, t, :, :].rearrange("p a h -> p (a h)"),
                                        ident_b[:, :])
                last.then_inc(z["mT_ps"], 1)
                wait_apart(pe, z["max_rows"], (b + 1) * 48)

                def values(u, g):
                    pe.wait_ge(z["exp_done"], u * H + 4 * (g + 1))
                    pe.wait_ge(z["ot_added"], u * G + (g + 1))
                    for k in range(KT):
                        for j in range(4):
                            last = pe.matmul(m_pv[g % 2][32 * j:32 * j + 32, :], v_now[:, k, 4 * g + j, :],
                                             probs[:, 4 * (g % 2) + j, k, :], start=(k == 0),
                                             stop=(k == KT - 1), tile_position=(0, 32 * j))
                    last.then_inc(z["pv_done"], 1)

                with pe.Fori(0, n) as i:
                    u = unit_of(pe, before, i)
                    chunk = chunk_of(pe, first, i)
                    pe.wait_ge(z["v_placed"], u + 1)
                    for h in range(H):
                        pe.wait_ge(z["exp_done"], u * H + (h + 1) - 2) if h >= 2 else None
                        for c in range(KT):
                            last = pe.matmul(sc_b[h % 2][:, c, :], k_stack[0:ROW_END, h, ds(i * CH + c * P, P)],
                                             q_stack[0:ROW_END, h, :], start=True, stop=bool(l))
                            if not l:
                                last = pe.matmul(sc_b[h % 2][:, c, :], ident_b[:, :],
                                                 mask0[:, ds(chunk * KT + c, 1), :
                                                       ].rearrange("p c t -> p (c t)"), start=False, stop=True)
                        last.then_inc(z["b_scores"], 1)
                        if h >= 5 and h % 4 == 1:
                            values(u, h // 4 - 1)
                    values(u, G - 1)
                pe.wait_ge(z["ot_added"], (before + n) * G + 2)
                for t in range(TT):
                    for g in range(G):
                        last = pe.transpose(sc[:, t // 2, (t % 2) * 512 + g * P:(t % 2) * 512 + (g + 1) * P],
                                            ot[:, g, t * P:(t + 1) * P], ident)
                    last.then_inc(z["oT_ps"], 1)
                for t in range(TT):
                    pe.wait_ge(z["on_ready"], b * TT + t + 1)
                    for k in range(KD):
                        last = pe.transpose(m_onT[:, t, k, :], on[:, t * D + k * P:t * D + (k + 1) * P], ident)
                    last.then_inc(z["onT_ps"], 1)
                for t in range(TT):
                    if t % 2 == 0:
                        pe.wait_ge(z["onT_kept"], b * 2 + t // 2 + 1)
                    if l:
                        pe.matmul(y_rows[:, t, :], ones_f[0:1, :], bvo[:, 1, :], start=True, stop=False)
                    for k in range(KD):
                        last = pe.matmul(y_rows[:, t, :], onT[:, t, k, :], wo[l][:, k, :],
                                         start=(k == 0 and not l), stop=(k == KD - 1))
                last.then_inc(z["o_ps"], 1)

            def router(b, l):
                tokens_to_columns(b, l, 1)
                for t in range(TT):
                    for k in range(KD):
                        last = pe.matmul(m_logits[l][:, t, :], xnT[:, k, t * P:(t + 1) * P],
                                         (gate0, gate1)[l][:, k, :], start=(k == 0), stop=(k == KD - 1))
                last.then_inc(at[l]["router_ps"], 1)

            def positions(b, l):
                n = E[l]
                pe.wait_ge(at[l]["chosen_ready"], b + 1)
                for t in range(TT):
                    for c in range(t):
                        pe.matmul(m_pos[l][:, t, :], ones_b[:, :], chosen[:, c, 0:n], start=(c == 0), stop=False)
                    pe.matmul(m_pos[l][:, t, :], tri_b[:, :], chosen[:, t, 0:n], start=(t == 0), stop=True)
                for t in range(TT):
                    last = pe.matmul(m_cnt[l], ones_b[:, :], chosen[:, t, 0:n], start=(t == 0), stop=(t == TT - 1))
                last.then_inc(at[l]["pos_ps"], 1)

            def shared(b):
                for j in range(SHK):
                    if j >= 2:
                        pe.wait_ge(s["act_ready"], b * SHK + j - 1)
                    for half_ in range(2):
                        for k in range(KD):
                            m = SHK * half_ + j
                            last = pe.matmul(sc[:, j % 2, half_ * 512:half_ * 512 + 512],
                                             gu_s[:, k, m * P:(m + 1) * P], xnT[:, k, :],
                                             start=(k == 0), stop=(k == KD - 1))
                    last.then_inc(s["pair_ready"], 1)

            def columns0(j, sem_value):
                pe.wait_ge(xg0_in[j], sem_value)
                for k in range(KD):
                    last = pe.transpose(mm[:, 512 * j + k * P:512 * j + (k + 1) * P],
                                        xg0[:, j, k * P:(k + 1) * P], ident)
                last.then_inc(s["xgT0_ps"], 1)

            def gate_up0(u, j, e):
                pe.wait_ge(s["xgT0_kept"], u * 2 + j + 1)
                for half_ in range(2):
                    for m in range(KD):
                        f = half_ * D + m * P
                        for k in range(KD):
                            last = pe.matmul(sc[:, j, half_ * 512 + m * P:half_ * 512 + (m + 1) * P],
                                             gu0[:, e, k, f:f + P], xgT0[:, j, k, :],
                                             start=(k == 0), stop=(k == KD - 1))
                last.then_inc(s["gu0_ps"], 1)

            def down0_(u, j, e):
                pe.wait_ge(s["act0_ready"], u * 2 + j + 1)
                pe.wait_ge(s["out0_ready"], u * 2 + j + 1)
                for k in range(KD):
                    last = pe.matmul(yy[:, 512 * j:512 * j + D], act0[:, j, k, :], down0[:, e, k, :],
                                     start=(k == 0), stop=(k == KD - 1))
                last.then_inc(s["y0_ps"], 1)

            with pe.Fori(0, B) as b:
                attention(b, 0)
                router(b, 0)
                positions(b, 0)
            pe.wait_ge(s["experts_in"], 2 * E0 * 16)
            wait_apart(pe, s["steps0_ready"], 1)
            columns0(0, 16)
            for e in range(E0):
                n, before = steps_of_expert(pe, e)
                with pe.Fori(0, n) as i:
                    u = unit_of(pe, before, i)
                    gate_up0(u, 0, e)
                    columns0(1, u * 16 + 16)
                    gate_up0(u, 1, e)
                    down0_(u, 0, e)
                    columns0(0, u * 16 + 32)
                    down0_(u, 1, e)
            wait_apart(pe, s["shared_in"], 32)
            with pe.Fori(0, B) as b:
                attention(b, 1)
                router(b, 1)
                shared(b)
                positions(b, 1)
                pe.wait_ge(s["act_ready"], (b + 1) * SHK)
                for t in range(TT):
                    for k in range(SHK):
                        last = pe.matmul(y_rows[:, t, :], act1[:, k, t * P:(t + 1) * P], down_s[:, k, :],
                                         start=(k == 0), stop=(k == SHK - 1))
                last.then_inc(s["y_ready"], 1)
            experts_pe(pe)

        @block.scalar
        def _(act):
            act.wait_ge(s["info_made"], 1)

            def columns_kept(b, l, norm):
                act.wait_ge(at[l]["xnT_ps"], b * 2 + norm + 1)
                act.activation(xnT[:, :, :], m_xT, ACT.Copy).then_inc(at[l]["xnT_ready"], 1)

            def attention(b, l):
                z = at[l]
                n, first, before = units(act, b, l)
                with act.Fori(0, n) as i:
                    u = unit_of(act, before, i)
                    act.wait_ge(z["kv_ps"], 2 * u + 2)
                    act.activation(v_all[:, ds(i * KT, KT), :], y_v, ACT.Copy).then_inc(z["v_kept"], 1)
                columns_kept(b, l, 0)
                act.wait_ge(z["mT_ps"], b + 1)
                act.activation(mT[:, :], m_mT, ACT.Copy).then_inc(z["mT_kept"], 1)
                act.wait_ge(z["v_kept"], before + n)
                with act.Fori(0, n) as i:
                    u = unit_of(act, before, i)
                    act.wait_ge(z["pv_done"], u * G + 1)
                    act.activation(v_now[:, :, :, 0:DH], v_all[:, ds(i * KT, KT), :].rearrange(
                        "p k (h d) -> p k h d", d=DH), ACT.Copy).then_inc(z["v_placed"], 1)
                    for h in range(H):
                        act.wait_ge(z["b_scores"], u * H + h + 1)
                        if h % 4 == 0 and h >= 8:
                            act.wait_ge(z["pv_done"], u * G + h // 4)
                        act.activation(probs[:, 4 * (h // 4 % 2) + h % 4, :, :], sc_b[h % 2], ACT.Exp
                                       ).then_inc(z["exp_done"], 1)
                for c in range(2):
                    act.wait_ge(z["onT_ps"], b * TT + 2 * c + 2)
                    act.activation(onT[:, 2 * c:2 * c + 2], m_onT[:, 2 * c:2 * c + 2], ACT.Copy
                                   ).then_inc(z["onT_kept"], 1)

            def kept0(j, value):
                act.wait_ge(s["xgT0_ps"], value)
                act.activation(xgT0[:, j], mm[:, 512 * j:512 * j + D].rearrange("p (k c) -> p k c", k=KD), ACT.Copy
                               ).then_inc(s["xgT0_kept"], 1)

            def gated0(u, j):
                act.wait_ge(s["gu0_ps"], u * 2 + j + 1)
                act.activation(silu0[:, j, :], sc[:, j, 0:D], ACT.Silu).then_inc(s["silu0_ready"], 1)

            with act.Fori(0, B) as b:
                attention(b, 0)
                columns_kept(b, 0, 1)
                act.wait_ge(at[0]["router_sub"], b + 1)
                act.activation(r8[:, 1], r8[:, 0], ACT.Exp).then_inc(at[0]["router_exp"], 1)
            wait_apart(act, s["steps0_ready"], 1)
            kept0(0, 3)
            for e in range(E0):
                n, before = steps_of_expert(act, e)
                with act.Fori(0, n) as i:
                    u = unit_of(act, before, i)
                    gated0(u, 0)
                    kept0(1, u * 2 + 4)
                    gated0(u, 1)
                    kept0(0, u * 2 + 5)
            with act.Fori(0, B) as b:
                attention(b, 1)
                columns_kept(b, 1, 1)
                act.wait_ge(at[1]["router_sub"], b + 1)
                act.activation(small[:, 8], small[:, 7], ACT.Exp, scale=-1.0)
                act.activation(r64[:, 2], r64[:, 1], ACT.Exp).then_inc(at[1]["router_exp"], 1)
                for j in range(SHK):
                    act.wait_ge(s["pair_ready"], b * SHK + j + 1)
                    act.activation(silu[:, j % 2, :], sc[:, j % 2, 0:512], ACT.Silu).then_inc(s["silu_ready"], 1)
            experts_act(act)

        @block.vector
        def _(dve):
            pro = Steps(dve, s["prologue_step"], 0, 64)
            dve.memset(ones_b[:, :], 1.0)
            dve.memset(ones_f[:, :], 1.0)
            dve.memset(carry[:, :, :], 0.0)
            dve.memset(v_now[:, :, :, DH:DH + 1], 1.0)
            dve.memset(v_now[:, :, :, DH + 1:32], 0.0)
            dve.memset(work[:, 6144:6400], 1.0)
            dve.memset(q_stack[ROW_NEG:P, :, :], 1.0)
            dve.wait_ge(s["consts_in"], 16)
            dve.tensor_copy(ident_b[:, :], ident)
            pro.step(dve.memset(small[:, 0], 0.0))
            pro.settle()
            dve.tensor_scalar(key_rows0[ROW_NEG:P, :], work[ROW_NEG:P, 6144:6400], 0.0,
                              consts[ROW_NEG:P, C_NEG + 2:C_NEG + 3], ALU.mult, ALU.add)
            dve.tensor_copy(tri_b[:, :], consts[:, C_TRI:C_TRI + P]).then_inc(s["consts_made"], 1)
            dve.wait_ge(s["masks_in"], 32)
            m_u8 = work[:, 0:1024].bitcast(U8).rearrange("p (c t) -> p c t", c=S // P)
            key_any = work[:, 2048:2048 + S // P]
            dve.tensor_reduce(key_any, m_u8, AX.X, ALU.max).then_inc(s["active_made"], 1)
            pro.step(dve.tensor_scalar(work[0:B * NCH, 1536:1536 + CH],
                                       work[0:B * NCH, 1024:1024 + CH].bitcast(I32), 0.0, None, ALU.not_equal))
            pro.settle()
            dve.tensor_reduce(work[0:B * NCH, 2064:2065], work[0:B * NCH, 1536:1536 + CH], AX.X, ALU.max
                              ).then_inc(s["active_made"], 1)
            dve.tensor_copy(mask01, m_u8).then_inc(s["mask_made"], 1)
            dve.tensor_scalar(mask0[:, :, :], m_u8, -1.0, -MASKED, ALU.add, ALU.mult).then_inc(s["active_made"], 1)
            dve.wait_ge(s["row_ps"], 1)
            dve.wait_ge(s["active_ps"], 1)
            pro.step(dve.tensor_scalar(small[:, 0], mm[:, 512:512 + TT], 1.0, None, ALU.min))
            pro.settle()
            pro.step(dve.reciprocal(small[:, 1], small[:, 0]))
            pro.settle()
            dve.tensor_scalar(nan_bias[:, :], small[:, 1], 0.0, None, ALU.mult)
            seen = work[0:1, 4224:4224 + 2 * B * NCH].rearrange("o (l b c) -> o l b c", l=2, b=B)
            for b in range(B):
                dve.tensor_reduce(seen[:, 0, b, :], mm[0:1, 0:S // P].rearrange("o (c k) -> o c k", k=KT),
                                  AX.X, ALU.max)
            pro.step(dve.tensor_copy(seen[:, 1], mm[0:1, 16:16 + B * NCH].rearrange("o (b c) -> o b c", b=B)))
            pro.settle()
            flat = work[0:1, 4224:4224 + 2 * B * NCH].rearrange("o (n c) -> o n c", c=NCH)
            up = work[0:1, 4352:4352 + 2 * B * NCH].rearrange("o (n c) -> o n c", c=NCH)
            down_ = work[0:1, 4608:4608 + 2 * B * NCH].rearrange("o (n c) -> o n c", c=NCH)
            pro.step(dve.tensor_scalar(flat, flat, 1.0, None, ALU.min))
            pro.settle()
            for c in range(NCH):
                dve.tensor_scalar(up[:, :, c], flat[:, :, c], float(c + 1), None, ALU.mult)
                pro.step(dve.tensor_scalar(down_[:, :, c], flat[:, :, c], float(NCH - c), None, ALU.mult))
            pro.settle()
            NB = 2 * B
            row = lambda k: work[0:1, 5120 + 64 * k:5120 + 64 * k + NB]
            dve.tensor_reduce(row(0), up, AX.X, ALU.max)
            pro.step(dve.tensor_reduce(row(1), down_, AX.X, ALU.max))
            pro.settle()
            pro.step(dve.tensor_scalar(row(2), row(0), 0.0, float(NCH), ALU.is_equal, ALU.mult))
            pro.settle()
            dve.tensor_tensor(row(3), row(0), row(2), ALU.add)
            pro.step(dve.tensor_tensor(row(4), row(1), row(2), ALU.add))
            pro.settle()
            pro.step(dve.tensor_scalar(row(5), row(4), -1.0, float(NCH), ALU.mult, ALU.add))
            pro.settle()
            dve.memset(work[0:1, 6144:6144 + B], 1.0)
            pro.step(dve.tensor_tensor(row(6), row(3), row(5), ALU.subtract))
            pro.settle()
            for l in range(2):
                pro.step(dve.tensor_tensor_scan(row(7)[:, l * B:(l + 1) * B], work[0:1, 6144:6144 + B],
                                                row(6)[:, l * B:(l + 1) * B], 0.0, ALU.mult, ALU.add))
            pro.settle()
            pro.step(dve.tensor_tensor(row(8), row(7), row(6), ALU.subtract))
            pro.settle()
            for k, r in enumerate((6, 5, 8)):
                last = dve.tensor_copy(info[:, :, k, :], row(r).rearrange("o (l b) -> o l b", l=2))
            last.then_inc(s["info_made"], 1)
            for z in at:
                dve.sem_inc(z["a_read"], 2)
                dve.sem_inc(z["ot_added"], 2)
                dve.sem_inc(z["pv_done"], 1)
            dve.sem_inc(s["ew_used"], EU)
            for sem in ("xgT0_ps", "wcol0_ready", "out0_ready"):
                dve.sem_inc(s[sem], 2)
            dve.wait_ge(s["info_made"], 1)
            dve.wait_ge(s["weights_in"], N_WEIGHTS * 16)

            def layer_norm(b, l, norm, st):
                z = at[l]
                if norm == 0:
                    dve.wait_ge(z["x_loaded"], (b + 1) * 16)
                for t in range(TT):
                    st.step(dve.bn_stats(stats[:, t, :], x[:, t, :]))
                st.settle(s["waits_passed"])
                for t in range(TT):
                    st.step(dve.bn_aggr(mv[:, t, :], stats[:, t, :]))
                st.settle()
                dve.tensor_scalar(var[:, :], mv[:, :, 1], LN_EPS, None, ALU.add).then_inc(z["var_ready"], 1)
                dve.wait_ge(z["rstd_ready"], b * 2 + norm + 1)
                for t in range(TT):
                    last = dve.tensor_scalar(xw[:, t, 0:D], x[:, t, :], mv[:, t, 0:1], rstd[:, t:t + 1],
                                             ALU.subtract, ALU.mult)
                last.then_inc(z["xn_ready"], 1)

            def split(st, f, r, parts, done):
                st.settle()
                st.step(dve.tensor_copy(parts[:, 0], f))
                st.settle()
                st.step(dve.tensor_tensor(r, f, parts[:, 0], ALU.subtract))
                st.settle()
                st.step(dve.tensor_copy(parts[:, 1], r))
                st.settle()
                dve.tensor_tensor(parts[:, 2], r, parts[:, 1], ALU.subtract).then_inc(done, 1)

            def attention(b, l, st):
                z = at[l]
                n, first, before = units(dve, b, l)
                with dve.Fori(0, n) as i:
                    u = unit_of(dve, before, i)
                    kv = Steps(dve, z["kv_step"], u * 16, 16)
                    if l:
                        dve.wait_ge(z["ctx_in"], (u + 1) * 32)
                        kv.step(dve.tensor_scalar(keym, keym_i, 0.0, None, ALU.not_equal))
                        kv.settle()
                        kv.step(dve.tensor_scalar(key_rows[1][ROW_NEG:P, :], keym[ROW_NEG:P, :],
                                                  consts[ROW_NEG:P, C_NEG:C_NEG + 1],
                                                  consts[ROW_NEG:P, C_NEG + 1:C_NEG + 2], ALU.mult, ALU.add))
                    dve.wait_ge(z["kv_ps"], 2 * u + 2)
                    if l:
                        for m in range(KD):
                            kv.step(dve.scalar_tensor_tensor(
                                out=kf[:, m, :], in0=y_k[:, m, :], scalar=bqk[:, 1, m:m + 1], in1=keym,
                                op0=ALU.add, op1=ALU.mult))
                    else:
                        kv.step(dve.tensor_copy(kf, y_k))
                    split(kv, kf, kr, ksp, z["k_split"])
                    kv.fill()
                layer_norm(b, l, 0, st)
                dve.wait_ge(z["q_ps"], b + 1)
                for m in range(KD):
                    if l:
                        st.step(dve.tensor_scalar(qf[:, m, :], y_q[:, m, :], bqk[:, 0, m:m + 1], DH ** -0.5,
                                                  ALU.add, ALU.mult))
                    else:
                        st.step(dve.tensor_scalar(qf[:, m, :], y_q[:, m, :], DH ** -0.5, None, ALU.mult))
                split(st, qf, qr, qsp, z["q_split"])
                st.step(dve.memset(mx[:, :, :], LOWEST))
                st.settle(s["waits_passed"])
                with dve.Fori(0, n) as i:
                    u = unit_of(dve, before, i)
                    for h in range(H):
                        dve.wait_ge(z["a_scores"], u * H + h + 1)
                        dve.tensor_reduce(mxu[:, :, h], sc_a[h % 2], AX.X, ALU.max).then_inc(z["a_read"], 1)
                    dve.wait_ge(z["a_read"], u * H + H + 2)
                    dve.tensor_tensor(mx[:, :, :], mx[:, :, :], mxu[:, :, :], ALU.max).then_inc(z["a_step"], 1)
                    dve.wait_ge(z["a_step"], u + 1)
                mx2, mr2 = mx[:, :, :], mres[:, :, :]
                st.step(dve.tensor_scalar(mx2, mx2, -1.0, None, ALU.mult))
                st.settle()
                st.step(dve.tensor_copy(msp[:, :, 0, :], mx2))
                st.settle()
                st.step(dve.tensor_tensor(mr2, mx2, msp[:, :, 0, :], ALU.subtract))
                st.settle()
                st.step(dve.tensor_copy(msp[:, :, 1, :], mr2))
                st.settle()
                dve.tensor_tensor(msp[:, :, 2, :], mr2, msp[:, :, 1, :], ALU.subtract).then_inc(z["max_split"], 1)
                st.step(dve.memset(ot[:, :, :], 0.0))
                st.settle(s["waits_passed"])
                with dve.Fori(0, n) as i:
                    u = unit_of(dve, before, i)
                    for g in range(G):
                        dve.wait_ge(z["pv_done"], u * G + g + 2)
                        dve.tensor_tensor(ot[:, g, :], m_pv[g % 2], ot[:, g, :], ALU.add).then_inc(z["ot_added"], 1)
                    dve.wait_ge(z["ot_added"], u * G + G + 2)
                for t in range(TT):
                    heads = slice(t * H, (t + 1) * H)
                    dve.wait_ge(z["oT_ps"], b * TT + t + 1)
                    st.step(dve.reciprocal(rden[:, heads], sc_oT[:, heads, DH]))
                    st.settle()
                    dve.tensor_tensor(on[:, t * D:(t + 1) * D].rearrange("p (h d) -> p h d", d=DH),
                                      sc_oT[:, heads, 0:DH], rden[:, heads].unsqueeze(2).to_broadcast((P, H, DH)),
                                      ALU.mult).then_inc(z["on_ready"], 1)
                dve.wait_ge(z["o_ps"], b + 1)
                for t in range(TT):
                    if l == 0:
                        last = dve.scalar_tensor_tensor(out=x[:, t, :], in0=y_rows[:, t, :],
                                                        scalar=nan_bias[:, t:t + 1], in1=x[:, t, :],
                                                        op0=ALU.add, op1=ALU.add)
                    else:
                        last = dve.tensor_tensor(x[:, t, :], y_rows[:, t, :], x[:, t, :], ALU.add)
                last.then_inc(z["o_added"], 1)
                dve.wait_ge(z["o_added"], b + 1)

            def router0(b, st):
                lg, p_, m8 = m_logits[0], r8[:, 2], r8[:, 5]
                oh, oh2, hot = r8[:, 3], r8[:, 4], r64[:, 4, :, 0:E0]
                dve.wait_ge(at[0]["router_ps"], b + 1)
                st.step(dve.tensor_reduce(small[:, 0], lg, AX.X, ALU.max))
                st.settle()
                for t in range(TT):
                    last = dve.tensor_scalar(r8[:, 0, t, :], lg[:, t, :], small[:, 0, t:t + 1], None, ALU.subtract)
                last.then_inc(at[0]["router_sub"], 1)
                dve.wait_ge(at[0]["router_exp"], b + 1)
                st.step(dve.tensor_reduce(small[:, 1], r8[:, 1], AX.X, ALU.add))
                st.settle()
                st.step(dve.reciprocal(small[:, 2], small[:, 1]))
                st.settle()
                for t in range(TT):
                    st.step(dve.tensor_scalar(p_[:, t, :], r8[:, 1, t, :], small[:, 2, t:t + 1], None, ALU.mult))
                st.settle(s["waits_passed"])
                for t in range(TT):
                    st.step(dve.max(m8[:, t, :], p_[:, t, :]))
                st.settle(s["waits_passed"])
                for t in range(TT):
                    st.step(dve.max_index(ix[:, t, :], m8[:, t, :], p_[:, t, :]))
                st.step(dve.tensor_tensor(small[:, 3], m8[:, :, 0], m8[:, :, 1], ALU.add))
                st.settle()
                st.step(dve.tensor_copy(r8[:, 0], ix[:, :, :]))
                st.step(dve.tensor_scalar(small[:, 4], small[:, 3], ROUTE_EPS, None, ALU.add))
                st.settle()
                st.step(dve.reciprocal(small[:, 5], small[:, 4]))
                for t in range(TT):
                    st.step(dve.tensor_scalar(oh[:, t, :], consts[:, C_I8:C_I8 + 8], r8[:, 0, t, 0:1], None,
                                              ALU.is_equal))
                st.settle()
                for t in range(TT):
                    st.step(dve.scalar_tensor_tensor(
                        out=hot[:, t, :], in0=consts[:, C_I8:C_I8 + 8], scalar=r8[:, 0, t, 1:2],
                        in1=oh[:, t, :], op0=ALU.is_equal, op1=ALU.add))
                st.settle()
                dve.tensor_copy(chosen[:, :, 0:E0], hot).then_inc(at[0]["chosen_ready"], 1)
                st.step(dve.tensor_tensor(oh, hot, p_, ALU.mult))
                st.settle()
                for t in range(TT):
                    st.step(dve.tensor_scalar(oh2[:, t, :], oh[:, t, :], small[:, 5, t:t + 1], None, ALU.mult))
                st.settle()
                st.step(dve.tensor_reduce(small[:, 1], oh2, AX.X, ALU.add))
                st.settle()
                st.step(dve.tensor_scalar(small[:, 2], small[:, 1], ROUTE_EPS, None, ALU.add))
                st.settle()
                st.step(dve.reciprocal(small[:, 3], small[:, 2]))
                st.settle()
                for t in range(TT):
                    st.step(dve.tensor_scalar(xw[:, t, D:D + E0], oh2[:, t, :], small[:, 3, t:t + 1], None,
                                              ALU.mult))

            def router1(b, st):
                lg, sub, ex, mk = r64[:, 0], r64[:, 1], r64[:, 2], r64[:, 3]
                m8 = r8[:, 5]
                dve.wait_ge(at[1]["router_ps"], b + 1)
                st.step(dve.tensor_copy(lg, m_logits[1][:, :, 0:E1]))
                st.step(dve.tensor_copy(small[:, 7], m_logits[1][:, :, E1]))
                st.settle(s["waits_passed"])
                for t in range(TT):
                    st.step(dve.max(m8[:, t, :], lg[:, t, :]))
                st.settle()
                for t in range(TT):
                    last = dve.tensor_scalar(sub[:, t, :], lg[:, t, :], m8[:, t, 0:1], None, ALU.subtract)
                last.then_inc(at[1]["router_sub"], 1)
                for t in range(TT):
                    st.step(dve.match_replace(mk[:, t, :], m8[:, t, :], lg[:, t, :], LOWEST))
                st.settle()
                st.step(dve.tensor_tensor(r64[:, 4], mk, lg, ALU.not_equal))
                st.settle()
                dve.tensor_copy(chosen[:, :, :], r64[:, 4]).then_inc(at[1]["chosen_ready"], 1)
                dve.wait_ge(at[1]["router_exp"], b + 1)
                st.step(dve.tensor_tensor(sub, ex, r64[:, 4], ALU.mult))
                st.step(dve.tensor_scalar(small[:, 9], small[:, 8], 1.0, None, ALU.add))
                st.settle()
                st.step(dve.tensor_reduce(small[:, 1], sub, AX.X, ALU.add))
                st.step(dve.reciprocal(small[:, 10], small[:, 9]))
                st.settle()
                st.step(dve.reciprocal(small[:, 2], small[:, 1]))
                st.settle()
                for t in range(TT):
                    st.step(dve.tensor_scalar(xw[:, t, D:XW], sub[:, t, :], small[:, 2, t:t + 1], None, ALU.mult))
                st.settle()

            def dispatch(b, l, st):
                n = E[l]
                numbers = consts[:, C_E1:C_E1 + n]
                pos, ok, picked, val, hot = (r64[:, k, :, 0:n] for k in range(5))
                d8, far = r8[:, 0], r8[:, 1]
                dve.wait_ge(at[l]["pos_ps"], b + 1)
                for t in range(TT):
                    st.step(dve.tensor_tensor(pos[:, t, :], m_pos[l][:, t, :], carry[:, l, 0:n], ALU.add))
                st.settle()
                st.step(dve.tensor_tensor(carry[:, l, 0:n], m_cnt[l], carry[:, l, 0:n], ALU.add))
                st.step(dve.scalar_tensor_tensor(out=ok, in0=pos, scalar=float(CAP if l else NTOK), in1=hot,
                                                 op0=ALU.is_lt, op1=ALU.mult))
                for t in range(TT):
                    st.step(dve.scalar_tensor_tensor(out=val[:, t, :], in0=pos[:, t, :], scalar=float(n),
                                                     in1=numbers, op0=ALU.mult, op1=ALU.add))
                st.settle()
                st.step(dve.tensor_tensor(picked, val, ok, ALU.mult))
                st.settle(s["waits_passed"])
                for t in range(TT):
                    st.step(dve.max(d8[:, t, :], picked[:, t, :]))
                st.settle()
                st.step(dve.tensor_scalar(far, d8, 0.0, FAR, ALU.is_equal, ALU.mult))
                st.settle()
                st.step(dve.scalar_tensor_tensor(out=slots[:, :, :], in0=d8, scalar=-1.0, in1=far,
                                                 op0=ALU.add, op1=ALU.add))
                st.step(dve.tensor_copy(tok_i[:, :], tok_f[:, :]))
                st.settle()
                dve.tensor_scalar(tok_f[:, :], tok_f[:, :], float(T), None, ALU.add).then_inc(at[l]["slots_ready"], 1)

            def shared(b):
                for j in range(SHK):
                    dve.wait_ge(s["silu_ready"], b * SHK + j + 1)
                    dve.tensor_tensor(act1[:, j, :], sc[:, j % 2, 512:1024], silu[:, j % 2, :], ALU.mult
                                      ).then_inc(s["act_ready"], 1)

            def count_steps():
                cnt, ones, upto, total = (counted[:, k, :] for k in range(4))
                pro.step(dve.memset(ones, 1.0))
                pro.step(dve.tensor_copy(cnt, carry[0:1, 0, 0:E0]))
                pro.step(dve.memset(total, 1.0))
                pro.settle()
                for j in range(1, NTOK // P // 2):
                    pro.step(dve.scalar_tensor_tensor(out=total, in0=cnt, scalar=float(2 * P * j), in1=total,
                                                      op0=ALU.is_gt, op1=ALU.add))
                    pro.settle()
                pro.step(dve.tensor_tensor_scan(upto, ones, total, 0.0, ALU.mult, ALU.add))
                pro.settle()
                pro.step(dve.tensor_tensor(upto, upto, total, ALU.subtract))
                pro.settle()
                pro.step(dve.tensor_copy(steps0[:, 0, :], total))
                pro.step(dve.tensor_copy(steps0[:, 1, :], upto))
                pro.step(dve.memset(out0[:, :, :], 0.0))
                pro.settle()
                dve.sem_inc(s["steps0_ready"], 1)

            def weights0(j, value, weighed):
                dve.wait_ge(xg0_in[j], value)
                dve.wait_ge(s["out0_ready"], weighed)
                dve.tensor_copy(wcol0[:, j, :], xg0[:, j, D:D + E0]).then_inc(s["wcol0_ready"], 1)

            def gated0(u, j):
                dve.wait_ge(s["silu0_ready"], u * 2 + j + 1)
                dve.tensor_tensor(act0[:, j].rearrange("p k c -> p (k c)"), sc[:, j, 512:512 + D], silu0[:, j, :],
                                  ALU.mult).then_inc(s["act0_ready"], 1)

            def weigh0(u, j, e):
                dve.wait_ge(s["y0_ps"], u * 2 + j + 1)
                dve.wait_ge(s["wcol0_ready"], u * 2 + j + 3)
                dve.wait_ge(added0[j], u * 16 + 32)
                dve.tensor_scalar(out0[:, j, :], yy[:, 512 * j:512 * j + D], wcol0[:, j, e:e + 1], None, ALU.mult
                                  ).then_inc(s["out0_ready"], 1)

            for l in range(2):
                z = at[l]
                pro.step(dve.tensor_copy(tok_f[:, :], consts[:, C_TOK:C_TOK + TT]))
                pro.settle()
                with dve.Fori(0, B) as b:
                    st = Steps(dve, z["dve_step"], b * 256, 256)
                    attention(b, l, st)
                    layer_norm(b, l, 1, st)
                    if l == 0:
                        router0(b, st)
                        dispatch(b, 0, st)
                    else:
                        router1(b, st)
                        shared(b)
                        dispatch(b, 1, st)
                        dve.wait_ge(s["y_ready"], b + 1)
                        for t in range(TT):
                            last = dve.scalar_tensor_tensor(out=x[:, t, :], in0=y_rows[:, t, :],
                                                            scalar=small[:, 10, t:t + 1], in1=x[:, t, :],
                                                            op0=ALU.mult, op1=ALU.add)
                        last.then_inc(s["y_added"], 1)
                    st.fill()
                if l == 0:
                    count_steps()
                    weights0(0, 16, 1)
                    for e in range(E0):
                        n, before = steps_of_expert(dve, e)
                        with dve.Fori(0, n) as i:
                            u = unit_of(dve, before, i)
                            gated0(u, 0)
                            weights0(1, u * 16 + 16, u * 2 + 2)
                            gated0(u, 1)
                            weigh0(u, 0, e)
                            weights0(0, u * 16 + 32, u * 2 + 3)
                            weigh0(u, 1, e)
            experts_dve(dve)


def constants():
    import numpy as np
    c = np.zeros((P, C_END), np.float32)
    i = np.arange(P)
    c[:, C_ID:C_ID + P] = i[:, None] == i[None, :]
    c[:, C_TRI:C_TRI + P] = i[:, None] < i[None, :]
    c[:, C_E1:C_E1 + 64] = np.arange(1, 65)
    c[:, C_I8:C_I8 + 8] = np.arange(8)
    rest = -1e9
    for part in range(3):
        v = float((np.float32(rest).view(np.uint32) & np.uint32(0xffff0000)).view(np.float32))
        rest -= v
        c[ROW_NEG + part, C_NEG], c[ROW_NEG + part, C_NEG + 1] = -v, v
        c[ROW_MAX + part, C_NEG + 1] = 1.0
        c[ROW_MAX + part, C_NEG + 2] = 1.0
    c[:, C_TOK:C_TOK + 4] = i[:, None] + P * np.arange(4)[None, :]
    return c


def kernel(**inputs):
    import concourse.bacc as bacc
    import numpy as np
    from concourse.bass_utils import run_bass_kernel_spmd

    g = {k: np.asarray(v) for k, v in inputs.items()}
    B, T, D = g["x"].shape
    arrays = {
        "consts": constants(),
        "x": g["x"],
        "ctxT": g["ctx_1024"].transpose(0, 2, 1),
        "mask0T": np.ascontiguousarray(g["mask_SxS2_bk0"].T).view(np.uint32),
        "mask1": g["mask_Bx1x1xS2_ik0"].reshape(B, -1),
        "wq0": g["L0_xattn_wq"].T, "wk0": g["L0_xattn_wk"].T,
        "wv0": g["L0_xattn_wv"].T, "wo0": g["L0_xattn_wo"].T,
        "wq1": g["L1_xattn_Wq"], "wk1": g["L1_xattn_Wk"], "wv1": g["L1_xattn_Wv"], "wo1": g["L1_xattn_Wo"],
        "bqk": np.stack([g["L1_xattn_bq"], g["L1_xattn_bk"]]).reshape(2, D // P, P).transpose(2, 0, 1), "bv": g["L1_xattn_bv"], "bo": g["L1_xattn_bo"],
        "gate0": g["L0_ffn_gate_w"].T, "gu0": g["L0_ffn_gate_up_proj"], "down0": g["L0_ffn_down_proj"],
        "gate1": np.concatenate([g["L1_ffn_gate_w"], g["L1_ffn_shared_gate_w"]], axis=1),
        "gu_s": g["L1_ffn_shared_gate_up_w"], "down_s": g["L1_ffn_shared_down_w"],
        "egu": g["L1_ffn_expert_gate_up_w"], "edown": g["L1_ffn_expert_down_w"],
    }
    arrays = {k: np.ascontiguousarray(v) for k, v in arrays.items()}
    nc = bacc.Bacc("TRN2", target_bir_lowering=False, num_devices=1)
    ap = {k: nc.dram_tensor("in_" + k, v.shape, mybir.dt.from_np(v.dtype), kind="ExternalInput").ap()
          for k, v in arrays.items()}
    for w in ("wq", "wk", "wv", "wo"):
        ap[w] = [ap[w + "0"], ap[w + "1"]]
    out = nc.dram_tensor("out", (B * T, D), F32, kind="ExternalOutput").ap()
    build(nc, ap, out)
    r = run_bass_kernel_spmd(nc, [{"in_" + k: v for k, v in arrays.items()}], core_ids=[0])
    return r.results[0]["out"].reshape(B, T, D)
```

```python
from contextlib import ExitStack

import concourse.bass as bass
from concourse import mybir

F32 = mybir.dt.float32
BF16 = mybir.dt.bfloat16
I32 = mybir.dt.int32
U32 = mybir.dt.uint32
U8 = mybir.dt.uint8
ALU = mybir.AluOpType
ACT = mybir.ActivationFunctionType
AX = mybir.AxisListType
ds = bass.ds

P = 128
PARTS = (0, 0, 1, 1, 0, 2), (0, 1, 0, 1, 2, 0)
ROW_NEG, ROW_MAX, ROW_END = 96, 99, 102
LOWEST = -3.0e38
MASKED = -1.0e30
LN_EPS, ROUTE_EPS = 1e-5, 1e-9
FAR = 1048576.0

C_ID, C_TRI, C_E1, C_I8, C_UP, C_DOWN, C_NEG, C_TOK, C_END = (
    0, 128, 256, 320, 328, 332, 336, 339, 343)


class Steps:

    def __init__(self, engine, sem, base, stride):
        self.engine, self.sem, self.base, self.stride, self.n = engine, sem, base, stride, 0

    def step(self, instruction):
        instruction.then_inc(self.sem, 1)
        self.n += 1

    def settle(self, apart=None):
        self.engine.wait_ge(self.sem, self.base + self.n)
        if apart is not None:
            self.engine.sem_inc(apart, 1)

    def fill(self):
        assert 0 < self.n < self.stride
        self.settle()
        self.engine.sem_inc(self.sem, self.stride - self.n)


def build(nc, a, out):
    B, T, D = a["x"].shape
    S = a["ctxT"].shape[2]
    H = 16
    DH = D // H
    KD = D // P
    TT = T // P
    CH = 256
    NCH = S // CH
    KT = CH // P
    G = H // 4
    E0, E1 = 8, 64
    CAP = 128
    E = (E0, E1)
    TOP = (2, 8)
    WIDTH = (D + E0, D + E1)
    XW = D + E1
    DUMMIES = 2 * P
    NTOK = B * T
    SHK = 4
    EU = 8
    N_WEIGHTS = 2 * 4 + 2 + 2
    K_DMAS = 6 + 1

    with ExitStack() as ctx:
        def sb(name, shape, dt=F32):
            return ctx.enter_context(nc.sbuf_tensor(name, shape, dt))

        def ps(name, shape, dt=F32):
            return ctx.enter_context(nc.psum_tensor(name, shape, dt))

        def sems(text, suffix=""):
            return {n: ctx.enter_context(nc.semaphore(n + suffix)) for n in text.split()}

        q_scratch = nc.dram_tensor("q_scratch", (3, D, T), BF16).ap()
        k_scratch = nc.dram_tensor("k_scratch", (3, D, S), BF16).ap()
        xw_table = [nc.dram_tensor(f"xw_table_{l}", (NTOK + DUMMIES, WIDTH[l]), F32).ap() for l in range(2)]
        slot_token = [nc.dram_tensor(f"slot_token_{l}", (n, 1), I32).ap() for l, n in enumerate((NTOK * E0, CAP * E1))]
        row_table = [nc.dram_tensor("row_table", (NTOK + DUMMIES, D), F32).ap(), out]
        spare = nc.dram_tensor("spare", (1, 1), F32).ap()

        consts = sb("consts", [P, C_END])
        ident = consts[:, C_ID:C_ID + P]
        ident_b = sb("ident_b", [P, P], BF16)
        tri_b = sb("tri_b", [P, P], BF16)
        ones_b = sb("ones_b", [P, P], BF16)
        ones_f = sb("ones_f", [P, P])
        wq = [sb(f"wq{l}", [P, KD, D]) for l in range(2)]
        wk = [sb(f"wk{l}", [P, KD, D]) for l in range(2)]
        wv = [sb(f"wv{l}", [P, KD, D]) for l in range(2)]
        wo = [sb(f"wo{l}", [P, KD, D]) for l in range(2)]
        bqkv = sb("bqkv", [P, 3, KD])
        bo_row = sb("bo_row", [1, D])
        bias_o = sb("bias_o", [P, D])
        gate0 = sb("gate0", [P, KD, E0])
        gate1 = sb("gate1", [P, KD, E1 + 1])
        fore = sb("fore", [P, 12288])
        gu0 = fore[:, 0:8192].rearrange("p (e k f) -> p e k f", e=E0, k=KD)
        down0 = fore[:, 8192:12288].rearrange("p (e k n) -> p e k n", e=E0, k=KD)
        x_front = fore[:, 0:1024].rearrange("p (t n) -> p t n", t=TT)
        xn_front = fore[:, 1024:2048].rearrange("p (t n) -> p t n", t=TT)
        xnT_front = fore[:, 2048:3072].rearrange("p (k t) -> p k t", k=KD)
        part_f = [fore[:, 3072:4096].rearrange("p (m t) -> p m t", m=KD),
                  sb("part_f1", [P, KD, T])[:, :, :]]
        part_r = fore[:, 4096:5120].rearrange("p (m t) -> p m t", m=KD)
        parts = fore[:, 5120:6656].bitcast(BF16).rearrange("p (a m t) -> p a m t", a=3, m=KD)
        ctx_cols = fore[:, 6656:8704].rearrange("p (k t) -> p k t", k=KD)
        keym_i = fore[:, 8704:9728].bitcast(I32)
        keym = fore[:, 9728:10752]
        key_rows = fore[:, 10752:11264].bitcast(BF16)
        down_s = fore[:, 11264:12288].rearrange("p (k n) -> p k n", k=SHK)
        mask0 = sb("mask0", [P, S // P, T], BF16)
        gu_s = mask0[:, :, :].rearrange("p c t -> p (c t)").bitcast(F32).rearrange("p (k f) -> p k f", k=KD)
        bq_scaled = sb("bq_scaled", [P, KD])
        nan_bias = sb("nan_bias", [P, TT])
        steps0 = sb("steps0", [1, 2, E0], I32)
        counted = sb("counted", [1, 4, E0])
        idx_all = sb("idx_all", [P, NTOK // P, E0], I32)
        idx_of = sb("idx_of", [P, 3, 2], I32)
        wcol0 = sb("wcol0", [P, 2, E0])
        info = sb("info", [1, 3, 2 * B], I32)

        x = sb("x_row", [P, TT, D])
        xw = sb("xw_row", [P, TT, XW])
        xnT = sb("xnT", [P, KD, T])
        q_stack = sb("q_stack", [P, H, T], BF16)
        k_stack = sb("k_stack", [P, H, S], BF16)
        v_all = sb("v_all", [P, S // P, D])
        v_now = sb("v_now", [P, KT, H, 32])
        ot = sb("ot", [P, G, T])
        work = sb("work", [P, 8192])
        mv_front = sb("mv_front", [P, TT, 2])
        var_front = sb("var_front", [P, TT])
        rstd_front = sb("rstd_front", [P, TT])
        stats = sb("stats", [P, TT, 6])
        mv = sb("mv", [P, TT, 2])
        var = sb("var", [P, TT])
        half = sb("half", [P, TT])
        rstd = sb("rstd", [P, TT])
        mx = sb("mx", [P, TT, H])
        mxu = sb("mxu", [P, TT, H])
        mres = sb("mres", [P, TT, H])
        msp = sb("msp", [P, TT, 3, H], BF16)
        rden = sb("rden", [P, TT * H])
        mT = sb("mT", [3 * H, T], BF16)
        small = sb("small", [P, 16, TT])
        r8 = sb("r8", [P, 6, TT, 8])
        ix = sb("ix", [P, TT, 8], U32)
        r64 = sb("r64", [P, 5, TT, E1])
        chosen = sb("chosen", [P, TT, E1], BF16)
        carry = sb("carry", [P, 2, E1])
        slots = sb("slots", [P, TT, 8], I32)
        tok_f = sb("tok_f", [P, TT])
        tok_i = sb("tok_i", [P, TT], I32)

        probs = work[:, :].rearrange("p (s k t) -> p s k t", s=8, k=KT)
        on = work[:, 0:1024]
        onT = work[:, 1024:2048].rearrange("p (t k c) -> p t k c", t=TT, k=KD)
        silu = work[:, 2048:3072].rearrange("p (s t) -> p s t", s=2)
        act1 = work[:, 3072:5120].rearrange("p (k t) -> p k t", k=SHK)
        xg0 = work[:, 0:2 * (D + E0)].rearrange("p (s n) -> p s n", s=2)
        xgT0 = work[:, 1024:1536].rearrange("p (s k c) -> p s k c", s=2, k=KD)
        silu0 = work[:, 1536:2048].rearrange("p (s n) -> p s n", s=2)
        act0 = work[:, 2048:2560].rearrange("p (s k c) -> p s k c", s=2, k=KD)
        out0 = work[:, 2560:3072].rearrange("p (s n) -> p s n", s=2)
        mask01 = work[:, 2112:4160].bitcast(BF16).rearrange("p (c t) -> p c t", c=S // P)
        slots_init = [work[:, 6912:7168].bitcast(I32), work[:, 6528:6592].bitcast(I32)]
        zeros = work[:, 6592:6592 + XW]
        xg = work[:, 0:EU * XW].rearrange("p (s n) -> p s n", s=EU)
        xgT = work[:, 2560:3072].rearrange("p (s k c) -> p s k c", s=2, k=KD)
        esilu = work[:, 3072:3328].rearrange("p (s c) -> p s c", s=2)
        eact = work[:, 3328:3584].rearrange("p (s c) -> p s c", s=2)
        eout = work[:, 3584:4096].rearrange("p (s n) -> p s n", s=2)
        ecol = work[:, 4096:4104]
        tok_of = work[:, 4160:4224].bitcast(I32)
        tok_now = work[:, 4224:4232].bitcast(I32)
        tok_add = work[:, 4232:4234].bitcast(I32)
        ew = gu0.rearrange("p e k f -> p e (k f)")
        ew_gu = [ew[:, j, 0:KD * 2 * P].rearrange("p (k f) -> p k f", k=KD) for j in range(EU)]
        ew_down = [ew[:, j, KD * 2 * P:KD * 2 * P + D] for j in range(EU)]
        sc = ps("sc", [P, 2, 1024])
        yy = ps("yy", [P, 1024])
        mm = ps("mm", [P, 1024])
        sc_a = [sc[:, s, :].rearrange("p (t k) -> p t k", t=TT) for s in range(2)]
        sc_b = [sc[:, s, :].rearrange("p (k t) -> p k t", k=KT) for s in range(2)]
        y_rows = yy[:, :].rearrange("p (t n) -> p t n", t=TT)
        sc_q = sc[:, 0, :].rearrange("p (m t) -> p m t", m=KD)
        sc_v = sc[:, 1, :].rearrange("p (t n) -> p t n", t=TT)
        y_cols = yy[:, :].rearrange("p (m t) -> p m t", m=KD)
        m_xT = mm[:, :].rearrange("p (k t) -> p k t", k=KD)
        m_onT = mm[:, :].rearrange("p (t k c) -> p t k c", t=TT, k=KD)
        sc_oT = sc[:, :, :].rearrange("p s n -> p (s n)").rearrange("p (m c) -> p m c", c=32)
        m_pv = [mm[:, 512 * s:512 * s + 512] for s in range(2)]
        m_mT = mm[0:3 * H, 0:T // 2].bitcast(BF16)
        m_logits = [mm[:, 0:TT * n].rearrange("p (t e) -> p t e", t=TT) for n in (E0, E1 + 1)]
        m_cnt = [mm[:, 512 + TT * n:512 + (TT + 1) * n] for n in E]
        m_pos = [mm[:, 512:512 + TT * n].rearrange("p (t e) -> p t e", t=TT) for n in E]

        s = sems("""consts_in weights_in bv_spread bias_ps bias_made tables_made half_made waits_passed consts_made
            masks_in active_made active_ps mask_made row_ps info_made table_filled prologue_step
            pair_ready silu_ready act_ready y_ready y_added shared_in
            steps0_ready idx0_in idx0_step xgT0_ps xgT0_kept gu0_ps silu0_ready act0_ready y0_ps
            wcol0_ready out0_ready experts0_added
            tokens_in idx1_step ew_used xgT_ps xgT_kept egu_ps esilu_ready eact_ready
            ey_ps ecol_ready ey_ready ey_added""")
        xg0_in = [ctx.enter_context(nc.semaphore(f"xg0_in_{j}")) for j in range(2)]
        added0 = [ctx.enter_context(nc.semaphore(f"added0_{j}")) for j in range(2)]
        xg_in = [ctx.enter_context(nc.semaphore(f"xg_in_{j}")) for j in range(EU)]
        ew_in = [ctx.enter_context(nc.semaphore(f"ew_in_{j}")) for j in range(EU)]
        common = sems("""x_loaded var_ready rstd_ready xn_ready xnT_ps xnT_ready
            router_ps router_sub router_exp chosen_ready pos_ps slots_ready row_stored
            front_loaded front_var front_rstd front_xn front_ps front_kept key_mask ctx_in key_in
            unit_ps unit_kept unit_step unit_split unit_spilled v_ps v_kept k_stacked dve_step
            q_stacked a_scores a_read a_step max_split mT_ps mT_kept max_rows v_placed b_scores
            exp_done pv_done ot_added oT_ps on_ready onT_ps onT_kept o_ps o_added""")
        at = [dict(common, **sems("tok_scattered", f"_{l}")) for l in range(2)]

        def units(engine, b):
            n = engine.value_load(info[0:1, 0, ds(b, 1)], min_val=1, max_val=NCH)
            first = engine.value_load(info[0:1, 1, ds(b, 1)], min_val=0, max_val=NCH - 1)
            before = engine.value_load(info[0:1, 2, ds(b, 1)], min_val=0, max_val=2 * NCH * B)
            return n, first, before

        def wait_apart(engine, sem, value):
            engine.wait_ge(sem, value)
            engine.sem_inc(s["waits_passed"], 1)

        def chunk_of(engine, first, i):
            return nc.s_assert_within(engine.snap(first + i), 0, NCH - 1, skip_runtime_bounds_check_because="first + how many <= NCH")

        def unit(f, k):
            return f * 3 + k + 1

        def by_rows(front, row):
            def of(engine, l):
                front(l * B, l == 0)
                with engine.Fori(l * B, (l + 1) * B - 1) as b:
                    row(b, b + 1)
                row((l + 1) * B - 1, None)
            return of

        def in_layer(engine, b, l):
            return b - l * B if l == 0 or isinstance(b, int) else engine.snap(b - l * B)

        def unit_of(engine, before, i):
            return engine.snap(before + i)

        def steps_of_expert(engine, e):
            n = engine.value_load(steps0[0:1, 0, e:e + 1], min_val=1, max_val=NTOK // P // 2)
            before = engine.value_load(steps0[0:1, 1, e:e + 1], min_val=0, max_val=E0 * NTOK // P // 2)
            return n, before

        def steps_of(b, e):
            return b * EU + e + 1

        def experts_load(sp):
            sp.dma_start(tok_of, slot_token[1].rearrange("(p e) o -> p (e o)", p=P)).then_inc(s["tokens_in"], 16)
            with sp.Fori(0, E1 // EU) as r:
                for j in range(EU):
                    sp.wait_ge(s["ew_used"], steps_of(r, j))
                    sp.dma_start(ew_gu[j], a["egu"][ds(r * EU + j, 1), :, :].rearrange("e (k p) f -> p (e k) f", p=P)
                                 ).then_inc(ew_in[j], 16)
                    sp.dma_start(ew_down[j], a["edown"][ds(r * EU + j, 1), :, :].rearrange("e p n -> p (e n)")
                                 ).then_inc(ew_in[j], 16)
            sp.wait_ge(s["ey_added"], E1 * 16 + 32)

        def experts_dma(pool):
            def copied(steps, dst, column):
                pool.tensor_copy(dst, column).then_inc(s["idx1_step"], 1)
                wait_apart(pool, s["idx1_step"], steps)

            def gather(j):
                pool.indirect_dma_start(
                    out=xg[:, j, :], out_offset=None, in_=xw_table[1],
                    in_offset=bass.IndirectOffsetOnAxis(ap=tok_now[:, j:j + 1].bitcast(U32), axis=0),
                    bounds_check=NTOK + DUMMIES - 1, oob_is_err=True).then_inc(xg_in[j], 16)

            def add_and_gather(r, gathers):
                for j in range(EU):
                    copied(r * 2 * EU + (EU + (2 if gathers else 1) * j + 1), tok_add[:, j % 2:j % 2 + 1], tok_of[:, ds(r * EU + j, 1)])
                    wait_apart(pool, s["ey_ready"], steps_of(r, j) + EU)
                    wait_apart(pool, s["ey_added"], (r * EU + j) * 16 + 32)
                    pool.indirect_dma_start(
                        out=row_table[1], in_=eout[:, j % 2, :], in_offset=None,
                        out_offset=bass.IndirectOffsetOnAxis(ap=tok_add[:, j % 2:j % 2 + 1].bitcast(U32), axis=0),
                        bounds_check=NTOK + DUMMIES - 1, oob_is_err=True,
                        compute_op=ALU.add).then_inc(s["ey_added"], 16)
                    if gathers:
                        copied(r * 2 * EU + (EU + 2 * j + 2), tok_now[:, j:j + 1], tok_of[:, ds(r * EU + (EU + j), 1)])
                        gather(j)

            pool.wait_ge(s["tokens_in"], 16)
            for j in range(EU):
                copied(j + 1, tok_now[:, j:j + 1], tok_of[:, j:j + 1])
                gather(j)
            with pool.Fori(0, E1 // EU - 1) as r:
                add_and_gather(r, True)
            add_and_gather(E1 // EU - 1, False)

        def experts_pe(pe):
            def columns(r, j):
                pe.wait_ge(xg_in[j], (r + 1) * 16)
                for k in range(KD):
                    last = pe.transpose(mm[:, 512 * (j % 2) + k * P:512 * (j % 2) + (k + 1) * P],
                                        xg[:, j, k * P:(k + 1) * P], ident)
                last.then_inc(s["xgT_ps"], 1)

            def gate_up(r, j):
                pe.wait_ge(s["xgT_kept"], steps_of(r, j))
                pe.wait_ge(ew_in[j], r * 32 + 64)
                for half_ in range(2):
                    for k in range(KD):
                        last = pe.matmul(sc[:, j % 2, 512 * half_:512 * half_ + CAP],
                                         ew_gu[j][:, k, half_ * P:(half_ + 1) * P], xgT[:, j % 2, k, :],
                                         start=(k == 0), stop=(k == KD - 1))
                last.then_inc(s["egu_ps"], 1)

            def down_(r, j):
                pe.wait_ge(s["eact_ready"], steps_of(r, j))
                pe.matmul(yy[:, 512 * (j % 2):512 * (j % 2) + D], eact[:, j % 2, :], ew_down[j],
                          start=True, stop=True).then_inc(s["ey_ps"], 1)

            with pe.Fori(0, E1 // EU) as r:
                for q in range(EU + 2):
                    if q < EU:
                        columns(r, q)
                    if 1 <= q <= EU:
                        gate_up(r, q - 1)
                    if q >= 2:
                        down_(r, q - 2)

        def experts_act(act):
            with act.Fori(0, E1 // EU) as r:
                for q in range(EU + 1):
                    if q < EU:
                        act.wait_ge(s["xgT_ps"], steps_of(r, q))
                        act.activation(xgT[:, q % 2, :, :], mm[:, 512 * (q % 2):512 * (q % 2) + D].rearrange(
                            "p (k c) -> p k c", k=KD), ACT.Copy).then_inc(s["xgT_kept"], 1)
                    if q >= 1:
                        act.wait_ge(s["egu_ps"], steps_of(r, q - 1))
                        act.activation(esilu[:, (q - 1) % 2, :], sc[:, (q - 1) % 2, 0:CAP], ACT.Silu
                                       ).then_inc(s["esilu_ready"], 1)

        def experts_dve(dve):
            with dve.Fori(0, E1 // EU) as r:
                for q in range(EU + 1):
                    if q < EU:
                        dve.wait_ge(s["esilu_ready"], steps_of(r, q))
                        dve.tensor_tensor(eact[:, q % 2, :], sc[:, q % 2, 512:512 + CAP], esilu[:, q % 2, :],
                                          ALU.mult).then_inc(s["eact_ready"], 1)
                        dve.wait_ge(xg_in[q], (r + 1) * 16)
                        wait_apart(dve, s["ey_ready"], steps_of(r, q))
                        dve.tensor_copy(ecol[:, q:q + 1], xg[:, q, ds(r * EU + (D + q), 1)]
                                        ).then_inc(s["ecol_ready"], 1)
                    if q >= 1:
                        j = q - 1
                        dve.wait_ge(s["ey_ps"], steps_of(r, j))
                        dve.wait_ge(s["ecol_ready"], steps_of(r, j))
                        dve.wait_ge(s["ey_added"], (r * EU + j) * 16 + 16)
                        dve.tensor_scalar(eout[:, j % 2, :], yy[:, 512 * (j % 2):512 * (j % 2) + D],
                                          ecol[:, j:j + 1], None, ALU.mult).then_inc(s["ey_ready"], 1)
                        dve.sem_inc(s["ew_used"], 1)

        block = ctx.enter_context(nc.Block())

        @block.sync
        def _(sp):
            def load(dst, src, sem=s["weights_in"]):
                sp.dma_start(dst, src).then_inc(sem, 16)

            load(consts[:, :], a["consts"], s["consts_in"])
            load(work[:, 0:1024].bitcast(U32).rearrange("p (c t) -> p c t", c=S // P),
                 a["mask0T"].rearrange("(c p) t -> p c t", p=P), s["masks_in"])
            load(work[0:B * NCH, 1024:1024 + CH].bitcast(I32), a["mask1"].rearrange("b (c k) -> (b c) k", k=CH), s["masks_in"])
            for l in range(2):
                load(wk[l][:, :, :], a["wk"][l].rearrange("(k p) n -> p k n", p=P))
                load(wv[l][:, :, :], a["wv"][l].rearrange("(k p) n -> p k n", p=P))
                load(wq[l][:, :, :], a["wq"][l].rearrange("(k p) n -> p k n", p=P))
                if l == 0:
                    load(bqkv[:, :, :], a["bqkv"])
                    load(bo_row[:, :], a["bo"].rearrange("(o n) -> o n", o=1))
                load(wo[l][:, :, :], a["wo"][l].rearrange("(k p) n -> p k n", p=P))
            load(gate0[:, :, :], a["gate0"].rearrange("(k p) n -> p k n", p=P))
            load(gate1[:, :, :], a["gate1"].rearrange("(k p) n -> p k n", p=P))
            sp.wait_ge(s["tables_made"], 3)
            load(slot_token[0].rearrange("(j p e) o -> p j (e o)", p=P, e=E0),
                 slots_init[0].rearrange("p (j e) -> p j e", e=E0), s["table_filled"])
            load(slot_token[1].rearrange("(p e) o -> p (e o)", p=P), slots_init[1], s["table_filled"])
            for l in range(2):
                for d in range(DUMMIES // P):
                    load(xw_table[l][NTOK + d * P:NTOK + (d + 1) * P, :], zeros[:, 0:WIDTH[l]], s["table_filled"])
                    load(row_table[l][NTOK + d * P:NTOK + (d + 1) * P, :], zeros[:, 0:D], s["table_filled"])
            sp.wait_ge(s["table_filled"], 160)
            sp.wait_ge(s["info_made"], 1)

            def rows(l):
                z = at[l]
                source = (a["x"].rearrange("b t n -> (b t) n"), row_table[0])[l]

                def loads(f, first_one):
                    if not first_one:
                        wait_apart(sp, z["front_xn"], f)
                    f_ = in_layer(sp, f, l)
                    sp.dma_start(x_front, source[ds(f_ * T, T), :].rearrange("(t p) n -> p t n", p=P)
                                 ).then_inc(z["front_loaded"], 16)
                    if not first_one:
                        wait_apart(sp, z["v_ps"], f * 2)
                        wait_apart(sp, z["unit_split"], f * 3)
                    sp.dma_start(ctx_cols, a["ctxT"][ds(f_, 1), :, :].rearrange("b (k p) t -> p (b k) t", p=P)
                                 ).then_inc(z["ctx_in"], 16)
                    if l:
                        sp.dma_start(keym_i, a["mask1"][ds(f_, 1), :].partition_broadcast(P)
                                     ).then_inc(z["key_in"], 16)

                def spill_keys(f, first_one):
                    if not first_one:
                        wait_apart(sp, z["k_stacked"], f * 16 * K_DMAS)
                    for half_ in range(2):
                        sp.wait_ge(z["unit_split"], unit(f, half_))
                        sp.dma_start(k_scratch[:, :, half_ * T:(half_ + 1) * T].rearrange("a (m p) t -> p a m t", p=P),
                                     parts).then_inc(z["unit_spilled"], 16)

                def stack(f, first_one):
                    wait_apart(sp, z["unit_spilled"], unit(f, 1) * 16)
                    for g, part in enumerate(PARTS[1]):
                        sp.dma_start(k_stack[DH * g:DH * (g + 1), :, :],
                                     k_scratch[part].rearrange("(h d) t -> d h t", d=DH)
                                     ).then_inc(z["k_stacked"], 16)
                    sp.wait_ge(z["key_mask"], f + 1) if l else None
                    sp.dma_start(k_stack[ROW_NEG:ROW_END, :, :],
                                 key_rows[ROW_NEG:ROW_END, :].unsqueeze(1).to_broadcast(
                                     (ROW_END - ROW_NEG, H, S))).then_inc(z["k_stacked"], 16)
                    if not first_one:
                        wait_apart(sp, z["q_stacked"], f * 96)
                    sp.wait_ge(z["unit_split"], unit(f, 2))
                    sp.dma_start(q_scratch.rearrange("a (m p) t -> p a m t", p=P), parts
                                 ).then_inc(z["unit_spilled"], 16)
                    sp.wait_ge(z["unit_spilled"], unit(f, 2) * 16)
                    for g, part in enumerate(PARTS[0]):
                        sp.dma_start(q_stack[DH * g:DH * (g + 1), :, :],
                                     q_scratch[part].rearrange("(h d) t -> d h t", d=DH)
                                     ).then_inc(z["q_stacked"], 16)

                def front(f, first_one):
                    loads(f, first_one)
                    spill_keys(f, first_one)
                    stack(f, first_one)

                def row(b, f):
                    b_ = in_layer(sp, b, l)
                    sp.dma_start(x[:, :, :], source[ds(b_ * T, T), :].rearrange("(t p) n -> p t n", p=P)
                                 ).then_inc(z["x_loaded"], 16)
                    if f is not None:
                        loads(f, False)
                    sp.wait_ge(z["mT_kept"], b + 1)
                    for part in range(3):
                        sp.dma_start(q_stack[ROW_MAX + part:ROW_MAX + part + 1, :, :],
                                     mT[part * H:(part + 1) * H, :]).then_inc(z["max_rows"], 16)
                    if f is not None:
                        spill_keys(f, False)
                        wait_apart(sp, z["oT_ps"], (b + 1) * TT)
                        stack(f, False)
                    wait_apart(sp, z["slots_ready"], b + 1)
                    sp.dma_start(xw_table[l][ds(b_ * T, T), :].rearrange("(t p) n -> p t n", p=P),
                                 xw[:, :, 0:WIDTH[l]]).then_inc(z["row_stored"], 16)
                    if l:
                        wait_apart(sp, s["y_added"], b + 2)
                    sp.dma_start(row_table[l][ds(b_ * T, T), :].rearrange("(t p) n -> p t n", p=P), x[:, :, :]
                                 ).then_inc(z["row_stored"], 16)
                    wait_apart(sp, z["row_stored"], (b + 1) * 32)

                by_rows(front, row)(sp, l)

            rows(0)
            sp.wait_ge(at[0]["tok_scattered"], (B * TOP[0] * TT + 1) * 16)
            sp.dma_start(idx_all[:, :, :], slot_token[0].rearrange("(j p e) o -> p j (e o)", p=P, e=E0)
                         ).then_inc(s["idx0_in"], 16)
            for e in range(E0):
                sp.dma_start(gu0[:, e, :, :], a["gu0"][e].rearrange("(k p) n -> p k n", p=P)).then_inc(ew_in[e], 16)
                sp.dma_start(down0[:, e, :, :], a["down0"][e].rearrange("(k p) n -> p k n", p=P)).then_inc(ew_in[e], 16)
            sp.wait_ge(s["experts0_added"], 1)
            sp.dma_start(gu_s, a["gu_s"].rearrange("(k p) n -> p k n", p=P)).then_inc(s["shared_in"], 16)
            sp.dma_start(down_s, a["down_s"].rearrange("(k p) n -> p k n", p=P)).then_inc(s["shared_in"], 16)
            rows(1)
            sp.wait_ge(at[1]["tok_scattered"], (B * TOP[1] * TT + 1) * 16)
            experts_load(sp)

        @block.gpsimd
        def _(pool):
            pool.iota(slots_init[0], pattern=[[0, NTOK // P // 2], [P, 2], [0, E0]], base=NTOK,
                      channel_multiplier=1).then_inc(s["tables_made"], 1)
            pool.iota(slots_init[1], pattern=[[0, E1]], base=NTOK, channel_multiplier=1
                      ).then_inc(s["tables_made"], 1)
            pool.iota(idx_of[:, 0, :], pattern=[[P, 2]], base=NTOK, channel_multiplier=1)
            pool.memset(zeros, 0.0).then_inc(s["tables_made"], 1)
            pool.memset(half[:, :], -0.5).then_inc(s["half_made"], 1)
            pool.wait_ge(s["half_made"], 1)
            for k, sem in enumerate((at[0]["tok_scattered"], at[1]["tok_scattered"], *added0, *2 * [s["ey_added"]])):
                pool.dma_start(spare, half[0:1, 0:1]).then_inc(sem, 16)
                pool.wait_ge(sem, 32 if k == 5 else 16)
            pool.wait_ge(s["table_filled"], 160)

            def rows(l):
                z = at[l]

                def front_norm(f):
                    pool.wait_ge(z["front_var"], f + 1)
                    pool.tensor_tensor(rstd_front[:, :], var_front[:, :], half[:, :], ALU.pow
                                       ).then_inc(z["front_rstd"], 1)

                def split_keys(f, k, first_one):
                    st = Steps(pool, z["unit_step"], (f * 2 + k) * 8, 8)
                    p_f = part_f[k]
                    pool.wait_ge(z["unit_kept"], unit(f, k))
                    if not first_one or k:
                        wait_apart(pool, z["unit_spilled"], (f * 3 + k) * 16)
                    if l:
                        pool.wait_ge(z["key_mask"], f + 1)
                        st.step(pool.tensor_tensor(p_f, p_f, keym[:, k * T:(k + 1) * T].unsqueeze(1)
                                                   .to_broadcast((P, KD, T)), ALU.mult))
                        st.settle(s["waits_passed"])
                    st.step(pool.tensor_copy(parts[:, 0], p_f))
                    st.settle()
                    st.step(pool.tensor_tensor(part_r, p_f, parts[:, 0], ALU.subtract))
                    st.settle(s["waits_passed"])
                    st.step(pool.tensor_copy(parts[:, 1], part_r))
                    st.fill()
                    pool.tensor_tensor(parts[:, 2], part_r, parts[:, 1], ALU.subtract).then_inc(z["unit_split"], 1)

                def front(f, first_one):
                    front_norm(f)
                    for k in range(2):
                        split_keys(f, k, first_one)

                def row(b, f):
                    if f is not None:
                        front_norm(f)
                        for k in range(2):
                            split_keys(f, k, False)
                    wait_apart(pool, z["tok_scattered"], in_layer(pool, b, l) * (16 * TOP[l] * TT) + 16)
                    pool.wait_ge(z["var_ready"], b + 1)
                    pool.tensor_tensor(rstd[:, :], var[:, :], half[:, :], ALU.pow).then_inc(z["rstd_ready"], 1)
                    wait_apart(pool, z["slots_ready"], b + 1)
                    for t in range(TT):
                        for k in range(TOP[l]):
                            pool.indirect_dma_start(
                                out=slot_token[l], out_offset=bass.IndirectOffsetOnAxis(
                                    ap=slots[:, t, k:k + 1].bitcast(U32), axis=0),
                                in_=tok_i[:, t:t + 1], in_offset=None,
                                bounds_check=CAP * E1 - 1 if l else NTOK * E0 - 1,
                                oob_is_err=False).then_inc(z["tok_scattered"], 16)

                by_rows(front, row)(pool, l)
                pool.wait_ge(z["tok_scattered"], (B * TOP[l] * TT + 1) * 16)

            def copied(u, k, dst, src):
                pool.tensor_copy(dst, src).then_inc(s["idx0_step"], 1)
                wait_apart(pool, s["idx0_step"], u * 6 + k + 1)

            def gather0(u, j, column):
                wait_apart(pool, s["xgT0_ps"], u * 2 + j + 1)
                wait_apart(pool, s["wcol0_ready"], u * 2 + j + 1)
                copied(u, 2 * j, idx_of[:, 1, j:j + 1], idx_of[:, 0, j:j + 1])
                copied(u, 2 * j + 1, idx_of[:, 0, j:j + 1], column)
                pool.indirect_dma_start(
                    out=xg0[:, j, :], out_offset=None, in_=xw_table[0],
                    in_offset=bass.IndirectOffsetOnAxis(ap=idx_of[:, 0, j:j + 1].bitcast(U32), axis=0),
                    bounds_check=NTOK + DUMMIES - 1, oob_is_err=True).then_inc(xg0_in[j], 16)

            def add0(u):
                for j in range(2):
                    wait_apart(pool, added0[j], u * 16 + 16)
                for j in range(2):
                    copied(u, 4 + j, idx_of[:, 2, j:j + 1], idx_of[:, 1, j:j + 1])
                    wait_apart(pool, s["out0_ready"], u * 2 + j + 1)
                    pool.indirect_dma_start(
                        out=row_table[0], in_=out0[:, j, :], in_offset=None,
                        out_offset=bass.IndirectOffsetOnAxis(ap=idx_of[:, 2, j:j + 1].bitcast(U32), axis=0),
                        bounds_check=NTOK + DUMMIES - 1, oob_is_err=True,
                        compute_op=ALU.add).then_inc(added0[j], 16)

            rows(0)
            pool.wait_ge(at[0]["row_stored"], B * 32)
            pool.wait_ge(s["idx0_in"], 16)
            wait_apart(pool, s["steps0_ready"], 1)
            for e in range(E0):
                n, before = steps_of_expert(pool, e)
                with pool.Fori(0, n) as i:
                    u = unit_of(pool, before, i)
                    for j in range(2):
                        gather0(u, j, idx_all[:, ds(i * 2 + j, 1), e])
                    add0(u)
            u = pool.snap(n + before)
            gather0(u, 0, idx_all[:, 0:1, 0])
            copied(u, 2, idx_of[:, 1, 1:2], idx_of[:, 0, 1:2])
            pool.sem_inc(s["idx0_step"], 1)
            add0(u)
            for j in range(2):
                wait_apart(pool, added0[j], u * 16 + 32)
            pool.sem_inc(s["experts0_added"], 1)
            rows(1)
            pool.wait_ge(at[1]["row_stored"], 2 * B * 32)
            experts_dma(pool)

        @block.tensor
        def _(pe):
            pe.wait_ge(s["consts_made"], 1)
            pe.wait_ge(s["active_made"], 3)
            pe.matmul(mm[0:1, 0:S // P], ones_f[:, 0:1], work[:, 2048:2048 + S // P], start=True, stop=True)
            pe.matmul(mm[0:1, 16:16 + B * NCH], work[0:B * NCH, 2064:2065], ident[0:B * NCH, 0:B * NCH],
                      start=True, stop=True).then_inc(s["active_ps"], 1)
            pe.wait_ge(s["mask_made"], 1)
            for t in range(TT):
                for c in range(S // P):
                    last = pe.matmul(mm[:, 512 + t:513 + t], mask01[:, c, t * P:(t + 1) * P], ones_b[:, 0:1],
                                     start=(c == 0), stop=(c == S // P - 1))
            last.then_inc(s["row_ps"], 1)
            pe.wait_ge(s["weights_in"], N_WEIGHTS * 16)
            pe.wait_ge(s["info_made"], 1)
            pe.wait_ge(s["bv_spread"], 1)
            for k in range(KD):
                pe.matmul(yy[:, 0:D], xnT[:, 0, k * P:(k + 1) * P], wo[1][:, k, :], start=(k == 0), stop=False)
            pe.matmul(yy[:, 0:D], ones_f[0:1, :], bo_row[:, :], start=False, stop=True).then_inc(s["bias_ps"], 1)
            pe.wait_ge(s["bias_made"], 1)

            def tokens_to_columns(b, l):
                pe.wait_ge(at[l]["xn_ready"], b + 1)
                for k in range(KD):
                    for t in range(TT):
                        last = pe.transpose(m_xT[:, k, t * P:(t + 1) * P], xw[:, t, k * P:(k + 1) * P], ident)
                last.then_inc(at[l]["xnT_ps"], 1)

            def keys(f, l, half_):
                z = at[l]
                if half_ == 0:
                    pe.wait_ge(z["ctx_in"], (f + 1) * 16)
                else:
                    pe.wait_ge(z["unit_kept"], unit(f, 0))
                for m in range(KD):
                    for k in range(KD):
                        last = pe.matmul(y_cols[:, m, :], wk[l][:, k, m * P:(m + 1) * P],
                                         ctx_cols[:, k, half_ * T:(half_ + 1) * T],
                                         start=(k == 0), stop=(k == KD - 1))
                last.then_inc(z["unit_ps"], 1)

            def front_columns(f, l):
                z = at[l]
                pe.wait_ge(z["unit_kept"], unit(f, 1))
                pe.wait_ge(z["front_xn"], f + 1)
                for k in range(KD):
                    for t in range(TT):
                        last = pe.transpose(y_cols[:, k, t * P:(t + 1) * P], xn_front[:, t, k * P:(k + 1) * P], ident)
                last.then_inc(z["front_ps"], 1)

            def queries(f, l):
                z = at[l]
                pe.wait_ge(z["front_kept"], f + 1)
                for m in range(KD):
                    for k in range(KD):
                        last = pe.matmul(sc_q[:, m, :], wq[l][:, k, m * P:(m + 1) * P], xnT_front[:, k, :],
                                         start=(k == 0), stop=(k == KD - 1))
                last.then_inc(z["unit_ps"], 1)

            def values_of(f, l, half_):
                z = at[l]
                dst = (sc_v, y_rows)[half_]
                for t in range(TT):
                    for k in range(KD):
                        at_ = half_ * T + t * P
                        last = pe.matmul(dst[:, t, :], ctx_cols[:, k, at_:at_ + P], wv[l][:, k, :],
                                         start=(k == 0), stop=(k == KD - 1))
                last.then_inc(z["v_ps"], 1)

            def attention(b, l, f):
                z = at[l]
                n, first, before = units(pe, b)
                wait_apart(pe, z["q_stacked"], (b + 1) * 96)
                wait_apart(pe, z["k_stacked"], (b + 1) * 16 * K_DMAS)
                wait_apart(pe, z["v_kept"], b * 2 + 2)
                with pe.Fori(0, n) as i:
                    u = unit_of(pe, before, i)
                    chunk = chunk_of(pe, first, i)
                    rows = ROW_MAX if l else ROW_NEG
                    for h in range(H):
                        pe.wait_ge(z["a_read"], u * H + (h + 1))
                        for t in range(TT):
                            last = pe.matmul(sc_a[h % 2][:, t, :], q_stack[0:rows, h, t * P:(t + 1) * P],
                                             k_stack[0:rows, h, ds(chunk * CH, CH)], start=True, stop=bool(l))
                            if not l:
                                for c in range(KT):
                                    last = pe.matmul(sc_a[h % 2][:, t, c * P:(c + 1) * P],
                                                     mask0[:, ds(chunk * KT + c, 1), t * P:(t + 1) * P
                                                           ].rearrange("p c t -> p (c t)"),
                                                     ident_b[:, :], start=False, stop=(c == KT - 1))
                        last.then_inc(z["a_scores"], 1)
                if f is not None:
                    if l:
                        pe.wait_ge(s["y_added"], b + 1)
                    keys(f, l, 0)
                wait_apart(pe, z["max_split"], b + 1)
                for t in range(TT):
                    last = pe.transpose(m_mT[:, t * P:(t + 1) * P], msp[:, t, :, :].rearrange("p a h -> p (a h)"),
                                        ident_b[:, :])
                last.then_inc(z["mT_ps"], 1)
                if f is not None:
                    keys(f, l, 1)
                wait_apart(pe, z["max_rows"], (b + 1) * 48)

                def values(u, g, k):
                    if k == 0:
                        pe.wait_ge(z["exp_done"], u * H + 4 * (g + 1))
                        pe.wait_ge(z["ot_added"], u * G + (g + 1))
                        if g == 0:
                            pe.wait_ge(z["v_placed"], u + 1)
                    for j in range(4):
                        last = pe.matmul(m_pv[g % 2][32 * j:32 * j + 32, :], v_now[:, k, 4 * g + j, :],
                                         probs[:, 4 * (g % 2) + j, k, :], start=(k == 0),
                                         stop=(k == KT - 1), tile_position=(0, 32 * j))
                    if k == KT - 1:
                        last.then_inc(z["pv_done"], 1)

                with pe.Fori(0, n) as i:
                    u = unit_of(pe, before, i)
                    chunk = chunk_of(pe, first, i)
                    for h in range(H):
                        pe.wait_ge(z["exp_done"], u * H + (h + 1) - 2) if h >= 2 else None
                        for c in range(KT):
                            last = pe.matmul(sc_b[h % 2][:, c, :], k_stack[0:ROW_END, h, ds(chunk * CH + c * P, P)],
                                             q_stack[0:ROW_END, h, :], start=True, stop=bool(l))
                            if not l:
                                last = pe.matmul(sc_b[h % 2][:, c, :], ident_b[:, :],
                                                 mask0[:, ds(chunk * KT + c, 1), :
                                                       ].rearrange("p c t -> p (c t)"), start=False, stop=True)
                        last.then_inc(z["b_scores"], 1)
                        if h >= 5 and 1 <= h % 4 <= KT:
                            values(u, h // 4 - 1, h % 4 - 1)
                    for k in range(KT):
                        values(u, G - 1, k)
                pe.wait_ge(z["ot_added"], (before + n) * G + 2)
                for t in range(TT):
                    for g in range(G):
                        last = pe.transpose(sc[:, t // 2, (t % 2) * 512 + g * P:(t % 2) * 512 + (g + 1) * P],
                                            ot[:, g, t * P:(t + 1) * P], ident)
                    last.then_inc(z["oT_ps"], 1)
                if f is not None:
                    front_columns(f, l)
                for t in range(TT):
                    pe.wait_ge(z["on_ready"], b * TT + t + 1)
                    for k in range(KD):
                        last = pe.transpose(m_onT[:, t, k, :], on[:, t * D + k * P:t * D + (k + 1) * P], ident)
                    last.then_inc(z["onT_ps"], 1)
                if f is not None:
                    pe.wait_ge(z["front_kept"], f + 1)
                elif l:
                    pe.wait_ge(s["y_added"], b + 1)
                for t in range(TT):
                    if t % 2 == 0:
                        pe.wait_ge(z["onT_kept"], b * 2 + t // 2 + 1)
                    for k in range(KD):
                        last = pe.matmul(y_rows[:, t, :], onT[:, t, k, :], wo[l][:, k, :],
                                         start=(k == 0), stop=(k == KD - 1))
                last.then_inc(z["o_ps"], 1)
                if f is not None:
                    queries(f, l)
                    values_of(f, l, 0)

            def router(b, l, f):
                tokens_to_columns(b, l)
                pe.wait_ge(at[l]["xnT_ready"], b + 1)
                for t in range(TT):
                    for k in range(KD):
                        last = pe.matmul(m_logits[l][:, t, :], xnT[:, k, t * P:(t + 1) * P],
                                         (gate0, gate1)[l][:, k, :], start=(k == 0), stop=(k == KD - 1))
                last.then_inc(at[l]["router_ps"], 1)
                pe.wait_ge(at[l]["o_added"], b + 1)
                if f is not None:
                    values_of(f, l, 1)

            def positions(b, l):
                n = E[l]
                pe.wait_ge(at[l]["chosen_ready"], b + 1)
                for t in range(TT):
                    for c in range(t):
                        pe.matmul(m_pos[l][:, t, :], ones_b[:, :], chosen[:, c, 0:n], start=(c == 0), stop=False)
                    pe.matmul(m_pos[l][:, t, :], tri_b[:, :], chosen[:, t, 0:n], start=(t == 0), stop=True)
                for t in range(TT):
                    last = pe.matmul(m_cnt[l], ones_b[:, :], chosen[:, t, 0:n], start=(t == 0), stop=(t == TT - 1))
                last.then_inc(at[l]["pos_ps"], 1)

            def shared(b, f):
                if f is not None:
                    pe.wait_ge(at[1]["unit_kept"], unit(f, 2))
                    pe.wait_ge(at[1]["v_kept"], f * 2 + 1)
                for j in range(SHK):
                    if j >= 2:
                        pe.wait_ge(s["act_ready"], b * SHK + j - 1)
                    for half_ in range(2):
                        for k in range(KD):
                            m = SHK * half_ + j
                            last = pe.matmul(sc[:, j % 2, half_ * 512:half_ * 512 + 512],
                                             gu_s[:, k, m * P:(m + 1) * P], xnT[:, k, :],
                                             start=(k == 0), stop=(k == KD - 1))
                    last.then_inc(s["pair_ready"], 1)

            def columns0(j, sem_value):
                pe.wait_ge(xg0_in[j], sem_value)
                for k in range(KD):
                    last = pe.transpose(mm[:, 512 * j + k * P:512 * j + (k + 1) * P],
                                        xg0[:, j, k * P:(k + 1) * P], ident)
                last.then_inc(s["xgT0_ps"], 1)

            def gate_up0(u, j, e):
                pe.wait_ge(s["xgT0_kept"], u * 2 + j + 1)
                for half_ in range(2):
                    for m in range(KD):
                        f = half_ * D + m * P
                        for k in range(KD):
                            last = pe.matmul(sc[:, j, half_ * 512 + m * P:half_ * 512 + (m + 1) * P],
                                             gu0[:, e, k, f:f + P], xgT0[:, j, k, :],
                                             start=(k == 0), stop=(k == KD - 1))
                last.then_inc(s["gu0_ps"], 1)

            def down0_(u, j, e):
                pe.wait_ge(s["act0_ready"], u * 2 + j + 1)
                pe.wait_ge(s["out0_ready"], u * 2 + j + 1)
                for k in range(KD):
                    last = pe.matmul(yy[:, 512 * j:512 * j + D], act0[:, j, k, :], down0[:, e, k, :],
                                     start=(k == 0), stop=(k == KD - 1))
                last.then_inc(s["y0_ps"], 1)

            def rows(l):
                def front(f, first_one):
                    keys(f, l, 0)
                    keys(f, l, 1)
                    front_columns(f, l)
                    queries(f, l)
                    values_of(f, l, 0)
                    values_of(f, l, 1)

                def row(b, f):
                    attention(b, l, f)
                    router(b, l, f)
                    positions(b, l)
                    if l:
                        shared(b, f)
                    if l:
                        pe.wait_ge(s["act_ready"], (b + 1) * SHK)
                        if f is not None:
                            pe.wait_ge(at[l]["v_kept"], f * 2 + 2)
                        for t in range(TT):
                            for k in range(SHK):
                                last = pe.matmul(y_rows[:, t, :], act1[:, k, t * P:(t + 1) * P], down_s[:, k, :],
                                                 start=(k == 0), stop=(k == SHK - 1))
                        last.then_inc(s["y_ready"], 1)

                by_rows(front, row)(pe, l)

            rows(0)
            wait_apart(pe, s["steps0_ready"], 1)
            columns0(0, 16)
            for e in range(E0):
                n, before = steps_of_expert(pe, e)
                wait_apart(pe, ew_in[e], 32)
                with pe.Fori(0, n) as i:
                    u = unit_of(pe, before, i)
                    gate_up0(u, 0, e)
                    columns0(1, u * 16 + 16)
                    gate_up0(u, 1, e)
                    down0_(u, 0, e)
                    columns0(0, u * 16 + 32)
                    down0_(u, 1, e)
            wait_apart(pe, s["shared_in"], 32)
            rows(1)
            experts_pe(pe)

        @block.scalar
        def _(act):
            act.wait_ge(s["info_made"], 1)
            act.wait_ge(s["bias_made"], 1)

            def columns_kept(b, l):
                act.wait_ge(at[l]["xnT_ps"], b + 1)
                act.activation(xnT[:, :, :], m_xT, ACT.Copy).then_inc(at[l]["xnT_ready"], 1)

            def unit_kept(f, l, k, first_one):
                z = at[l]
                act.wait_ge(z["unit_ps"], unit(f, k))
                if not first_one or k:
                    act.wait_ge(z["unit_split"], f * 3 + (0, 0, 1)[k]) if k != 1 else None
                src = sc_q if k == 2 else y_cols
                scale = 1.0 if k < 2 else DH ** -0.5
                if l:
                    for m in range(KD):
                        bias = bqkv[:, 1, m:m + 1] if k < 2 else bq_scaled[:, m:m + 1]
                        last = act.activation(part_f[k % 2][:, m, :], src[:, m, :], ACT.Identity, bias=bias, scale=scale)
                else:
                    last = act.activation(part_f[k % 2], src, ACT.Copy, scale=scale)
                last.then_inc(z["unit_kept"], 1)

            def front_kept(f, l, first_one):
                act.wait_ge(at[l]["front_ps"], f + 1)
                if not first_one:
                    act.wait_ge(at[l]["unit_ps"], f * 3)
                act.activation(xnT_front, y_cols, ACT.Copy).then_inc(at[l]["front_kept"], 1)

            def values_kept(f, l, half_):
                act.wait_ge(at[l]["v_ps"], f * 2 + half_ + 1)
                act.activation(v_all[:, half_ * TT:(half_ + 1) * TT, :], (sc_v, y_rows)[half_], ACT.Copy
                               ).then_inc(at[l]["v_kept"], 1)

            def attention(b, l, f):
                z = at[l]
                n, first, before = units(act, b)
                if f is not None:
                    unit_kept(f, l, 0, False)
                act.wait_ge(z["mT_ps"], b + 1)
                act.activation(mT[:, :], m_mT, ACT.Copy).then_inc(z["mT_kept"], 1)
                if f is not None:
                    unit_kept(f, l, 1, False)
                act.wait_ge(z["v_kept"], b * 2 + 2)
                with act.Fori(0, n) as i:
                    u = unit_of(act, before, i)
                    chunk = chunk_of(act, first, i)
                    act.wait_ge(z["pv_done"], u * G + 1)
                    act.activation(v_now[:, :, :, 0:DH], v_all[:, ds(chunk * KT, KT), :].rearrange(
                        "p k (h d) -> p k h d", d=DH), ACT.Copy).then_inc(z["v_placed"], 1)
                    for h in range(H):
                        act.wait_ge(z["b_scores"], u * H + h + 1)
                        if h % 4 == 0 and h >= 8:
                            act.wait_ge(z["pv_done"], u * G + h // 4)
                        act.activation(probs[:, 4 * (h // 4 % 2) + h % 4, :, :], sc_b[h % 2], ACT.Exp
                                       ).then_inc(z["exp_done"], 1)
                if f is not None:
                    front_kept(f, l, False)
                for c in range(2):
                    act.wait_ge(z["onT_ps"], b * TT + 2 * c + 2)
                    act.activation(onT[:, 2 * c:2 * c + 2], m_onT[:, 2 * c:2 * c + 2], ACT.Copy
                                   ).then_inc(z["onT_kept"], 1)
                if f is not None:
                    unit_kept(f, l, 2, False)
                    act.wait_ge(z["v_placed"], before + n)
                    values_kept(f, l, 0)
                columns_kept(b, l)

            def kept0(j, value):
                act.wait_ge(s["xgT0_ps"], value)
                act.activation(xgT0[:, j], mm[:, 512 * j:512 * j + D].rearrange("p (k c) -> p k c", k=KD), ACT.Copy
                               ).then_inc(s["xgT0_kept"], 1)

            def gated0(u, j):
                act.wait_ge(s["gu0_ps"], u * 2 + j + 1)
                act.activation(silu0[:, j, :], sc[:, j, 0:D], ACT.Silu).then_inc(s["silu0_ready"], 1)

            def rows(l):
                z = at[l]

                def front(f, first_one):
                    for k in range(2):
                        unit_kept(f, l, k, first_one)
                    front_kept(f, l, first_one)
                    unit_kept(f, l, 2, first_one)
                    for half_ in range(2):
                        values_kept(f, l, half_)

                def row(b, f):
                    attention(b, l, f)
                    act.wait_ge(z["router_sub"], b + 1)
                    if l == 0:
                        act.activation(r8[:, 1], r8[:, 0], ACT.Exp).then_inc(z["router_exp"], 1)
                        if f is not None:
                            values_kept(f, l, 1)
                        return
                    act.activation(small[:, 8], small[:, 7], ACT.Exp, scale=-1.0)
                    act.activation(r64[:, 2], r64[:, 1], ACT.Exp).then_inc(z["router_exp"], 1)
                    if f is not None:
                        values_kept(f, l, 1)
                    for j in range(SHK):
                        act.wait_ge(s["pair_ready"], b * SHK + j + 1)
                        act.activation(silu[:, j % 2, :], sc[:, j % 2, 0:512], ACT.Silu).then_inc(s["silu_ready"], 1)

                by_rows(front, row)(act, l)

            rows(0)
            wait_apart(act, s["steps0_ready"], 1)
            kept0(0, 3)
            for e in range(E0):
                n, before = steps_of_expert(act, e)
                with act.Fori(0, n) as i:
                    u = unit_of(act, before, i)
                    gated0(u, 0)
                    kept0(1, u * 2 + 4)
                    gated0(u, 1)
                    kept0(0, u * 2 + 5)
            rows(1)
            experts_act(act)

        @block.vector
        def _(dve):
            pro = Steps(dve, s["prologue_step"], 0, 64)
            dve.memset(ones_b[:, :], 1.0)
            dve.memset(ones_f[:, :], 1.0)
            dve.memset(carry[:, :, :], 0.0)
            dve.memset(v_now[:, :, :, DH:DH + 1], 1.0)
            dve.memset(v_now[:, :, :, DH + 1:32], 0.0)
            dve.memset(work[:, 6144:6400], 1.0)
            dve.memset(q_stack[ROW_NEG:P, :, :], 1.0)
            dve.wait_ge(s["consts_in"], 16)
            dve.tensor_copy(ident_b[:, :], ident)
            pro.step(dve.memset(small[:, 0], 0.0))
            pro.settle()
            for c in range(NCH):
                dve.tensor_scalar(key_rows[ROW_NEG:P, c * CH:(c + 1) * CH], work[ROW_NEG:P, 6144:6400], 0.0,
                                  consts[ROW_NEG:P, C_NEG + 2:C_NEG + 3], ALU.mult, ALU.add)
            dve.tensor_copy(tri_b[:, :], consts[:, C_TRI:C_TRI + P]).then_inc(s["consts_made"], 1)
            dve.wait_ge(s["masks_in"], 32)
            m_u8 = work[:, 0:1024].bitcast(U8).rearrange("p (c t) -> p c t", c=S // P)
            key_any = work[:, 2048:2048 + S // P]
            dve.tensor_reduce(key_any, m_u8, AX.X, ALU.max).then_inc(s["active_made"], 1)
            pro.step(dve.tensor_scalar(work[0:B * NCH, 1536:1536 + CH],
                                       work[0:B * NCH, 1024:1024 + CH].bitcast(I32), 0.0, None, ALU.not_equal))
            pro.settle()
            dve.tensor_reduce(work[0:B * NCH, 2064:2065], work[0:B * NCH, 1536:1536 + CH], AX.X, ALU.max
                              ).then_inc(s["active_made"], 1)
            dve.tensor_copy(mask01, m_u8).then_inc(s["mask_made"], 1)
            dve.tensor_scalar(mask0[:, :, :], m_u8, -1.0, -MASKED, ALU.add, ALU.mult).then_inc(s["active_made"], 1)
            dve.wait_ge(s["row_ps"], 1)
            dve.wait_ge(s["active_ps"], 1)
            pro.step(dve.tensor_scalar(small[:, 0], mm[:, 512:512 + TT], 1.0, None, ALU.min))
            pro.settle()
            pro.step(dve.reciprocal(small[:, 1], small[:, 0]))
            pro.settle()
            dve.tensor_scalar(nan_bias[:, :], small[:, 1], 0.0, None, ALU.mult)
            seen = work[0:1, 4224:4224 + 2 * B * NCH].rearrange("o (l b c) -> o l b c", l=2, b=B)
            for b in range(B):
                dve.tensor_reduce(seen[:, 0, b, :], mm[0:1, 0:S // P].rearrange("o (c k) -> o c k", k=KT),
                                  AX.X, ALU.max)
            pro.step(dve.tensor_copy(seen[:, 1], mm[0:1, 16:16 + B * NCH].rearrange("o (b c) -> o b c", b=B)))
            pro.settle()
            flat = work[0:1, 4224:4224 + 2 * B * NCH].rearrange("o (n c) -> o n c", c=NCH)
            up = work[0:1, 4352:4352 + 2 * B * NCH].rearrange("o (n c) -> o n c", c=NCH)
            down_ = work[0:1, 4608:4608 + 2 * B * NCH].rearrange("o (n c) -> o n c", c=NCH)
            pro.step(dve.tensor_scalar(flat, flat, 1.0, None, ALU.min))
            pro.settle()
            for c in range(NCH):
                dve.tensor_scalar(up[:, :, c], flat[:, :, c], float(c + 1), None, ALU.mult)
                pro.step(dve.tensor_scalar(down_[:, :, c], flat[:, :, c], float(NCH - c), None, ALU.mult))
            pro.settle()
            NB = 2 * B
            row = lambda k: work[0:1, 5120 + 64 * k:5120 + 64 * k + NB]
            dve.tensor_reduce(row(0), up, AX.X, ALU.max)
            pro.step(dve.tensor_reduce(row(1), down_, AX.X, ALU.max))
            pro.settle()
            pro.step(dve.tensor_scalar(row(2), row(0), 0.0, float(NCH), ALU.is_equal, ALU.mult))
            pro.settle()
            dve.tensor_tensor(row(3), row(0), row(2), ALU.add)
            pro.step(dve.tensor_tensor(row(4), row(1), row(2), ALU.add))
            pro.settle()
            pro.step(dve.tensor_scalar(row(5), row(4), -1.0, float(NCH), ALU.mult, ALU.add))
            pro.settle()
            dve.memset(work[0:1, 6144:6144 + 2 * B], 1.0)
            pro.step(dve.tensor_tensor(row(6), row(3), row(5), ALU.subtract))
            pro.settle()
            pro.step(dve.tensor_tensor_scan(row(7), work[0:1, 6144:6144 + NB], row(6), 0.0, ALU.mult, ALU.add))
            pro.settle()
            pro.step(dve.tensor_tensor(row(8), row(7), row(6), ALU.subtract))
            pro.settle()
            for k, r in enumerate((6, 5, 8)):
                last = dve.tensor_copy(info[:, k, :], row(r))
            last.then_inc(s["info_made"], 1)
            dve.sem_inc(common["a_read"], 2)
            dve.sem_inc(common["ot_added"], 2)
            dve.sem_inc(common["pv_done"], 1)
            dve.sem_inc(s["ew_used"], EU)
            dve.sem_inc(s["ey_ready"], EU)
            for sem in ("xgT0_ps", "wcol0_ready", "out0_ready"):
                dve.sem_inc(s[sem], 2)
            dve.sem_inc(s["y_added"], B + 1)
            dve.sem_inc(common["key_mask"], B)
            dve.sem_inc(s["y_ready"], B)
            for sem in ("pair_ready", "silu_ready", "act_ready"):
                dve.sem_inc(s[sem], B * SHK)
            dve.wait_ge(s["info_made"], 1)
            dve.wait_ge(s["weights_in"], N_WEIGHTS * 16)
            dve.tensor_scalar(bq_scaled[:, :], bqkv[:, 0, :], DH ** -0.5, None, ALU.mult)
            for k in range(KD):
                last = dve.tensor_scalar(xnT[:, 0, k * P:(k + 1) * P], ones_f[:, :], bqkv[:, 2, k:k + 1], None, ALU.mult)
            last.then_inc(s["bv_spread"], 1)
            dve.wait_ge(s["bias_ps"], 1)
            dve.tensor_copy(bias_o[:, :], yy[:, 0:D]).then_inc(s["bias_made"], 1)

            def layer_norm(b, l, st, front):
                z = at[l]
                if front:
                    src, dst, mv_, var_, rstd_ = x_front, xn_front, mv_front, var_front, rstd_front
                    dve.wait_ge(z["front_loaded"], (b + 1) * 16)
                else:
                    src, dst, mv_, var_, rstd_ = x, xw, mv, var, rstd
                for t in range(TT):
                    st.step(dve.bn_stats(stats[:, t, :], src[:, t, :]))
                st.settle(s["waits_passed"])
                for t in range(TT):
                    st.step(dve.bn_aggr(mv_[:, t, :], stats[:, t, :]))
                st.settle()
                dve.tensor_scalar(var_[:, :], mv_[:, :, 1], LN_EPS, None, ALU.add
                                  ).then_inc(z["front_var" if front else "var_ready"], 1)
                dve.wait_ge(z["front_rstd" if front else "rstd_ready"], b + 1)
                for t in range(TT):
                    last = dve.tensor_scalar(dst[:, t, 0:D], src[:, t, :], mv_[:, t, 0:1], rstd_[:, t:t + 1],
                                             ALU.subtract, ALU.mult)
                last.then_inc(z["front_xn" if front else "xn_ready"], 1)

            def front(f, l, st, first_one):
                z = at[l]
                if l:
                    if not first_one:
                        dve.wait_ge(z["unit_split"], f * 3)
                        wait_apart(dve, z["k_stacked"], f * 16 * K_DMAS)
                    dve.wait_ge(z["key_in"], (in_layer(dve, f, l) + 1) * 16)
                    st.step(dve.tensor_scalar(keym, keym_i, 0.0, None, ALU.not_equal))
                    st.settle()
                    dve.tensor_scalar(key_rows[ROW_NEG:P, :], keym[ROW_NEG:P, :],
                                      consts[ROW_NEG:P, C_NEG:C_NEG + 1], consts[ROW_NEG:P, C_NEG + 1:C_NEG + 2],
                                      ALU.mult, ALU.add).then_inc(z["key_mask"], 1)
                if not first_one:
                    dve.wait_ge(z["front_ps"], f)
                layer_norm(f, l, st, True)

            def split_queries(f, l, st):
                z = at[l]
                dve.wait_ge(z["unit_kept"], unit(f, 2))
                dve.wait_ge(z["unit_split"], f * 3 + 2)
                wait_apart(dve, z["unit_spilled"], (f * 3 + 2) * 16)
                st.step(dve.tensor_copy(parts[:, 0], part_f[0]))
                st.settle()
                st.step(dve.tensor_tensor(part_r, part_f[0], parts[:, 0], ALU.subtract))
                st.settle()
                st.step(dve.tensor_copy(parts[:, 1], part_r))
                st.settle()
                dve.tensor_tensor(parts[:, 2], part_r, parts[:, 1], ALU.subtract).then_inc(z["unit_split"], 1)

            def attention(b, l, f, st):
                z = at[l]
                n, first, before = units(dve, b)
                st.step(dve.memset(mx[:, :, :], LOWEST))
                st.settle(s["waits_passed"])
                with dve.Fori(0, n) as i:
                    u = unit_of(dve, before, i)
                    for h in range(H):
                        dve.wait_ge(z["a_scores"], u * H + h + 1)
                        dve.tensor_reduce(mxu[:, :, h], sc_a[h % 2], AX.X, ALU.max).then_inc(z["a_read"], 1)
                    dve.wait_ge(z["a_read"], u * H + H + 2)
                    dve.tensor_tensor(mx[:, :, :], mx[:, :, :], mxu[:, :, :], ALU.max).then_inc(z["a_step"], 1)
                    dve.wait_ge(z["a_step"], u + 1)
                mx2, mr2 = mx[:, :, :], mres[:, :, :]
                st.step(dve.tensor_scalar(mx2, mx2, -1.0, None, ALU.mult))
                st.settle()
                st.step(dve.tensor_copy(msp[:, :, 0, :], mx2))
                st.settle()
                st.step(dve.tensor_tensor(mr2, mx2, msp[:, :, 0, :], ALU.subtract))
                st.settle()
                st.step(dve.tensor_copy(msp[:, :, 1, :], mr2))
                st.settle()
                dve.tensor_tensor(msp[:, :, 2, :], mr2, msp[:, :, 1, :], ALU.subtract).then_inc(z["max_split"], 1)
                st.step(dve.memset(ot[:, :, :], 0.0))
                if f is not None:
                    front(f, l, st, False)
                if l:
                    dve.wait_ge(z["x_loaded"], (b + 1) * 16)
                    st.step(dve.tensor_tensor(x[:, :, :], x[:, :, :], bias_o[:, :].unsqueeze(1).to_broadcast(
                        (P, TT, D)), ALU.add))
                st.settle(s["waits_passed"])
                with dve.Fori(0, n) as i:
                    u = unit_of(dve, before, i)
                    for g in range(G):
                        dve.wait_ge(z["pv_done"], u * G + g + 2)
                        dve.tensor_tensor(ot[:, g, :], m_pv[g % 2], ot[:, g, :], ALU.add).then_inc(z["ot_added"], 1)
                    dve.wait_ge(z["ot_added"], u * G + G + 2)
                for t in range(TT):
                    heads = slice(t * H, (t + 1) * H)
                    dve.wait_ge(z["oT_ps"], b * TT + t + 1)
                    st.step(dve.reciprocal(rden[:, heads], sc_oT[:, heads, DH]))
                    st.settle()
                    dve.tensor_tensor(on[:, t * D:(t + 1) * D].rearrange("p (h d) -> p h d", d=DH),
                                      sc_oT[:, heads, 0:DH], rden[:, heads].unsqueeze(2).to_broadcast((P, H, DH)),
                                      ALU.mult).then_inc(z["on_ready"], 1)
                dve.wait_ge(z["o_ps"], b + 1)
                dve.wait_ge(z["x_loaded"], (b + 1) * 16)
                for t in range(TT):
                    if l == 0:
                        last = dve.scalar_tensor_tensor(out=x[:, t, :], in0=y_rows[:, t, :],
                                                        scalar=nan_bias[:, t:t + 1], in1=x[:, t, :],
                                                        op0=ALU.add, op1=ALU.add)
                    else:
                        last = dve.tensor_tensor(x[:, t, :], y_rows[:, t, :], x[:, t, :], ALU.add)
                last.then_inc(z["o_added"], 1)
                dve.wait_ge(z["o_added"], b + 1)

            def over_experts(v, n):
                return v.unsqueeze(2).to_broadcast((P, TT, n))

            def over_tiles(v, n):
                return v.unsqueeze(1).to_broadcast((P, TT, n))

            def router0(b, st):
                lg, p_, m8 = m_logits[0], r8[:, 2], r8[:, 5]
                oh, oh2, hot = r8[:, 3], r8[:, 4], r64[:, 4, :, 0:E0]
                dve.wait_ge(at[0]["router_ps"], b + 1)
                st.step(dve.tensor_reduce(small[:, 0], lg, AX.X, ALU.max))
                st.settle()
                dve.tensor_tensor(r8[:, 0], lg, over_experts(small[:, 0], E0), ALU.subtract).then_inc(at[0]["router_sub"], 1)
                dve.wait_ge(at[0]["router_exp"], b + 1)
                st.step(dve.tensor_reduce(small[:, 1], r8[:, 1], AX.X, ALU.add))
                st.settle()
                st.step(dve.reciprocal(small[:, 2], small[:, 1]))
                st.settle()
                st.step(dve.tensor_tensor(p_, r8[:, 1], over_experts(small[:, 2], E0), ALU.mult))
                st.settle(s["waits_passed"])
                for t in range(TT):
                    st.step(dve.max(m8[:, t, :], p_[:, t, :]))
                st.settle(s["waits_passed"])
                for t in range(TT):
                    st.step(dve.max_index(ix[:, t, :], m8[:, t, :], p_[:, t, :]))
                st.step(dve.tensor_tensor(small[:, 3], m8[:, :, 0], m8[:, :, 1], ALU.add))
                st.settle()
                st.step(dve.tensor_copy(r8[:, 0], ix[:, :, :]))
                st.step(dve.tensor_scalar(small[:, 4], small[:, 3], ROUTE_EPS, None, ALU.add))
                st.settle()
                st.step(dve.reciprocal(small[:, 5], small[:, 4]))
                numbers = over_tiles(consts[:, C_I8:C_I8 + E0], E0)
                st.step(dve.tensor_tensor(oh, numbers, over_experts(r8[:, 0, :, 0], E0), ALU.is_equal))
                st.step(dve.tensor_tensor(oh2, numbers, over_experts(r8[:, 0, :, 1], E0), ALU.is_equal))
                st.settle()
                st.step(dve.tensor_tensor(hot, oh, oh2, ALU.add))
                st.settle()
                dve.tensor_copy(chosen[:, :, 0:E0], hot).then_inc(at[0]["chosen_ready"], 1)
                st.step(dve.tensor_tensor(oh, hot, p_, ALU.mult))
                st.settle()
                st.step(dve.tensor_tensor(oh2, oh, over_experts(small[:, 5], E0), ALU.mult))
                st.settle()
                st.step(dve.tensor_reduce(small[:, 1], oh2, AX.X, ALU.add))
                st.settle()
                st.step(dve.tensor_scalar(small[:, 2], small[:, 1], ROUTE_EPS, None, ALU.add))
                st.settle()
                st.step(dve.reciprocal(small[:, 3], small[:, 2]))
                st.settle()
                st.step(dve.tensor_tensor(xw[:, :, D:D + E0], oh2, over_experts(small[:, 3], E0), ALU.mult))

            def router1(b, st):
                lg, sub, ex, mk = r64[:, 0], r64[:, 1], r64[:, 2], r64[:, 3]
                m8 = r8[:, 5]
                dve.wait_ge(at[1]["router_ps"], b + 1)
                st.step(dve.tensor_copy(lg, m_logits[1][:, :, 0:E1]))
                st.step(dve.tensor_copy(small[:, 7], m_logits[1][:, :, E1]))
                st.settle(s["waits_passed"])
                for t in range(TT):
                    st.step(dve.max(m8[:, t, :], lg[:, t, :]))
                st.settle()
                dve.tensor_tensor(sub, lg, over_experts(m8[:, :, 0], E1), ALU.subtract).then_inc(at[1]["router_sub"], 1)
                for t in range(TT):
                    st.step(dve.match_replace(mk[:, t, :], m8[:, t, :], lg[:, t, :], LOWEST))
                st.settle()
                st.step(dve.tensor_tensor(r64[:, 4], mk, lg, ALU.not_equal))
                st.settle()
                dve.tensor_copy(chosen[:, :, :], r64[:, 4]).then_inc(at[1]["chosen_ready"], 1)
                dve.wait_ge(at[1]["router_exp"], b + 1)
                st.step(dve.tensor_tensor(sub, ex, r64[:, 4], ALU.mult))
                st.step(dve.tensor_scalar(small[:, 9], small[:, 8], 1.0, None, ALU.add))
                st.settle()
                st.step(dve.tensor_reduce(small[:, 1], sub, AX.X, ALU.add))
                st.step(dve.reciprocal(small[:, 10], small[:, 9]))
                st.settle()
                st.step(dve.reciprocal(small[:, 2], small[:, 1]))
                st.settle()
                st.step(dve.tensor_tensor(xw[:, :, D:XW], sub, over_experts(small[:, 2], E1), ALU.mult))
                st.settle()

            def dispatch(b, l, st):
                n = E[l]
                numbers = consts[:, C_E1:C_E1 + n]
                pos, ok, picked, val, hot = (r64[:, k, :, 0:n] for k in range(5))
                d8, far = r8[:, 0], r8[:, 1]
                dve.wait_ge(at[l]["pos_ps"], b + 1)
                st.step(dve.tensor_tensor(pos, m_pos[l], over_tiles(carry[:, l, 0:n], n), ALU.add))
                st.settle()
                st.step(dve.tensor_tensor(carry[:, l, 0:n], m_cnt[l], carry[:, l, 0:n], ALU.add))
                st.step(dve.scalar_tensor_tensor(out=ok, in0=pos, scalar=float(CAP if l else NTOK), in1=hot,
                                                 op0=ALU.is_lt, op1=ALU.mult))
                st.step(dve.scalar_tensor_tensor(out=val, in0=pos, scalar=float(n), in1=over_tiles(numbers, n),
                                                 op0=ALU.mult, op1=ALU.add))
                st.settle()
                st.step(dve.tensor_tensor(picked, val, ok, ALU.mult))
                st.settle(s["waits_passed"])
                for t in range(TT):
                    st.step(dve.max(d8[:, t, :], picked[:, t, :]))
                st.settle()
                st.step(dve.tensor_scalar(far, d8, 0.0, FAR, ALU.is_equal, ALU.mult))
                st.settle()
                st.step(dve.scalar_tensor_tensor(out=slots[:, :, :], in0=d8, scalar=-1.0, in1=far,
                                                 op0=ALU.add, op1=ALU.add))
                st.step(dve.tensor_copy(tok_i[:, :], tok_f[:, :]))
                st.settle()
                dve.tensor_scalar(tok_f[:, :], tok_f[:, :], float(T), None, ALU.add).then_inc(at[l]["slots_ready"], 1)

            def shared(b):
                for j in range(SHK):
                    dve.wait_ge(s["silu_ready"], b * SHK + j + 1)
                    dve.tensor_tensor(act1[:, j, :], sc[:, j % 2, 512:1024], silu[:, j % 2, :], ALU.mult
                                      ).then_inc(s["act_ready"], 1)

            def count_steps():
                cnt, ones, upto, total = (counted[:, k, :] for k in range(4))
                pro.step(dve.memset(ones, 1.0))
                pro.step(dve.tensor_copy(cnt, carry[0:1, 0, 0:E0]))
                pro.step(dve.memset(total, 1.0))
                pro.settle()
                for j in range(1, NTOK // P // 2):
                    pro.step(dve.scalar_tensor_tensor(out=total, in0=cnt, scalar=float(2 * P * j), in1=total,
                                                      op0=ALU.is_gt, op1=ALU.add))
                    pro.settle()
                pro.step(dve.tensor_tensor_scan(upto, ones, total, 0.0, ALU.mult, ALU.add))
                pro.settle()
                pro.step(dve.tensor_tensor(upto, upto, total, ALU.subtract))
                pro.settle()
                pro.step(dve.tensor_copy(steps0[:, 0, :], total))
                pro.step(dve.tensor_copy(steps0[:, 1, :], upto))
                pro.step(dve.memset(out0[:, :, :], 0.0))
                pro.settle()
                dve.sem_inc(s["steps0_ready"], 1)

            def weights0(j, value, weighed):
                dve.wait_ge(xg0_in[j], value)
                dve.wait_ge(s["out0_ready"], weighed)
                dve.tensor_copy(wcol0[:, j, :], xg0[:, j, D:D + E0]).then_inc(s["wcol0_ready"], 1)

            def gated0(u, j):
                dve.wait_ge(s["silu0_ready"], u * 2 + j + 1)
                dve.tensor_tensor(act0[:, j].rearrange("p k c -> p (k c)"), sc[:, j, 512:512 + D], silu0[:, j, :],
                                  ALU.mult).then_inc(s["act0_ready"], 1)

            def weigh0(u, j, e):
                dve.wait_ge(s["y0_ps"], u * 2 + j + 1)
                dve.wait_ge(s["wcol0_ready"], u * 2 + j + 3)
                dve.wait_ge(added0[j], u * 16 + 32)
                dve.tensor_scalar(out0[:, j, :], yy[:, 512 * j:512 * j + D], wcol0[:, j, e:e + 1], None, ALU.mult
                                  ).then_inc(s["out0_ready"], 1)

            for l in range(2):
                z = at[l]
                pro.step(dve.tensor_copy(tok_f[:, :], consts[:, C_TOK:C_TOK + TT]))
                pro.settle()

                def front_(f, first_one):
                    front(f, l, pro, first_one)
                    split_queries(f, l, pro)

                def row(b, f):
                    st = Steps(dve, z["dve_step"], b * 256, 256)
                    attention(b, l, f, st)
                    layer_norm(b, l, st, False)
                    if f is not None:
                        split_queries(f, l, st)
                    if l == 0:
                        router0(b, st)
                        dispatch(b, 0, st)
                    else:
                        router1(b, st)
                        dispatch(b, 1, st)
                        shared(b)
                        dve.wait_ge(s["y_ready"], b + 1)
                        for t in range(TT):
                            last = dve.scalar_tensor_tensor(out=x[:, t, :], in0=y_rows[:, t, :],
                                                            scalar=small[:, 10, t:t + 1], in1=x[:, t, :],
                                                            op0=ALU.mult, op1=ALU.add)
                        last.then_inc(s["y_added"], 1)
                    st.fill()

                by_rows(front_, row)(dve, l)
                if l == 0:
                    count_steps()
                    weights0(0, 16, 1)
                    for e in range(E0):
                        n, before = steps_of_expert(dve, e)
                        with dve.Fori(0, n) as i:
                            u = unit_of(dve, before, i)
                            gated0(u, 0)
                            weights0(1, u * 16 + 16, u * 2 + 2)
                            gated0(u, 1)
                            weigh0(u, 0, e)
                            weights0(0, u * 16 + 32, u * 2 + 3)
                            weigh0(u, 1, e)
            experts_dve(dve)


def constants():
    import numpy as np
    c = np.zeros((P, C_END), np.float32)
    i = np.arange(P)
    c[:, C_ID:C_ID + P] = i[:, None] == i[None, :]
    c[:, C_TRI:C_TRI + P] = i[:, None] < i[None, :]
    c[:, C_E1:C_E1 + 64] = np.arange(1, 65)
    c[:, C_I8:C_I8 + 8] = np.arange(8)
    rest = -1e9
    for part in range(3):
        v = float((np.float32(rest).view(np.uint32) & np.uint32(0xffff0000)).view(np.float32))
        rest -= v
        c[ROW_NEG + part, C_NEG], c[ROW_NEG + part, C_NEG + 1] = -v, v
        c[ROW_MAX + part, C_NEG + 1] = 1.0
        c[ROW_MAX + part, C_NEG + 2] = 1.0
    c[:, C_TOK:C_TOK + 4] = i[:, None] + P * np.arange(4)[None, :]
    return c


def kernel(**inputs):
    import concourse.bacc as bacc
    import numpy as np
    from concourse.bass_utils import run_bass_kernel_spmd

    g = {k: np.asarray(v) for k, v in inputs.items()}
    B, T, D = g["x"].shape
    arrays = {
        "consts": constants(),
        "x": g["x"],
        "ctxT": g["ctx_1024"].transpose(0, 2, 1),
        "mask0T": np.ascontiguousarray(g["mask_SxS2_bk0"].T).view(np.uint32),
        "mask1": g["mask_Bx1x1xS2_ik0"].reshape(B, -1),
        "wq0": g["L0_xattn_wq"].T, "wk0": g["L0_xattn_wk"].T,
        "wv0": g["L0_xattn_wv"].T, "wo0": g["L0_xattn_wo"].T,
        "wq1": g["L1_xattn_Wq"], "wk1": g["L1_xattn_Wk"], "wv1": g["L1_xattn_Wv"], "wo1": g["L1_xattn_Wo"],
        "bqkv": np.stack([g["L1_xattn_bq"], g["L1_xattn_bk"], g["L1_xattn_bv"]]
                         ).reshape(3, D // P, P).transpose(2, 0, 1),
        "bo": g["L1_xattn_bo"],
        "gate0": g["L0_ffn_gate_w"].T, "gu0": g["L0_ffn_gate_up_proj"], "down0": g["L0_ffn_down_proj"],
        "gate1": np.concatenate([g["L1_ffn_gate_w"], g["L1_ffn_shared_gate_w"]], axis=1),
        "gu_s": g["L1_ffn_shared_gate_up_w"], "down_s": g["L1_ffn_shared_down_w"],
        "egu": g["L1_ffn_expert_gate_up_w"], "edown": g["L1_ffn_expert_down_w"],
    }
    arrays = {k: np.ascontiguousarray(v) for k, v in arrays.items()}
    nc = bacc.Bacc("TRN2", target_bir_lowering=False, num_devices=1)
    ap = {k: nc.dram_tensor("in_" + k, v.shape, mybir.dt.from_np(v.dtype), kind="ExternalInput").ap()
          for k, v in arrays.items()}
    for w in ("wq", "wk", "wv", "wo"):
        ap[w] = [ap[w + "0"], ap[w + "1"]]
    out = nc.dram_tensor("out", (B * T + 2 * P, D), F32, kind="ExternalOutput").ap()
    build(nc, ap, out)
    r = run_bass_kernel_spmd(nc, [{"in_" + k: v for k, v in arrays.items()}], core_ids=[0])
    return r.results[0]["out"][:B * T].reshape(B, T, D)
```
